# Optimizing a Trainium2 kernel written in Bass

```python
import numpy as np
import jax
import jax.numpy as jnp

def _softmax(x, axis=-1):
    return jax.nn.softmax(x, axis=axis)

def _gelu(x):
    return jax.nn.gelu(x, approximate=True)

def _silu(x):
    return jax.nn.silu(x)

def _sigmoid(x):
    return jax.nn.sigmoid(x)

def _layernorm(x, axis=-1, eps=1e-05):
    m = jnp.mean(x, axis=axis, keepdims=True)
    v = jnp.var(x, axis=axis, keepdims=True)
    return (x - m) / jnp.sqrt(v + eps)

def _scatter_add(tgt, idx, src, axis=0):
    return tgt.at[idx].add(src)

def _segment_sum(src, seg, n):
    return jax.ops.segment_sum(src, seg, n)
kernel_name = 'mk_sandwich_d2_jaxref_r4_0d09eb'

def setup_inputs(seed: int=0):
    np.random.seed(seed)
    _w = jnp.asarray

    def _L0_attn_setup():
        import jax, jax.numpy as jnp
        import numpy as np
        EPS = 1e-05
        key = jax.random.key(seed)
        ks = jax.random.split(key, 7)
        B, T, H = (4, 1024, 256)
        x = jax.random.normal(ks[0], (B, T, H), dtype=jnp.float32)
        gamma = jnp.ones((H,), dtype=jnp.float32)
        beta = jnp.zeros((H,), dtype=jnp.float32)
        s = 1.0 / np.sqrt(H)
        Wg = jax.random.uniform(ks[1], (H, H), minval=-s, maxval=s, dtype=jnp.float32)
        bg = jax.random.uniform(ks[2], (H,), minval=-s, maxval=s, dtype=jnp.float32)
        Wc = jax.random.uniform(ks[3], (H, H), minval=-s, maxval=s, dtype=jnp.float32)
        bc = jax.random.uniform(ks[4], (H,), minval=-s, maxval=s, dtype=jnp.float32)
        return {'x': x, 'gamma': gamma, 'beta': beta, 'Wg': Wg, 'bg': bg, 'Wc': Wc, 'bc': bc}
    _L0_attn_in = _L0_attn_setup()

    def _L0_ffn_setup():
        import jax, jax.numpy as jnp
        import numpy as np
        D_IN, D_HID = (256, 1024)

        def _ternary(key, shape):
            return jax.random.randint(key, shape, -1, 2).astype(jnp.float32)

        def _tlin(x, w, s):
            return jnp.einsum('bsi,oi->bso', x, w) * s
        key = jax.random.key(seed)
        ks = jax.random.split(key, 12)
        inv = lambda fan: 1.0 / np.sqrt(fan).astype(np.float32)
        return {'x': jax.random.normal(ks[0], (4, 512, D_IN), dtype=jnp.float32), 'w1_w': _ternary(ks[1], (D_HID, D_IN)), 'w1_s': jax.random.uniform(ks[2], (D_HID,), dtype=jnp.float32) * inv(D_IN), 'w2_w': _ternary(ks[3], (D_HID, D_IN)), 'w2_s': jax.random.uniform(ks[4], (D_HID,), dtype=jnp.float32) * inv(D_IN), 'h1_w': _ternary(ks[5], (D_HID, D_HID)), 'h1_s': jax.random.uniform(ks[6], (D_HID,), dtype=jnp.float32) * inv(D_HID), 'h2_w': _ternary(ks[7], (D_HID, D_HID)), 'h2_s': jax.random.uniform(ks[8], (D_HID,), dtype=jnp.float32) * inv(D_HID), 'w3_w': _ternary(ks[9], (D_IN, D_HID)), 'w3_s': jax.random.uniform(ks[10], (D_IN,), dtype=jnp.float32) * inv(D_HID)}
    _L0_ffn_in = _L0_ffn_setup()

    def _L1_attn_setup():
        import jax, jax.numpy as jnp
        import numpy as np
        B, T, C, I = (4, 1024, 256, 1024)

        def rmsnorm(x, w, eps=1e-06):
            return x * jax.lax.rsqrt(jnp.mean(x * x, axis=-1, keepdims=True) + eps) * w

        def shift(h):
            return jnp.pad(h, ((0, 0), (1, 0), (0, 0)))[:, :-1]

        def wkv_scan(k, v, w, u):
            ew = jnp.exp(jnp.clip(w, -20.0, 20.0))

            def step(carry, kv):
                a, b = carry
                kt, vt = kv
                ekt = jnp.exp(jnp.clip(u + kt, -20.0, 20.0))
                out = (a + ekt * vt) / (b + ekt + 1e-08)
                ek = jnp.exp(jnp.clip(kt, -20.0, 20.0))
                return ((ew * a + ek * vt, ew * b + ek), out)
            init = (jnp.zeros((k.shape[0], k.shape[2]), jnp.float32), jnp.zeros((k.shape[0], k.shape[2]), jnp.float32))
            _, out = jax.lax.scan(step, init, (k.swapaxes(0, 1), v.swapaxes(0, 1)))
            return out.swapaxes(0, 1)
        key = jax.random.key(seed)
        ks = jax.random.split(key, 16)
        s = 1.0 / np.sqrt(C)
        si = 1.0 / np.sqrt(I)
        return {'x': jax.random.normal(ks[0], (B, T, C), jnp.float32), 'ln1_w': jnp.ones((C,), jnp.float32), 'ln2_w': jnp.ones((C,), jnp.float32), 'time_decay': jax.random.normal(ks[1], (C,), jnp.float32) * 0.1 - 5.0, 'time_first': jax.random.normal(ks[2], (C,), jnp.float32) * 0.01, 'time_mix_k': jnp.full((C,), 0.5, jnp.float32), 'time_mix_v': jnp.full((C,), 0.5, jnp.float32), 'time_mix_r': jnp.full((C,), 0.5, jnp.float32), 'W_key': jax.random.normal(ks[3], (C, C), jnp.float32) * s, 'W_value': jax.random.normal(ks[4], (C, C), jnp.float32) * s, 'W_recept': jax.random.normal(ks[5], (C, C), jnp.float32) * s, 'W_out': jax.random.normal(ks[6], (C, C), jnp.float32) * s, 'time_mix_k2': jnp.full((C,), 0.5, jnp.float32), 'time_mix_r2': jnp.full((C,), 0.5, jnp.float32), 'W_key2': jax.random.normal(ks[7], (C, I), jnp.float32) * s, 'W_value2': jax.random.normal(ks[8], (I, C), jnp.float32) * si, 'W_recept2': jax.random.normal(ks[9], (C, C), jnp.float32) * s}
    _L1_attn_in = _L1_attn_setup()

    def _L1_ffn_setup():
        import jax, jax.numpy as jnp
        import numpy as np
        B, S, H, DFF, E, K = (2, 512, 256, 512, 8, 2)

        def _moe(x, Wg, W1, b1, W2, b2, W3, b3):
            Bm, Sm, Hm = x.shape
            xt = x.reshape(-1, Hm)
            gout = xt @ Wg.T
            topv, topi = jax.lax.top_k(gout, K)
            w = jax.nn.softmax(topv, axis=-1)
            comb = jnp.einsum('tke,tk->te', jax.nn.one_hot(topi, E, dtype=x.dtype), w)
            g = jnp.einsum('th,efh->etf', xt, W1) + b1[:, None, :]
            v = jnp.einsum('th,efh->etf', xt, W2) + b2[:, None, :]
            h = jax.nn.silu(g) * v
            eo = jnp.einsum('etf,ehf->eth', h, W3) + b3[:, None, :]
            out = jnp.einsum('eth,te->th', eo, comb)
            return out.reshape(Bm, Sm, Hm)
        key = jax.random.key(seed)
        ks = jax.random.split(key, 8)
        sc_h = 1.0 / np.sqrt(H)
        sc_f = 1.0 / np.sqrt(DFF)
        x = jax.random.normal(ks[0], (B, S, H), dtype=jnp.float32)
        Wg = jax.random.uniform(ks[1], (E, H), jnp.float32, -sc_h, sc_h)
        W1 = jax.random.uniform(ks[2], (E, DFF, H), jnp.float32, -sc_h, sc_h)
        b1 = jax.random.uniform(ks[3], (E, DFF), jnp.float32, -sc_h, sc_h)
        W2 = jax.random.uniform(ks[4], (E, DFF, H), jnp.float32, -sc_h, sc_h)
        b2 = jax.random.uniform(ks[5], (E, DFF), jnp.float32, -sc_h, sc_h)
        W3 = jax.random.uniform(ks[6], (E, H, DFF), jnp.float32, -sc_f, sc_f)
        b3 = jax.random.uniform(ks[7], (E, H), jnp.float32, -sc_f, sc_f)
        return {'x': x, 'Wg': Wg, 'W1': W1, 'b1': b1, 'W2': W2, 'b2': b2, 'W3': W3, 'b3': b3}
    _L1_ffn_in = _L1_ffn_setup()
    _d = {'L0_attn_x': _L0_attn_in['x'], 'L0_attn_gamma': _L0_attn_in['gamma'], 'L0_attn_beta': _L0_attn_in['beta'], 'L0_attn_Wg': _L0_attn_in['Wg'], 'L0_attn_bg': _L0_attn_in['bg'], 'L0_attn_Wc': _L0_attn_in['Wc'], 'L0_attn_bc': _L0_attn_in['bc'], 'L0_ffn_w1_w': _L0_ffn_in['w1_w'], 'L0_ffn_w1_s': _L0_ffn_in['w1_s'], 'L0_ffn_w2_w': _L0_ffn_in['w2_w'], 'L0_ffn_w2_s': _L0_ffn_in['w2_s'], 'L0_ffn_h1_w': _L0_ffn_in['h1_w'], 'L0_ffn_h1_s': _L0_ffn_in['h1_s'], 'L0_ffn_h2_w': _L0_ffn_in['h2_w'], 'L0_ffn_h2_s': _L0_ffn_in['h2_s'], 'L0_ffn_w3_w': _L0_ffn_in['w3_w'], 'L0_ffn_w3_s': _L0_ffn_in['w3_s'], 'L1_attn_ln1_w': _L1_attn_in['ln1_w'], 'L1_attn_ln2_w': _L1_attn_in['ln2_w'], 'L1_attn_time_decay': _L1_attn_in['time_decay'], 'L1_attn_time_first': _L1_attn_in['time_first'], 'L1_attn_time_mix_k': _L1_attn_in['time_mix_k'], 'L1_attn_time_mix_v': _L1_attn_in['time_mix_v'], 'L1_attn_time_mix_r': _L1_attn_in['time_mix_r'], 'L1_attn_W_key': _L1_attn_in['W_key'], 'L1_attn_W_value': _L1_attn_in['W_value'], 'L1_attn_W_recept': _L1_attn_in['W_recept'], 'L1_attn_W_out': _L1_attn_in['W_out'], 'L1_attn_time_mix_k2': _L1_attn_in['time_mix_k2'], 'L1_attn_time_mix_r2': _L1_attn_in['time_mix_r2'], 'L1_attn_W_key2': _L1_attn_in['W_key2'], 'L1_attn_W_value2': _L1_attn_in['W_value2'], 'L1_attn_W_recept2': _L1_attn_in['W_recept2'], 'L1_ffn_Wg': _L1_ffn_in['Wg'], 'L1_ffn_W1': _L1_ffn_in['W1'], 'L1_ffn_b1': _L1_ffn_in['b1'], 'L1_ffn_W2': _L1_ffn_in['W2'], 'L1_ffn_b2': _L1_ffn_in['b2'], 'L1_ffn_W3': _L1_ffn_in['W3'], 'L1_ffn_b3': _L1_ffn_in['b3']}
    _x0 = _d['L0_attn_x']
    _d['L0_attn_x'] = jax.random.normal(jax.random.fold_in(jax.random.key(seed), 1), (4, 1024, 256), dtype=_x0.dtype)
    del _x0
    return _d

def reference(L0_attn_x, L0_attn_gamma, L0_attn_beta, L0_attn_Wg, L0_attn_bg, L0_attn_Wc, L0_attn_bc, L0_ffn_w1_w, L0_ffn_w1_s, L0_ffn_w2_w, L0_ffn_w2_s, L0_ffn_h1_w, L0_ffn_h1_s, L0_ffn_h2_w, L0_ffn_h2_s, L0_ffn_w3_w, L0_ffn_w3_s, L1_attn_ln1_w, L1_attn_ln2_w, L1_attn_time_decay, L1_attn_time_first, L1_attn_time_mix_k, L1_attn_time_mix_v, L1_attn_time_mix_r, L1_attn_W_key, L1_attn_W_value, L1_attn_W_recept, L1_attn_W_out, L1_attn_time_mix_k2, L1_attn_time_mix_r2, L1_attn_W_key2, L1_attn_W_value2, L1_attn_W_recept2, L1_ffn_Wg, L1_ffn_W1, L1_ffn_b1, L1_ffn_W2, L1_ffn_b2, L1_ffn_W3, L1_ffn_b3):

    def _L0_attn_ref(x, gamma, beta, Wg, bg, Wc, bc):
        import jax, jax.numpy as jnp
        import numpy as np
        EPS = 1e-05
        mu = jnp.mean(x, axis=-1, keepdims=True)
        var = jnp.mean((x - mu) ** 2, axis=-1, keepdims=True)
        normed = (x - mu) * jax.lax.rsqrt(var + EPS) * gamma + beta
        z = jax.nn.sigmoid(jnp.einsum('bth,oh->bto', normed, Wg) + bg)
        c = jnp.einsum('bth,oh->bto', normed, Wc) + bc
        B, T, H = x.shape

        def step(h, zc):
            z_t, c_t = zc
            h = (1.0 - z_t) * h + z_t * c_t
            return (h, h)
        h0 = jnp.zeros((B, H), dtype=x.dtype)
        _, hs = jax.lax.scan(step, h0, (jnp.swapaxes(z, 0, 1), jnp.swapaxes(c, 0, 1)))
        return jnp.swapaxes(hs, 0, 1) + x

    def _L0_ffn_ref(x, w1_w, w1_s, w2_w, w2_s, h1_w, h1_s, h2_w, h2_s, w3_w, w3_s):
        import jax, jax.numpy as jnp
        import numpy as np
        D_IN, D_HID = (256, 1024)

        def _ternary(key, shape):
            return jax.random.randint(key, shape, -1, 2).astype(jnp.float32)

        def _tlin(x, w, s):
            return jnp.einsum('bsi,oi->bso', x, w) * s
        h = jax.nn.silu(_tlin(x, w1_w, w1_s)) * _tlin(x, w2_w, w2_s)
        h = jax.nn.gelu(_tlin(h, h1_w, h1_s), approximate=False)
        h = jax.nn.gelu(_tlin(h, h2_w, h2_s), approximate=False)
        return _tlin(h, w3_w, w3_s)

    def _L1_attn_ref(x, ln1_w, ln2_w, time_decay, time_first, time_mix_k, time_mix_v, time_mix_r, W_key, W_value, W_recept, W_out, time_mix_k2, time_mix_r2, W_key2, W_value2, W_recept2):
        import jax, jax.numpy as jnp
        import numpy as np
        B, T, C, I = (4, 1024, 256, 1024)

        def rmsnorm(x, w, eps=1e-06):
            return x * jax.lax.rsqrt(jnp.mean(x * x, axis=-1, keepdims=True) + eps) * w

        def shift(h):
            return jnp.pad(h, ((0, 0), (1, 0), (0, 0)))[:, :-1]

        def wkv_scan(k, v, w, u):
            ew = jnp.exp(jnp.clip(w, -20.0, 20.0))

            def step(carry, kv):
                a, b = carry
                kt, vt = kv
                ekt = jnp.exp(jnp.clip(u + kt, -20.0, 20.0))
                out = (a + ekt * vt) / (b + ekt + 1e-08)
                ek = jnp.exp(jnp.clip(kt, -20.0, 20.0))
                return ((ew * a + ek * vt, ew * b + ek), out)
            init = (jnp.zeros((k.shape[0], k.shape[2]), jnp.float32), jnp.zeros((k.shape[0], k.shape[2]), jnp.float32))
            _, out = jax.lax.scan(step, init, (k.swapaxes(0, 1), v.swapaxes(0, 1)))
            return out.swapaxes(0, 1)
        h = rmsnorm(x, ln1_w)
        sh = shift(h)
        xk = h * time_mix_k + sh * (1 - time_mix_k)
        xv = h * time_mix_v + sh * (1 - time_mix_v)
        xr = h * time_mix_r + sh * (1 - time_mix_r)
        k = xk @ W_key
        v = xv @ W_value
        r = jax.nn.sigmoid(xr @ W_recept)
        w = -jnp.exp(time_decay)
        u = time_first
        wkv = wkv_scan(k.astype(jnp.float32), v.astype(jnp.float32), w, u).astype(x.dtype)
        x = x + r * wkv @ W_out
        h = rmsnorm(x, ln2_w)
        sh = shift(h)
        xk = h * time_mix_k2 + sh * (1 - time_mix_k2)
        xr = h * time_mix_r2 + sh * (1 - time_mix_r2)
        k2 = jnp.square(jax.nn.relu(xk @ W_key2))
        r2 = jax.nn.sigmoid(xr @ W_recept2)
        return x + r2 * (k2 @ W_value2)

    def _L1_ffn_ref(x, Wg, W1, b1, W2, b2, W3, b3):
        import jax, jax.numpy as jnp
        import numpy as np
        B, S, H, DFF, E, K = (2, 512, 256, 512, 8, 2)

        def _moe(x, Wg, W1, b1, W2, b2, W3, b3):
            Bm, Sm, Hm = x.shape
            xt = x.reshape(-1, Hm)
            gout = xt @ Wg.T
            topv, topi = jax.lax.top_k(gout, K)
            w = jax.nn.softmax(topv, axis=-1)
            comb = jnp.einsum('tke,tk->te', jax.nn.one_hot(topi, E, dtype=x.dtype), w)
            g = jnp.einsum('th,efh->etf', xt, W1) + b1[:, None, :]
            v = jnp.einsum('th,efh->etf', xt, W2) + b2[:, None, :]
            h = jax.nn.silu(g) * v
            eo = jnp.einsum('etf,ehf->eth', h, W3) + b3[:, None, :]
            out = jnp.einsum('eth,te->th', eo, comb)
            return out.reshape(Bm, Sm, Hm)
        return _moe(x, Wg, W1, b1, W2, b2, W3, b3)
    x = L0_attn_x
    x = x + _layernorm(_L0_attn_ref(_layernorm(x, axis=-1), L0_attn_gamma, L0_attn_beta, L0_attn_Wg, L0_attn_bg, L0_attn_Wc, L0_attn_bc), axis=-1)
    x = x + _layernorm(_L0_ffn_ref(_layernorm(x, axis=-1), L0_ffn_w1_w, L0_ffn_w1_s, L0_ffn_w2_w, L0_ffn_w2_s, L0_ffn_h1_w, L0_ffn_h1_s, L0_ffn_h2_w, L0_ffn_h2_s, L0_ffn_w3_w, L0_ffn_w3_s), axis=-1)
    x = x + _layernorm(_L1_attn_ref(_layernorm(x, axis=-1), L1_attn_ln1_w, L1_attn_ln2_w, L1_attn_time_decay, L1_attn_time_first, L1_attn_time_mix_k, L1_attn_time_mix_v, L1_attn_time_mix_r, L1_attn_W_key, L1_attn_W_value, L1_attn_W_recept, L1_attn_W_out, L1_attn_time_mix_k2, L1_attn_time_mix_r2, L1_attn_W_key2, L1_attn_W_value2, L1_attn_W_recept2), axis=-1)
    x = x + _layernorm(_L1_ffn_ref(_layernorm(x, axis=-1), L1_ffn_Wg, L1_ffn_W1, L1_ffn_b1, L1_ffn_W2, L1_ffn_b2, L1_ffn_W3, L1_ffn_b3), axis=-1)
    return x

_drawn_inputs = setup_inputs


def setup_inputs(seed=0):
    import zlib

    import numpy as np

    out = dict(_drawn_inputs(seed))
    spreads = {'L0_attn_gamma': (1.0, 0.2),
     'L0_attn_beta': (0.0, 0.1),
     'L1_attn_ln1_w': (1.0, 0.6),
     'L1_attn_ln2_w': (1.0, 0.2),
     'L1_attn_time_mix_k': (0.5, 0.6),
     'L1_attn_time_mix_v': (0.5, 0.6),
     'L1_attn_time_mix_r': (0.5, 0.6),
     'L1_attn_time_mix_k2': (0.5, 0.2),
     'L1_attn_time_mix_r2': (0.5, 0.597)}
    factors = {'L0_attn_bg': 3.234,
     'L1_attn_time_decay': 5.582,
     'L1_attn_time_first': 200.0,
     'L1_ffn_b1': 2.902,
     'L1_ffn_b2': 2.905}
    for name, (base, spread) in spreads.items():
        noise = np.random.default_rng([zlib.crc32(name.encode()), seed]).standard_normal(out[name].shape)
        drawn = base * np.exp(spread * noise) if base else spread * noise
        out[name] = jnp.asarray(drawn.astype(out[name].dtype))
    for name, factor in factors.items():
        out[name] = (out[name] * factor).astype(out[name].dtype)
    return out
```

```python
import concourse.bass as bass
from concourse import mybir
from contextlib import ExitStack
import numpy as np

fp32 = mybir.dt.float32
fp32r = mybir.dt.float32r
u32 = mybir.dt.uint32
i32 = mybir.dt.int32
bf16 = mybir.dt.bfloat16
ALU = mybir.AluOpType
ACT = mybir.ActivationFunctionType
AX = mybir.AxisListType
ADD, SUB, MUL, MAX, MIN = ALU.add, ALU.subtract, ALU.mult, ALU.max, ALU.min

P = 128
N_TOK = 4096
SEQ = 1024
D = 256
DC = D // P
HID = 1024
HC = HID // P
BLK = 512
TPB = BLK // P
NBLK = N_TOK // BLK
EXP = 8
FF = 512
FC = FF // P
REGION = N_TOK + P
N_TILES = 2 * N_TOK // P + EXP
ROW = D + 4
PARTS = 3
LN_EPS = 1e-5
RMS_EPS = 1e-6
CLIP = (float(np.exp(np.float32(-20.0))), float(np.exp(np.float32(20.0))))

VEC = {}
_at = 0
for _name, _n in [("gamma", DC), ("beta", DC), ("bg", DC), ("bc", DC), ("w1_s", HC), ("w2_s", HC),
                  ("h1_s", HC), ("h2_s", HC), ("ln1_w", DC), ("ln2_w", DC), ("decay", DC), ("first", DC),
                  ("mix_k", DC), ("mix_v", DC), ("mix_r", DC), ("mix_k2", DC), ("mix_r2", DC)]:
    VEC[_name] = _at
    _at += _n
N_VEC = _at


class Steps:
    def __init__(self, eng, s, per):
        self.eng, self.s, self.per = eng, s, per

    def start(self, b):
        self.base, self.k = b * self.per, 0

    def mark(self, ins):
        self.k += 1
        ins.then_inc(self.s, 1)

    def link(self, ins):
        self.mark(ins)
        self.wait()

    def wait(self):
        self.eng.wait_ge(self.s, self.base + self.k)

    def end(self):
        assert self.k == self.per, self.k


def build(nc, x_in, vecs_in, w3s_in, wg_in, wc_in, w1_in, w2_in, h1_in, h2_in, w3_in,
          wk_in, wv_in, wr_in, wo_in, wk2_in, wv2_in, wr2_in,
          wg8_in, m1_in, m2_in, m3_in, bias_in, rowc_in, out):
    ctx = ExitStack()
    with ctx:
        cursor = [nc.sbuf_base + (-nc.sbuf_base) % 64]

        def sb(name, shape, dt=fp32, at=None):
            size = 2 if dt == bf16 else 4
            for n in shape[1:]:
                size *= n
            where = cursor[0] if at is None else at
            place[name] = where
            if at is None:
                cursor[0] += size + (-size) % 64
            return nc.alloc_sbuf_tensor_at(name, shape, dt, offset=where)

        place = {}

        phase_sems = []

        def sem(name):
            phase_sems.append(nc.alloc_semaphore(name))
            return phase_sems[-1]

        def end_phase():
            nc.clear_and_free_semaphores(list(phase_sems))
            phase_sems.clear()
            nc.all_engine_barrier()

        xs_mid = nc.dram_tensor("x_after_ffn", [N_TOK, D], fp32, kind="Internal").ap()
        x_blocks = x_in.rearrange("(t p) d -> p t d", p=P)
        mid_blocks = xs_mid.rearrange("(t p) d -> p t d", p=P)
        out_blocks = out.rearrange("(t p) d -> p t d", p=P)
        x3_dram = nc.dram_tensor("x_after_mixing", [N_TOK, D], fp32, kind="Internal").ap()
        x3_blocks = x3_dram.rearrange("(t p) d -> p t d", p=P)
        routed = nc.dram_tensor("routed_rows", [EXP * REGION + P, ROW], fp32, kind="Internal").ap()
        expert_out = nc.dram_tensor("expert_rows", [2 * N_TOK + N_TILES * P, D], fp32, kind="Internal").ap()

        ident = sb("ident", [P, P])
        vecs = sb("vecs", [P, N_VEC])
        neg_bg = sb("neg_bg", [P, DC])
        carry_on = sb("carry_on", [P, NBLK + 2])
        w3s_row = sb("w3s_row", [P, D])

        def vec(name, c):
            return vecs[:, VEC[name] + c:VEC[name] + c + 1]

        wg8 = sb("wg8", [P, DC, EXP])
        upper, ones_bf = sb("upper", [P, P], bf16), sb("ones_bf", [P, P], bf16)
        expert_no = sb("expert_no", [P, EXP])
        expert_no8 = sb("expert_no8", [P, EXP])
        taken = sb("taken", [P, EXP])
        twice_token = sb("twice_token", [P, TPB])
        ids_i = sb("ids_i", [P, TPB], i32)
        eno_i = sb("eno_i", [P, EXP], i32)
        shared_from = cursor[0]
        w_gate_hi, w_gate_lo = (sb(f"w_gate_{s}", [P, DC, D], fp32r) for s in ("hi", "lo"))
        w_cand_hi, w_cand_lo = (sb(f"w_cand_{s}", [P, DC, D], fp32r) for s in ("hi", "lo"))
        w1 = sb("w1", [P, DC, HID], fp32r)
        w2 = sb("w2", [P, DC, HID], fp32r)
        h1w = sb("h1w", [P, HC, HID], fp32r)
        h2w = sb("h2w", [P, HC, HID], fp32r)
        w3 = sb("w3", [P, HC, D], fp32r)

        ha_hi, ha_lo = (sb(f"ha_{s}", [P, HC, BLK], fp32r) for s in ("hi", "lo"))
        hb_hi, hb_lo = (sb(f"hb_{s}", [P, HC, BLK], fp32r) for s in ("hi", "lo"))
        yt_hi, yt_lo = (sb(f"yt_{s}", [P, DC, BLK], fp32r) for s in ("hi", "lo"))
        xa = sb("xa", [P, TPB, D])
        xb = sb("xb", [P, TPB, D])
        yn = sb("yn", [P, TPB, D])
        o1 = sb("o1", [P, TPB, D])
        hs = o1[:, :, :].rearrange("p t d -> p (t d)").rearrange("p (c n) -> p c n", c=DC)
        o2 = sb("o2", [P, TPB, D])
        act2 = sb("act2", [P, 2, BLK])
        f2 = sb("f2", [P, 2, BLK])
        zc = sb("zc", [P, BLK])
        carry = sb("carry", [P, DC])
        st1, mv1 = sb("st1", [P, TPB, 6]), sb("mv1", [P, TPB, 2])
        st2, mv2 = sb("st2", [P, TPB, 6]), sb("mv2", [P, TPB, 2])
        v1a, r1a = sb("v1a", [P, 2, TPB]), sb("r1a", [P, 2, TPB])
        inv_r2 = sb("inv_r2", [P, TPB])
        r12 = sb("r12", [P, TPB])
        v2a, r2a = sb("v2a", [P, TPB]), sb("r2a", [P, TPB])
        N_CHK = 7
        chk = sb("chk", [P, N_CHK])
        chk1, chk_all = sb("chk1", [P, 1]), sb("chk_all", [P, 1])
        split_flag = sb("split_flag", [1, 1], u32)

        bank = [ctx.enter_context(nc.psum_tensor(f"bank{n}", [P, BLK], fp32)) for n in range(8)]
        ff = bank[0:4]
        pyo = bank[4:6]
        pt = bank[6:8]

        s_const = sem("const_loaded")
        s_ident0, s_ident = sem("ident_zeroed"), sem("ident_ready")
        s_masks = sem("masks_ready")
        s_wst = sem("small_weights_staged")
        s_stage = [sem(f"staged{n}") for n in range(7)]
        s_round = sem("weights_rounded")
        s_chk = sem("weights_checked")
        s_raw = sem("weights_in_place")
        s_flag0, s_flag1, s_flag = sem("flag_summed"), sem("flag_reduced"), sem("flag_ready")
        s_wsplit = sem("small_weights_split")
        s_wlo = sem("small_weights_low")
        s_x = sem("x_loaded")
        s_dve_on, s_pool_on = sem("vector_goes_on"), sem("pool_goes_on")
        s_p1 = sem("p1_steps")
        s_v1 = sem("p1_variances")
        s_r1 = sem("p1_roots")
        s_yn = sem("p1_normalized")
        s_t1 = sem("p1_transposed")
        s_aff = sem("p1_affine")
        s_nt = sem("p1_split")
        s_z, s_c = sem("gate_product"), sem("candidate_product")
        s_sig = sem("gates_ready")
        s_zc = sem("gated_candidate")
        s_scan = sem("scanned")
        s_ht = sem("scan_transposed")
        s_vo, s_ro = sem("p1_out_variances"), sem("p1_out_roots")
        s_xa = sem("p1_done")
        s_v2, s_r2 = sem("ffn_in_variances"), sem("ffn_in_roots")
        s_y2 = sem("ffn_normalized")
        s_t2 = sem("ffn_transposed")
        s_yhi, s_ylo = sem("ffn_in_high"), sem("ffn_in_low")
        s_l1a, s_l1b = sem("w1_product"), sem("w2_product")
        s_silu = sem("silu_ready")
        s_f1, s_f1hi, s_f1lo = sem("h_product"), sem("h_high"), sem("h_low")
        s_l2, s_l3 = sem("h1_product"), sem("h2_product")
        s_g2, s_g2hi, s_g2lo = sem("gelu1_ready"), sem("gelu1_high"), sem("gelu1_low")
        s_g3, s_g3hi, s_g3lo = sem("gelu2_ready"), sem("gelu2_high"), sem("gelu2_low")
        s_l4 = sem("w3_product")
        s_y4 = sem("ffn_scaled")
        s_p2 = sem("ffn_steps")
        s_p3 = sem("ffn_out_steps")
        s_v4, s_r4 = sem("ffn_out_variances"), sem("ffn_out_roots")
        s_o2 = sem("ffn_done")
        s_xb = sem("xb_filled")
        s_st = sem("ffn_stored")

        block_ctx = ExitStack()
        block = block_ctx.enter_context(nc.Block())

        stage_w1 = sb("stage_w1", [P, DC * HID], at=place["ha_hi"])
        stage_w2 = sb("stage_w2", [P, DC * HID], at=place["ha_hi"] + 4 * DC * HID)
        stage_w3 = sb("stage_w3", [P, HC * D], at=place["ha_lo"])
        HALF = HC * HID // 2
        stage_h1 = [sb(f"stage_h1_{s}", [P, HALF], at=place["hb_" + s]) for s in ("hi", "lo")]
        stage_h2 = [sb(f"stage_h2_{n}", [P, HALF], at=place[s + "_hi"]) for n, s in enumerate(("ha", "hb"))]

        def flat(w):
            return w[:, :, :].rearrange("p c n -> p (c n)")

        ffn_weights = [(w1_in, stage_w1, flat(w1)), (w2_in, stage_w2, flat(w2)), (w3_in, stage_w3, flat(w3)),
                       (h1_in[:, 0:HALF], stage_h1[0], flat(h1w)[:, 0:HALF]), (h1_in[:, HALF:], stage_h1[1], flat(h1w)[:, HALF:]),
                       (h2_in[:, 0:HALF], stage_h2[0], flat(h2w)[:, 0:HALF]), (h2_in[:, HALF:], stage_h2[1], flat(h2w)[:, HALF:])]
        EARLY = 5

        @block.sync
        def _(sp):
            sp.dma_start(xa[:, :, :], x_blocks[:, 0:TPB, :]).then_inc(s_x, 16)
            sp.dma_start(vecs[:, :], vecs_in).then_inc(s_const, 16)
            sp.dma_start(o2[:, 0:2, :], wg_in).then_inc(s_wst, 16)
            sp.dma_start(o2[:, 2:4, :], wc_in).then_inc(s_wst, 16)
            sp.dma_start(w3s_row[:, :], w3s_in).then_inc(s_const, 16)
            for n, (src, stage, _) in enumerate(ffn_weights[:EARLY]):
                sp.dma_start(stage[:, :], src).then_inc(s_stage[n], 16)
            for n, (src, stage, dst) in enumerate(ffn_weights):
                if n == EARLY:
                    sp.wait_ge(s_raw, 16 * EARLY)
                    for m in range(EARLY, len(ffn_weights)):
                        sp.dma_start(ffn_weights[m][1][:, :], ffn_weights[m][0]).then_inc(s_stage[m], 16)
                sp.wait_ge(s_chk, n + 1)
                sp.dma_start(dst.bitcast(fp32), stage[:, :]).then_inc(s_raw, 16)

            def store_and_load(b, more):
                sp.wait_ge(s_xb, b + 1)
                sp.wait_ge(s_y2, b + 1)
                if more:
                    sp.dma_start(xa[:, :, :], x_blocks[:, bass.ds((b + 1) * TPB, TPB), :]).then_inc(s_x, 16)

            def store(b):
                sp.wait_ge(s_o2, b + 1)
                sp.dma_start(mid_blocks[:, bass.ds(b * TPB, TPB), :], o2[:, :, :]).then_inc(s_st, 16)

            store_and_load(0, True)
            with sp.Fori(0, NBLK - 2) as i:
                store(i)
                store_and_load(i + 1, True)
            store(NBLK - 2)
            store(NBLK - 1)
            sp.wait_ge(s_st, 16 * NBLK)

        @block.gpsimd
        def _(pool):
            nc.gpsimd.memset(ident[:, :], 0.0).then_inc(s_ident0, 1)
            pool.wait_ge(s_ident0, 1)
            nc.gpsimd.affine_select(out=ident[:, :], in_=ident[:, :], compare_op=ALU.not_equal, fill=1.0, base=0,
                                    pattern=[[-1, P]], channel_multiplier=1).then_inc(s_ident, 1)
            pool.wait_ge(s_wst, 32)
            nc.gpsimd.tensor_copy(w_gate_hi[:, :, :], o2[:, 0:2, :]).then_inc(s_wsplit, 1)
            nc.gpsimd.tensor_copy(w_cand_hi[:, :, :], o2[:, 2:4, :]).then_inc(s_wsplit, 1)
            pool.wait_ge(s_flag0, 1)
            nc.gpsimd.partition_all_reduce(chk_all[:, :], chk1[:, :], P, bass.bass_isa.ReduceOp.max).then_inc(s_flag1, 1)
            pool.wait_ge(s_xa, 1)
            nc.gpsimd.tensor_copy(xb[:, :, :], xa[:, :, :]).then_inc(s_xb, 1)
            with pool.Fori(1, NBLK) as i:
                pool.wait_ge(s_xa, i + 1)
                pool.wait_ge(s_o2, i)
                pool.sem_inc(s_pool_on)
                nc.gpsimd.tensor_copy(xb[:, :, :], xa[:, :, :]).then_inc(s_xb, 1)


        @block.tensor
        def _(pe):
            mm = nc.tensor.matmul

            def transpose_in(b, s_in, s_out, n_out):
                pe.wait_ge(s_in, b + 1)
                for c in range(DC):
                    for t in range(TPB):
                        last = nc.tensor.transpose(pt[c][:, t * P:(t + 1) * P], yn[:, t, c * P:(c + 1) * P], ident[:, :])
                    last.then_inc(s_out, 1)

            def p1_transpose(b, first=False):
                if not first:
                    pe.wait_ge(s_ylo, b * DC)
                transpose_in(b, s_yn, s_t1, DC)

            def p1_gates(b, m):
                pe.wait_ge(s_nt, b * DC + 2)
                if m:
                    pe.wait_ge(s_zc, b * DC + m)
                for dst, hi, lo, done in ((pt[0], w_gate_hi, w_gate_lo, s_z), (pt[1], w_cand_hi, w_cand_lo, s_c)):
                    n = 0
                    for c in range(DC):
                        for w, y in ((hi, yt_hi), (lo, yt_hi), (hi, yt_lo)):
                            last = mm(dst[:, :], w[:, c, m * P:(m + 1) * P], y[:, c, :], start=n == 0, stop=n == 3 * DC - 1)
                            n += 1
                    last.then_inc(done, 1)

            def p1_back(b):
                pe.wait_ge(s_scan, b * DC + DC)
                for t in range(TPB):
                    for c in range(DC):
                        last = nc.tensor.transpose(pt[t // 2][:, (t % 2) * D + c * P:(t % 2) * D + (c + 1) * P],
                                                   hs[:, c, t * P:(t + 1) * P], ident[:, :])
                last.then_inc(s_ht, 1)

            def ffn_transpose(b):
                transpose_in(b, s_y2, s_t2, DC)

            def group(dst, w, m, hi, lo, n_k, fast, before=None):
                n = 0
                for k in range(n_k):
                    if before:
                        before(k)
                    for x in (hi, lo):
                        a, y = w[:, k, m * P:(m + 1) * P], x[:, k, :]
                        if not fast:
                            a, y = a.bitcast(fp32), y.bitcast(fp32)
                        last = mm(dst[:, :], a, y, start=n == 0, stop=n == 2 * n_k - 1)
                        n += 1
                return last

            def layer1(b, fast):
                pe.wait_ge(s_ylo, b * DC + DC)
                for m in range(HC):
                    if m >= 2:
                        pe.wait_ge(s_f1, b * HC + m - 1)
                    group(ff[2 * (m % 2)], w1, m, yt_hi, yt_lo, DC, fast).then_inc(s_l1a, 1)
                    group(ff[2 * (m % 2) + 1], w2, m, yt_hi, yt_lo, DC, fast).then_inc(s_l1b, 1)

            def layer2(b, ms, fast):
                for m in ms:
                    if m == 0:
                        pe.wait_ge(s_f1, b * HC + HC - 1)
                    if m >= 4:
                        pe.wait_ge(s_g2, b * HC + m - 3)
                    group(ff[m % 4], h1w, m, ha_hi, ha_lo, HC, fast,
                          (lambda k: pe.wait_ge(s_f1lo, b * HC + k + 1)) if m == 0 else None).then_inc(s_l2, 1)

            def layer3(b, ms, fast):
                for m in ms:
                    if m < 4:
                        pe.wait_ge(s_g2, b * HC + m + 5)
                    else:
                        pe.wait_ge(s_g3, b * HC + m - 3)
                    group(ff[m % 4], h2w, m, hb_hi, hb_lo, HC, fast,
                          (lambda k: pe.wait_ge(s_g2lo, b * HC + k + 1)) if m == 0 else None).then_inc(s_l3, 1)

            def layer4(b, fast):
                for t in range(TPB):
                    n = 0
                    for k in range(HC):
                        if t == 0:
                            pe.wait_ge(s_g3lo, b * HC + k + 1)
                        for x in (ha_hi, ha_lo):
                            a, y = x[:, k, t * P:(t + 1) * P], w3[:, k, :]
                            if not fast:
                                a, y = a.bitcast(fp32), y.bitcast(fp32)
                            last = mm(pyo[t // 2][:, (t % 2) * D:(t % 2 + 1) * D], a, y, start=n == 0, stop=n == 2 * HC - 1)
                            n += 1
                    if t % 2:
                        last.then_inc(s_l4, 1)

            pe.wait_ge(s_ident, 1)
            p1_transpose(0, first=True)
            pe.wait_ge(s_wlo, 2)
            p1_gates(0, 0)
            p1_gates(0, 1)
            p1_back(0)
            ffn_transpose(0)
            pe.wait_ge(s_raw, 16 * 7)
            pe.wait_ge(s_flag, 1)
            needs_split = pe.value_load(split_flag[0:1, 0:1], min_val=0, max_val=1)

            def both(layer, *args):
                with pe.If(needs_split == 0):
                    layer(*args, True)
                with pe.Else():
                    layer(*args, False)

            with pe.Fori(0, NBLK - 1) as i:
                both(layer1, i)
                both(layer2, i, range(0, 2))
                p1_transpose(i + 1)
                both(layer2, i, range(2, 4))
                p1_gates(i + 1, 0)
                both(layer2, i, range(4, 6))
                p1_gates(i + 1, 1)
                both(layer2, i, range(6, 8))
                both(layer3, i, range(0, 4))
                p1_back(i + 1)
                both(layer3, i, range(4, 8))
                ffn_transpose(i + 1)
                both(layer4, i)
            both(layer1, NBLK - 1)
            both(layer2, NBLK - 1, range(8))
            both(layer3, NBLK - 1, range(8))
            both(layer4, NBLK - 1)

        @block.scalar
        def _(act):
            fn = nc.scalar.activation

            def p1_roots(b):
                act.wait_ge(s_v1, b + 1)
                fn(r1a[:, :, :], v1a[:, :, :], ACT.Sqrt).then_inc(s_r1, 1)

            def p1_affine(b):
                for c in range(DC):
                    act.wait_ge(s_t1, b * DC + c + 1)
                    fn(act2[:, c, :], pt[c][:, :], ACT.Identity, scale=vec("gamma", c), bias=vec("beta", c)).then_inc(s_aff, 1)

            def p1_gates(b, m):
                act.wait_ge(s_z, b * DC + m + 1)
                if m == 0:
                    act.wait_ge(s_nt, b * DC + DC)
                else:
                    act.wait_ge(s_scan, b * DC + m)
                fn(act2[:, 0, :], pt[0][:, :], ACT.Sigmoid, bias=vec("bg", m)).then_inc(s_sig, 1)
                fn(act2[:, 1, :], pt[0][:, :], ACT.Sigmoid, bias=neg_bg[:, m:m + 1], scale=-1.0).then_inc(s_sig, 1)

            def roots(b, s_in, s_out, v, r):
                act.wait_ge(s_in, b + 1)
                fn(r, v, ACT.Sqrt).then_inc(s_out, 1)

            def p1_out(b):
                roots(b, s_vo, s_ro, v1a[:, 0, :], r1a[:, 0, :])
                roots(b, s_v2, s_r2, v1a[:, 1, :], r1a[:, 1, :])

            def ffn_in(b):
                for c in range(DC):
                    act.wait_ge(s_t2, b * DC + c + 1)
                    fn(yt_hi[:, c, :], pt[c][:, :], ACT.Copy).then_inc(s_yhi, 1)

            def layer1(b):
                for m in range(HC):
                    act.wait_ge(s_l1a, b * HC + m + 1)
                    if m >= 2:
                        act.wait_ge(s_f1, b * HC + m - 1)
                    fn(act2[:, m % 2, :], ff[2 * (m % 2)][:, :], ACT.Silu, scale=vec("w1_s", m)).then_inc(s_silu, 1)
                    act.wait_ge(s_f1, b * HC + m + 1)
                    fn(ha_hi[:, m, :], f2[:, m % 2, :], ACT.Copy).then_inc(s_f1hi, 1)

            def hidden(b, ms, s_in, s_low, s_out, scale):
                for m in ms:
                    act.wait_ge(s_in, b * HC + m + 1)
                    if m >= 2:
                        act.wait_ge(s_low, b * HC + m - 1)
                    fn(f2[:, m % 2, :], ff[m % 4][:, :], ACT.Gelu, scale=vec(scale, m)).then_inc(s_out, 1)

            def layer2(b, ms):
                hidden(b, ms, s_l2, s_g2lo, s_g2, "h1_s")

            def layer3(b, ms):
                hidden(b, ms, s_l3, s_g3lo, s_g3, "h2_s")

            act.wait_ge(s_const, 32)
            fn(neg_bg[:, :], vecs[:, VEC["bg"]:VEC["bg"] + DC], ACT.Copy, scale=-1.0).then_inc(s_masks, 1)
            p1_roots(0)
            p1_affine(0)

            def round_weights(ns):
                for n in ns:
                    act.wait_ge(s_stage[n], 16)
                    fn(ffn_weights[n][2], ffn_weights[n][1][:, :], ACT.Copy).then_inc(s_round, 1)

            round_weights(range(0, 3))
            act.wait_ge(s_masks, 3)
            p1_gates(0, 0)
            p1_gates(0, 1)
            round_weights(range(3, 5))
            p1_out(0)
            ffn_in(0)
            round_weights(range(5, 7))
            with act.Fori(0, NBLK - 1) as i:
                layer1(i)
                p1_roots(i + 1)
                layer2(i, range(0, 2))
                p1_affine(i + 1)
                layer2(i, range(2, 4))
                p1_gates(i + 1, 0)
                layer2(i, range(4, 6))
                p1_gates(i + 1, 1)
                layer2(i, range(6, 8))
                layer3(i, range(0, 4))
                p1_out(i + 1)
                layer3(i, range(4, 8))
                ffn_in(i + 1)
                roots(i, s_v4, s_r4, v2a[:, :], r2a[:, :])
            layer1(NBLK - 1)
            layer2(NBLK - 1, range(8))
            layer3(NBLK - 1, range(8))
            roots(NBLK - 1, s_v4, s_r4, v2a[:, :], r2a[:, :])

        @block.vector
        def _(dve):
            ts, tt, stt, cp = nc.vector.tensor_scalar, nc.vector.tensor_tensor, nc.vector.scalar_tensor_tensor, nc.vector.tensor_copy

            p1, p2, p3 = Steps(dve, s_p1, 16), Steps(dve, s_p2, 3), Steps(dve, s_p3, 5)

            def stats(steps, src, st, mv):
                for t in range(TPB):
                    last = nc.vector.bn_stats(st[:, t, :], src[:, t, :])
                steps.link(last)
                dve.sem_inc(s_dve_on)
                for t in range(TPB):
                    last = nc.vector.bn_aggr(mv[:, t, :], st[:, t, :])
                steps.link(last)

            def recip_var(steps, mv, dst, s_out):
                steps.link(ts(dst, mv[:, :, 1], LN_EPS, None, ADD))
                nc.vector.reciprocal(dst, dst).then_inc(s_out, 1)

            def p1_in(b):
                p1.start(b)
                dve.wait_ge(s_x, (b + 1) * 16)
                stats(p1, xa, st1, mv1)
                p1.link(ts(v1a[:, 0, :], mv1[:, :, 1], LN_EPS, None, ADD))
                p1.link(nc.vector.reciprocal(v1a[:, 0, :], v1a[:, 0, :]))
                p1.link(tt(v1a[:, 1, :], mv1[:, :, 1], v1a[:, 0, :], MUL))
                p1.link(ts(v1a[:, 1, :], v1a[:, 1, :], LN_EPS, None, ADD))
                nc.vector.reciprocal(v1a[:, 1, :], v1a[:, 1, :]).then_inc(s_v1, 1)
                dve.wait_ge(s_r1, b + 1)
                p1.mark(tt(r12[:, :], r1a[:, 0, :], r1a[:, 1, :], MUL))
                p1.link(nc.vector.reciprocal(inv_r2[:, :], r1a[:, 1, :]))
                for t in range(TPB):
                    last = ts(yn[:, t, :], xa[:, t, :], mv1[:, t, 0:1], r12[:, t:t + 1], SUB, MUL)
                last.then_inc(s_yn, 1)

            def p1_split(b):
                for c in range(DC):
                    dve.wait_ge(s_aff, b * DC + c + 1)
                    last = cp(yt_hi[:, c, :], act2[:, c, :])
                p1.link(last)
                for c in range(DC):
                    tt(yt_lo[:, c, :], act2[:, c, :], yt_hi[:, c, :].bitcast(fp32), SUB).then_inc(s_nt, 1)

            def p1_scan(b, m):
                dve.wait_ge(s_c, b * DC + m + 1)
                dve.wait_ge(s_sig, (b * DC + m) * 2 + 2)
                stt(zc[:, :], pt[1][:, :], vec("bc", m), act2[:, 0, :], ADD, MUL).then_inc(s_zc, 1)
                dve.wait_ge(s_zc, b * DC + m + 1)
                nc.vector.tensor_tensor_scan(hs[:, m, :], act2[:, 1, :], zc[:, :], carry[:, m:m + 1], MUL, ADD).then_inc(s_scan, 1)
                dve.wait_ge(s_scan, b * DC + m + 1)
                p1.link(tt(carry[:, m:m + 1], hs[:, m, BLK - 1:BLK], carry_on[:, bass.ds(b + 1, 1)], MUL))

            def p1_out(b):
                dve.wait_ge(s_ht, b + 1)
                for t in range(TPB):
                    last = stt(o1[:, t, :], yn[:, t, :], inv_r2[:, t:t + 1], pt[t // 2][:, (t % 2) * D:(t % 2 + 1) * D], MUL, ADD)
                p1.link(last)
                stats(p1, o1, st1, mv1)
                recip_var(p1, mv1, v1a[:, 0, :], s_vo)
                dve.wait_ge(s_ro, b + 1)
                for t in range(TPB):
                    last = ts(o1[:, t, :], o1[:, t, :], mv1[:, t, 0:1], r1a[:, 0, t:t + 1], SUB, MUL)
                p1.link(last)
                tt(xa[:, :, :], xa[:, :, :], o1[:, :, :], ADD).then_inc(s_xa, 1)
                p1.end()
                dve.wait_ge(s_xa, b + 1)

            def ffn_norm(b):
                p2.start(b)
                stats(p2, xa, st1, mv1)
                recip_var(p2, mv1, v1a[:, 1, :], s_v2)
                dve.wait_ge(s_r2, b + 1)
                for t in range(TPB):
                    last = ts(yn[:, t, :], xa[:, t, :], mv1[:, t, 0:1], r1a[:, 1, t:t + 1], SUB, MUL)
                last.then_inc(s_y2, 1)
                p2.end()

            def ffn_in(b):
                for c in range(DC):
                    dve.wait_ge(s_yhi, b * DC + c + 1)
                    tt(yt_lo[:, c, :], pt[c][:, :], yt_hi[:, c, :].bitcast(fp32), SUB).then_inc(s_ylo, 1)

            def layer1(b):
                for m in range(HC):
                    dve.wait_ge(s_l1b, b * HC + m + 1)
                    dve.wait_ge(s_silu, b * HC + m + 1)
                    if m >= 2:
                        dve.wait_ge(s_f1lo, b * HC + m - 1)
                    stt(f2[:, m % 2, :], ff[2 * (m % 2) + 1][:, :], vec("w2_s", m), act2[:, m % 2, :], MUL, MUL).then_inc(s_f1, 1)
                    if m:
                        low1(b, m - 1)
                low1(b, HC - 1)

            def low1(b, m):
                dve.wait_ge(s_f1hi, b * HC + m + 1)
                tt(ha_lo[:, m, :], f2[:, m % 2, :], ha_hi[:, m, :].bitcast(fp32), SUB).then_inc(s_f1lo, 1)

            def hidden(b, ms, s_in, s_high, s_low, hi, lo):
                for m in ms:
                    dve.wait_ge(s_in, b * HC + m + 1)
                    cp(hi[:, m, :], f2[:, m % 2, :]).then_inc(s_high, 1)
                    dve.wait_ge(s_high, b * HC + m + 1)
                    tt(lo[:, m, :], f2[:, m % 2, :], hi[:, m, :].bitcast(fp32), SUB).then_inc(s_low, 1)

            def layer2(b, ms):
                hidden(b, ms, s_g2, s_g2hi, s_g2lo, hb_hi, hb_lo)

            def layer3(b, ms):
                hidden(b, ms, s_g3, s_g3hi, s_g3lo, ha_hi, ha_lo)

            def ffn_out(b, first=False):
                p3.start(b)
                if not first:
                    dve.wait_ge(s_st, b * 16)
                for n in range(2):
                    dve.wait_ge(s_l4, 2 * b + n + 1)
                    for t in range(2 * n, 2 * n + 2):
                        last = tt(o2[:, t, :], pyo[n][:, (t % 2) * D:(t % 2 + 1) * D], w3s_row[:, :], MUL)
                p3.link(last)
                stats(p3, o2, st2, mv2)
                p3.link(ts(v2a[:, :], mv2[:, :, 1], LN_EPS, None, ADD))
                nc.vector.reciprocal(v2a[:, :], v2a[:, :]).then_inc(s_v4, 1)
                dve.wait_ge(s_r4, b + 1)
                for t in range(TPB):
                    last = ts(o2[:, t, :], o2[:, t, :], mv2[:, t, 0:1], r2a[:, t:t + 1], SUB, MUL)
                p3.link(last)
                dve.wait_ge(s_xb, b + 1)
                tt(o2[:, :, :], o2[:, :, :], xb[:, :, :], ADD).then_inc(s_o2, 1)
                p3.end()

            nc.vector.memset(carry[:, :], 0.0)
            nc.vector.memset(carry_on[:, 0:NBLK + 2:2], 0.0).then_inc(s_masks, 1)
            nc.vector.memset(carry_on[:, 1:NBLK + 2:2], 1.0).then_inc(s_masks, 1)
            p1_in(0)
            p1_split(0)
            dve.wait_ge(s_wsplit, 2)
            tt(w_gate_lo[:, :, :], o2[:, 0:2, :], w_gate_hi[:, :, :].bitcast(fp32), SUB).then_inc(s_wlo, 1)
            tt(w_cand_lo[:, :, :], o2[:, 2:4, :], w_cand_hi[:, :, :].bitcast(fp32), SUB).then_inc(s_wlo, 1)

            def weight_check(ns):
                for n in ns:
                    _, staged, rounded = ffn_weights[n]
                    dve.wait_ge(s_round, n + 1)
                    stt(rounded, rounded.bitcast(fp32), 0.0, staged[:, :], ADD, ALU.not_equal,
                        accum_out=chk[:, n:n + 1]).then_inc(s_chk, 1)

            weight_check(range(0, 3))
            dve.wait_ge(s_masks, 3)
            p1_scan(0, 0)
            p1_scan(0, 1)
            weight_check(range(3, 5))
            p1_out(0)
            ffn_norm(0)
            ffn_in(0)
            weight_check(range(5, 7))
            dve.wait_ge(s_chk, 7)
            nc.vector.reduce_sum(chk1[:, :], chk[:, :], axis=AX.X).then_inc(s_flag0, 1)
            dve.wait_ge(s_flag1, 1)
            ts(split_flag[:, :], chk_all[0:1, :], 0.0, None, ALU.is_gt).then_inc(s_flag, 1)
            layer1(0)
            p1_in(1)
            layer2(0, range(0, 2))

            def rest(i, first=False):
                p1_split(i + 1)
                layer2(i, range(2, 4))
                p1_scan(i + 1, 0)
                layer2(i, range(4, 6))
                p1_scan(i + 1, 1)
                layer2(i, range(6, 8))
                layer3(i, range(0, 4))
                p1_out(i + 1)
                ffn_norm(i + 1)
                layer3(i, range(4, 8))
                ffn_in(i + 1)
                ffn_out(i, first)

            rest(0, True)
            with dve.Fori(1, NBLK - 1) as i:
                layer1(i)
                p1_in(i + 1)
                layer2(i, range(0, 2))
                rest(i)
            layer1(NBLK - 1)
            layer2(NBLK - 1, range(8))
            layer3(NBLK - 1, range(8))
            ffn_out(NBLK - 1)

        block_ctx.close()
        end_phase()

        cursor[0] = shared_from
        kvr = {n: [[sb(f"w_{n}_{when}_{s}", [P, DC, D], fp32r) for s in ("hi", "lo")] for when in ("now", "before")]
               for n in ("k", "v", "r")}
        w_out = [sb(f"w_out_{s}", [P, DC, D], fp32r) for s in ("hi", "lo")]
        w_r2 = [sb(f"w_r2_{s}", [P, DC, D], fp32r) for s in ("hi", "lo")]
        w_k2 = [sb(f"w_k2_{s}", [P, DC, HID], fp32r) for s in ("hi", "lo")]
        w_v2 = [sb(f"w_v2_{s}", [P, HC, D], fp32r) for s in ("hi", "lo")]
        x_pre, x_fin = sb("x_pre", [P, TPB, D]), sb("x_fin", [P, TPB, D])
        y_new, y_res = sb("y_new", [P, TPB, D]), sb("y_res", [P, TPB, D])
        y_rms = sb("y_rms", [P, TPB, D])
        x1 = y_res
        h2n = sb("h2n", [P, TPB, D])
        xr = sb("xr", [P, TPB, ROW])
        EXT = BLK + 2
        hT = [sb(f"hT_{s}", [P, DC, EXT], fp32r) for s in ("hi", "lo")]
        h2T = sb("h2T", [P, DC, EXT])
        ek, ekt, e_r = (sb(n, [P, DC, BLK]) for n in ("ek", "ekt", "e_r"))
        st_a, st_b = sb("st_a", [P, DC, EXT]), sb("st_b", [P, DC, EXT])
        ekv, num = sb("ekv", [P, BLK]), sb("num", [P, DC, BLK])
        rw = [sb(f"rw_{s}", [P, DC, BLK], fp32r) for s in ("hi", "lo")]
        mixf = sb("mixf", [P, 2, BLK])
        d2 = sb("d2", [P, DC, BLK], at=place["h2n"])
        xk2 = [sb(f"xk2_{s}", [P, DC, BLK], fp32r) for s in ("hi", "lo")]
        xr2 = [sb(f"xr2_{s}", [P, DC, BLK], fp32r) for s in ("hi", "lo")]
        kf, kg = sb("kf", [P, 2, BLK]), sb("kg", [P, 2, BLK])
        k2 = [sb(f"k2_{s}", [P, HC, BLK], fp32r) for s in ("hi", "lo")]
        o3 = sb("o3", [P, TPB, D])
        ew = sb("ew", [P, DC])
        one_minus = sb("one_minus", [P, 3 * DC])
        bnA, mvA = sb("bnA", [P, TPB, 6]), sb("mvA", [P, TPB, 2])
        bnB, mvB = sb("bnB", [P, TPB, 6]), sb("mvB", [P, TPB, 2])
        varA, rootA = sb("varA", [P, 2, TPB]), sb("rootA", [P, 2, TPB])
        varB, rootB = sb("varB", [P, TPB]), sb("rootB", [P, TPB])
        varC, rootC = sb("varC", [P, TPB]), sb("rootC", [P, TPB])
        msq, r12A = sb("msq", [P, TPB]), sb("r12A", [P, TPB])
        v0, v1, i0, i1 = (sb(n, [P, TPB]) for n in ("v0", "v1", "i0", "i1"))
        oh0, oh1 = sb("oh0", [P, TPB, EXP]), sb("oh1", [P, TPB, EXP])
        eq, key, g2, pr = (sb(n, [P, TPB, EXP], at=place["ekv"] + 4 * j * TPB * EXP)
                           for j, n in enumerate(("eq", "key", "g2", "pr")))
        chosen = sb("chosen", [P, TPB, EXP], bf16)
        gap, e_gap, gate0, gate1 = (sb(n, [P, TPB]) for n in ("gap", "e_gap", "gate0", "gate1"))
        pos_f, pos_i = sb("pos_f", [P, 2 * TPB]), sb("pos_i", [P, 2 * TPB], i32)
        varD, rootD = sb("varD", [P, TPB]), sb("rootD", [P, TPB])
        xtT = sb("xtT", [P, DC, BLK], at=place["h2n"])
        stage = {}
        at = place["k2_hi"]
        for n, size in (("k", DC * D), ("v", DC * D), ("r", DC * D), ("out", DC * D), ("r2", DC * D),
                        ("k2", DC * HID), ("v2", HC * D)):
            stage[n] = sb(f"stage_{n}", [P, size], at=at)
            at += 4 * size
        fold = [sb(f"fold_{n}", [P, DC * D], at=place["xk2_hi"] + n * 4 * DC * D) for n in range(2)]

        b_t = bank[0:2]
        b_w = bank[2:4]
        b_k, b_r = bank[4], bank[5]
        b_v = bank[6:8]

        c_stage = {n: sem(f"staged_{n}") for n in stage}
        c_prep, c_const = sem("c_prep_steps"), sem("c_constants")
        c_act_const = sem("c_act_constants")
        c_w = sem("c_weights_split")
        c_x, c_xf = sem("c_x_loaded"), sem("c_x_reloaded")
        c_pre, c_va, c_ra, c_y = sem("c_pre_steps"), sem("c_pre_variances"), sem("c_pre_roots"), sem("c_normalized")
        c_yn, c_vread, c_f1 = sem("c_residual_ready"), sem("c_values_read"), sem("c_gated")
        c_yres = sem("c_residual_copied")
        c_t, c_carry, c_hhi, c_hsplit = sem("c_transposed"), sem("c_h_carried"), sem("c_h_high"), sem("c_h_split")
        c_kp, c_vp, c_rp = sem("c_key_product"), sem("c_value_product"), sem("c_recept_product")
        c_ek, c_er = sem("c_exp_key"), sem("c_exp_recept")
        c_scan = sem("c_scan_steps")
        c_rw, c_rwhi, c_rwlo = sem("c_wkv_ready"), sem("c_wkv_high"), sem("c_wkv_low")
        c_wo = sem("c_out_product")
        c_x1s, c_x1, c_vb, c_rb, c_h2n = sem("c_x1_steps"), sem("c_x1_ready"), sem("c_x1_variances"), sem("c_x1_roots"), sem("c_x1_normalized")
        c_t2, c_h2 = sem("c_x1_transposed"), sem("c_h2_affine")
        c_d2, c_mix, c_mixhi, c_mixlo, c_h2c = sem("c_h2_step"), sem("c_mixed"), sem("c_mix_high"), sem("c_mix_low"), sem("c_h2_carried")
        c_k2p, c_relu, c_k2hi, c_k2sq, c_k2lo = sem("c_key2_product"), sem("c_relu"), sem("c_key2_high"), sem("c_key2_squared"), sem("c_key2_low")
        c_r2p, c_r2 = sem("c_recept2_product"), sem("c_recept2_ready")
        c_v2p = sem("c_value2_product")
        c_fin, c_vc, c_rc, c_done, c_st = sem("c_final_steps"), sem("c_final_variances"), sem("c_final_roots"), sem("c_block_done"), sem("c_stored")
        r_pool_on = sem("r_pool_goes_on")
        c_dve_on = sem("c_vector_goes_on")
        r_iota, r_const, r_wg = sem("r_iotas"), sem("r_constants"), sem("r_gate_loaded")
        r_vd, r_rd, r_xt = sem("r_variances"), sem("r_roots"), sem("r_normalized")
        r_t, r_tc, r_g = sem("r_transposed"), sem("r_copied"), sem("r_gate_product")
        r_steps, r_dv, r_ex, r_m, r_rank = sem("r_steps"), sem("r_gap"), sem("r_exp"), sem("r_chosen"), sem("r_rank_product")
        r_run, r_pos, r_sc = sem("r_ranks_read"), sem("r_positions"), sem("r_scattered")

        block_ctx = ExitStack()
        block = block_ctx.enter_context(nc.Block())

        @block.sync
        def _(sp):
            sp.dma_start(x_pre[:, :, :], mid_blocks[:, 0:TPB, :]).then_inc(c_x, 16)
            for n, src in (("k", wk_in), ("v", wv_in), ("r", wr_in), ("out", wo_in), ("k2", wk2_in), ("r2", wr2_in), ("v2", wv2_in)):
                sp.dma_start(stage[n][:, :], src).then_inc(c_stage[n], 16)

            sp.dma_start(wg8[:, :, :], wg8_in).then_inc(r_wg, 16)
            sp.dma_start(x_fin[:, :, :], mid_blocks[:, 0:TPB, :]).then_inc(c_xf, 16)
            sp.wait_ge(c_yn, 1)
            sp.dma_start(x_pre[:, :, :], mid_blocks[:, TPB:2 * TPB, :]).then_inc(c_x, 16)

            def load_pre(i):
                sp.wait_ge(c_yn, i + 2)
                sp.dma_start(x_pre[:, :, :], mid_blocks[:, bass.ds((i + 2) * TPB, TPB), :]).then_inc(c_x, 16)

            def store(b, last=False):
                sp.wait_ge(c_done, b + 1)
                sp.dma_start(x3_blocks[:, bass.ds(b * TPB, TPB), :], o3[:, :, :]).then_inc(c_st, 16)
                if not last:
                    sp.dma_start(x_fin[:, :, :], mid_blocks[:, bass.ds((b + 1) * TPB, TPB), :]).then_inc(c_xf, 16)

            load_pre(0)
            with sp.Fori(1, NBLK - 2) as i:
                load_pre(i)
                store(i - 1)
            store(NBLK - 3)
            store(NBLK - 2)
            store(NBLK - 1, True)
            sp.wait_ge(c_st, 16 * NBLK)
            sp.wait_ge(r_sc, 16 * 2 * TPB * NBLK)

        @block.gpsimd
        def _(pool):
            def squares(b):
                for m in range(HC):
                    pool.wait_ge(c_relu, b * HC + m + 1)
                    if m >= 2:
                        pool.wait_ge(c_k2lo, b * HC + m - 1)
                    nc.gpsimd.tensor_tensor(kg[:, m % 2, :], kf[:, m % 2, :], kf[:, m % 2, :], MUL).then_inc(c_k2sq, 1)
                    pool.wait_ge(c_k2sq, b * HC + m + 1)
                    pool.wait_ge(c_k2hi, b * HC + m + 1)
                    nc.gpsimd.tensor_tensor(k2[1][:, m, :], kg[:, m % 2, :], k2[0][:, m, :].bitcast(fp32), SUB).then_inc(c_k2lo, 1)

            def scatter(b):
                pool.wait_ge(r_pos, b + 1)
                pool.sem_inc(r_pool_on)
                for k in range(2):
                    for t in range(TPB):
                        nc.gpsimd.indirect_dma_start(
                            routed, bass.IndirectOffsetOnAxis(ap=pos_i[:, k * TPB + t:k * TPB + t + 1], axis=0),
                            xr[:, t, :], None).then_inc(r_sc, 16)

            nc.gpsimd.iota(eno_i[:, :], pattern=[[1, EXP]], base=0, channel_multiplier=0).then_inc(r_iota, 1)
            nc.gpsimd.iota(ids_i[:, :], pattern=[[2 * P, TPB]], base=0, channel_multiplier=2).then_inc(r_iota, 1)
            nc.gpsimd.memset(upper[:, :], 1.0).then_inc(r_iota, 1)
            pool.wait_ge(r_iota, 3)
            nc.gpsimd.affine_select(out=upper[:, :], in_=upper[:, :], compare_op=ALU.is_gt, fill=0.0, base=0,
                                    pattern=[[1, P]], channel_multiplier=-1).then_inc(r_iota, 1)
            squares(0)
            with pool.Fori(1, NBLK) as i:
                squares(i)
                scatter(i - 1)
            scatter(NBLK - 1)

        @block.tensor
        def _(pe):
            mm = nc.tensor.matmul

            def transpose(dst, src, b, s_in, s_out):
                pe.wait_ge(s_in, b + 1)
                for c in range(DC):
                    for t in range(TPB):
                        last = nc.tensor.transpose(dst[c][:, t * P:(t + 1) * P], src[:, t, c * P:(c + 1) * P], ident[:, :])
                    last.then_inc(s_out, 1)

            def product(dst, m, pairs):
                terms = [(w[i][:, c, m * P:(m + 1) * P], y[j](c)) for w, y in pairs for c in range(DC) for i, j in ((0, 0), (1, 0), (0, 1))]
                for n, (a, y) in enumerate(terms):
                    last = mm(dst[:, :], a, y, start=n == 0, stop=n == len(terms) - 1)
                return last

            now = [lambda c, h=h: h[:, c, 1:BLK + 1] for h in hT]
            before = [lambda c, h=h: h[:, c, 0:BLK] for h in hT]

            def kvr_products(b, m, first=False, second=False):
                pe.wait_ge(c_hsplit, b * DC + DC)
                if m == 0:
                    if not first and not second:
                        pe.wait_ge(c_relu, b * HC - HC)
                else:
                    pe.wait_ge(c_ek, (b * DC + m) * 2)
                product(b_k, m, ((kvr["k"][0], now), (kvr["k"][1], before))).then_inc(c_kp, 1)
                product(b_v[m], m, ((kvr["v"][0], now), (kvr["v"][1], before))).then_inc(c_vp, 1)
                if m:
                    pe.wait_ge(c_er, b * DC + m)
                product(b_r, m, ((kvr["r"][0], now), (kvr["r"][1], before))).then_inc(c_rp, 1)

            def token_product(dst, x, w, n_k, s_done):
                for t in range(TPB):
                    terms = [(x[i][:, k, t * P:(t + 1) * P], w[j][:, k, :]) for k in range(n_k) for i, j in ((0, 0), (0, 1), (1, 0))]
                    for n, (a, y) in enumerate(terms):
                        last = mm(dst[t // 2][:, (t % 2) * D:(t % 2 + 1) * D], a, y, start=n == 0, stop=n == len(terms) - 1)
                    if t % 2:
                        last.then_inc(s_done, 1)

            def out_product(b, first=False):
                pe.wait_ge(c_rwlo, b * DC + DC)
                if not first:
                    pe.wait_ge(c_r2, b * 2)
                token_product(b_w, rw, w_out, DC, c_wo)

            def keys2(b, ms):
                pe.wait_ge(c_mixlo, b * 4 + 2)
                for m in ms:
                    if m >= 2:
                        pe.wait_ge(c_relu, b * HC + m - 1)
                    product((b_k, b_r)[m % 2], m, ((w_k2, [lambda c, h=h: h[:, c, :] for h in xk2]),)).then_inc(c_k2p, 1)

            def recept2(b):
                pe.wait_ge(c_mixlo, b * 4 + 4)
                token_product(b_w, xr2, w_r2, DC, c_r2p)

            def values2(b):
                pe.wait_ge(c_k2lo, b * HC + HC)
                token_product(b_t, k2, w_v2, HC, c_v2p)

            def route_in(b):
                pe.wait_ge(r_xt, b + 1)
                for c in range(DC):
                    for t in range(TPB):
                        last = nc.tensor.transpose(b_w[c][:, t * P:(t + 1) * P], xr[:, t, c * P:(c + 1) * P], ident[:, :])
                    last.then_inc(r_t, 1)

            def route_gate(b):
                pe.wait_ge(r_tc, b * DC + DC)
                for t in range(TPB):
                    for c in range(DC):
                        last = mm(b_w[0][:, t * EXP:(t + 1) * EXP], xtT[:, c, t * P:(t + 1) * P], wg8[:, c, :], start=c == 0, stop=c == DC - 1)
                last.then_inc(r_g, 1)

            def route_rank(b):
                pe.wait_ge(r_m, b + 1)
                for t in range(TPB):
                    for n in range(t + 1):
                        mm(b_w[1][:, t * EXP:(t + 1) * EXP], (upper if n == t else ones_bf)[:, :], chosen[:, n, :], start=n == 0, stop=n == t)
                for n in range(TPB):
                    last = mm(b_w[1][:, TPB * EXP:(TPB + 1) * EXP], ones_bf[:, :], chosen[:, n, :], start=n == 0, stop=n == TPB - 1)
                last.then_inc(r_rank, 1)

            def transpose_in(b):
                if not (isinstance(b, int) and b == 0):
                    pe.wait_ge(c_vread, b * DC)
                transpose(b_v, y_rms, b, c_y, c_t)

            def transpose_mid(b):
                if not (isinstance(b, int) and b == 0):
                    pe.wait_ge(c_f1, b)
                transpose(b_t, h2n, b, c_h2n, c_t2)

            def second_half(b, first=False, more=True):
                keys2(b, range(0, 5))
                if not first:
                    route_in(b - 1)
                keys2(b, range(5, 6))
                if not first:
                    route_gate(b - 1)
                keys2(b, range(6, HC))
                if not first:
                    route_rank(b - 1)
                values2(b)
                if more:
                    transpose_in(b + 2)
                if not first:
                    pe.wait_ge(r_run, b)
                recept2(b)

            transpose_in(0)
            pe.wait_ge(c_w, 3)
            kvr_products(0, 0, True)
            kvr_products(0, 1, True)
            transpose_in(1)

            def step(i, first=False, more=True):
                out_product(i, first)
                kvr_products(i + 1, 0, second=first)
                transpose_mid(i)
                kvr_products(i + 1, 1)
                pe.wait_ge(c_ek, (i + 2) * DC * 2)
                pe.wait_ge(c_er, (i + 2) * DC)
                second_half(i, first, more)

            pe.wait_ge(c_w, 7)
            step(0, True)
            with pe.Fori(1, NBLK - 2) as i:
                step(i)
            step(NBLK - 2, more=False)
            out_product(NBLK - 1)
            transpose_mid(NBLK - 1)
            second_half(NBLK - 1, more=False)
            pe.wait_ge(c_r2, NBLK * 2)
            route_in(NBLK - 1)
            route_gate(NBLK - 1)
            route_rank(NBLK - 1)

        @block.scalar
        def _(act):
            fn = nc.scalar.activation

            def root(b, s_in, s_out, v, r):
                act.wait_ge(s_in, b + 1)
                fn(r, v, ACT.Sqrt).then_inc(s_out, 1)

            def pre_root(b):
                root(b, c_va, c_ra, varA[:, :, :], rootA[:, :, :])

            def h_high(b):
                act.wait_ge(c_carry, b + 1)
                for c in range(DC):
                    act.wait_ge(c_t, b * DC + c + 1)
                    fn(hT[0][:, c, 1:BLK + 1], b_v[c][:, :], ACT.Copy, scale=vec("ln1_w", c)).then_inc(c_hhi, 1)

            def exp_key(b, m):
                act.wait_ge(c_kp, b * DC + m + 1)
                fn(ek[:, m, :], b_k[:, :], ACT.Exp).then_inc(c_ek, 1)
                fn(ekt[:, m, :], b_k[:, :], ACT.Exp, bias=vec("first", m)).then_inc(c_ek, 1)

            def exp_recept(b, m):
                act.wait_ge(c_rp, b * DC + m + 1)
                fn(e_r[:, m, :], b_r[:, :], ACT.Exp, scale=-1.0).then_inc(c_er, 1)

            def wkv_high(b, m):
                act.wait_ge(c_rw, b * DC + m + 1)
                fn(rw[0][:, m, :], num[:, m, :], ACT.Copy).then_inc(c_rwhi, 1)

            def h2_affine(b):
                if isinstance(b, int) and b == 0:
                    pass
                else:
                    act.wait_ge(c_h2c, b)
                for c in range(DC):
                    act.wait_ge(c_t2, b * DC + c + 1)
                    fn(h2T[:, c, 1:BLK + 1], b_t[c][:, :], ACT.Copy, scale=vec("ln2_w", c)).then_inc(c_h2, 1)

            def mix_high(b):
                for n in range(4):
                    act.wait_ge(c_mix, b * 4 + n + 1)
                    fn((xk2, xr2)[n // 2][0][:, n % 2, :], mixf[:, n % 2, :], ACT.Copy).then_inc(c_mixhi, 1)

            def keys2(b, m):
                act.wait_ge(c_k2p, b * HC + m + 1)
                if m >= 2:
                    act.wait_ge(c_k2sq, b * HC + m - 1)
                fn(kf[:, m % 2, :], (b_k, b_r)[m % 2][:, :], ACT.Relu).then_inc(c_relu, 1)
                act.wait_ge(c_relu, b * HC + m + 1)
                fn(k2[0][:, m, :], kf[:, m % 2, :], ACT.Square).then_inc(c_k2hi, 1)

            def recept2(b):
                for n in range(2):
                    act.wait_ge(c_r2p, b * 2 + n + 1)
                    fn(o3[:, 2 * n:2 * n + 2, :], b_w[n][:, :].rearrange("p (t d) -> p t d", d=D), ACT.Sigmoid).then_inc(c_r2, 1)

            def route_copy(b):
                for c in range(DC):
                    act.wait_ge(r_t, b * DC + c + 1)
                    fn(xtT[:, c, :], b_w[c][:, :], ACT.Copy).then_inc(r_tc, 1)

            def route_exp(b):
                act.wait_ge(r_dv, b + 1)
                fn(e_gap[:, :], gap[:, :], ACT.Exp).then_inc(r_ex, 1)

            fn(ew[:, :], vecs[:, VEC["decay"]:VEC["decay"] + DC], ACT.Exp).then_inc(c_act_const, 1)
            act.wait_ge(c_const, 1)
            fn(ew[:, :], ew[:, :], ACT.Exp).then_inc(c_act_const, 1)
            pre_root(0)
            h_high(0)
            for m in range(DC):
                exp_key(0, m)
                exp_recept(0, m)
            wkv_high(0, 0)
            wkv_high(0, 1)
            pre_root(1)
            h_high(1)

            def second_half(b, first=False, more=True):
                keys2(b, 0)
                if not first:
                    root(b - 1, c_vc, c_rc, varC[:, :], rootC[:, :])
                for m in range(1, 4):
                    keys2(b, m)
                if not first:
                    root(b - 1, r_vd, r_rd, varD[:, :], rootD[:, :])
                keys2(b, 4)
                if more:
                    pre_root(b + 2)
                keys2(b, 5)
                if not first:
                    route_copy(b - 1)
                keys2(b, 6)
                keys2(b, 7)
                if not first:
                    route_exp(b - 1)

            def recept2_out(b):
                if not (isinstance(b, int) and b == 0):
                    act.wait_ge(c_st, b * 16)
                recept2(b)

            def step(i, first=False, more=True):
                exp_key(i + 1, 0)
                root(i, c_vb, c_rb, varB[:, :], rootB[:, :])
                exp_recept(i + 1, 0)
                h2_affine(i)
                exp_key(i + 1, 1)
                mix_high(i)
                exp_recept(i + 1, 1)
                second_half(i, first, more)
                wkv_high(i + 1, 0)
                if more:
                    h_high(i + 2)
                recept2_out(i)
                wkv_high(i + 1, 1)

            step(0, first=True)
            with act.Fori(1, NBLK - 2) as i:
                step(i)
            step(NBLK - 2, more=False)
            b = NBLK - 1
            root(b, c_vb, c_rb, varB[:, :], rootB[:, :])
            h2_affine(b)
            mix_high(b)
            second_half(b, more=False)
            recept2_out(b)
            root(b, c_vc, c_rc, varC[:, :], rootC[:, :])
            root(b, r_vd, r_rd, varD[:, :], rootD[:, :])
            route_copy(b)
            route_exp(b)

        @block.vector
        def _(dve):
            ts, tt, stt, cp = nc.vector.tensor_scalar, nc.vector.tensor_tensor, nc.vector.scalar_tensor_tensor, nc.vector.tensor_copy

            pre_s, scan_s, x1_s, fin_s = Steps(dve, c_pre, 7), Steps(dve, c_scan, 18), Steps(dve, c_x1s, 5), Steps(dve, c_fin, 8)
            rt = Steps(dve, r_steps, 20)

            def stats(steps, src, bn, mv):
                for t in range(TPB):
                    last = nc.vector.bn_stats(bn[:, t, :], src[:, t, :])
                steps.link(last)
                dve.sem_inc(c_dve_on)
                for t in range(TPB):
                    last = nc.vector.bn_aggr(mv[:, t, :], bn[:, t, :])
                steps.link(last)

            def pre(b):
                pre_s.start(b)
                dve.wait_ge(c_x, (b + 1) * 16)
                stats(pre_s, x_pre, bnA, mvA)
                pre_s.link(ts(varA[:, 0, :], mvA[:, :, 1], LN_EPS, None, ADD))
                pre_s.link(nc.vector.reciprocal(varA[:, 0, :], varA[:, 0, :]))
                pre_s.link(tt(varA[:, 1, :], mvA[:, :, 1], varA[:, 0, :], MUL))
                pre_s.link(ts(varA[:, 1, :], varA[:, 1, :], RMS_EPS, None, ADD))
                nc.vector.reciprocal(varA[:, 1, :], varA[:, 1, :]).then_inc(c_va, 1)
                dve.wait_ge(c_ra, b + 1)
                pre_s.link(tt(r12A[:, :], rootA[:, 0, :], rootA[:, 1, :], MUL))
                for t in range(TPB):
                    last = ts(y_rms[:, t, :], x_pre[:, t, :], mvA[:, t, 0:1], r12A[:, t:t + 1], SUB, MUL)
                last.then_inc(c_y, 1)
                pre_s.end()

            def normed(b):
                for t in range(TPB):
                    last = ts(y_new[:, t, :], x_pre[:, t, :], mvA[:, t, 0:1], rootA[:, 0, t:t + 1], SUB, MUL)
                last.then_inc(c_yn, 1)

            def b_is_not_first(b):
                return not (isinstance(b, int) and b == 0)

            def h_carry(b):
                if b_is_not_first(b):
                    dve.wait_ge(c_rp, b * DC)
                    for h in hT:
                        last = tt(h[:, :, 0:1], h[:, :, BLK:BLK + 1].bitcast(fp32),
                                  carry_on[:, bass.ds(b, 1)].unsqueeze(1).to_broadcast([P, DC, 1]), MUL)
                else:
                    for h in hT:
                        last = cp(h[:, :, 0:1], carry_on[:, 0:1].unsqueeze(1).to_broadcast([P, DC, 1]))
                last.then_inc(c_carry, 1)

            def h_low(b):
                dve.wait_ge(c_carry, b + 1)
                for c in range(DC):
                    dve.wait_ge(c_hhi, b * DC + c + 1)
                    stt(hT[1][:, c, 1:BLK + 1], b_v[c][:, :], vec("ln1_w", c), hT[0][:, c, 1:BLK + 1].bitcast(fp32), MUL, SUB).then_inc(c_hsplit, 1)

            def scan(b, m):
                if m == 0:
                    scan_s.start(b)
                lo, hi = CLIP
                dve.wait_ge(c_ek, (b * DC + m) * 2 + 2)
                scan_s.mark(ts(ek[:, m, :], ek[:, m, :], lo, hi, MAX, MIN))
                scan_s.link(ts(ekt[:, m, :], ekt[:, m, :], lo, hi, MAX, MIN))
                dve.wait_ge(c_vp, b * DC + m + 1)
                scan_s.mark(tt(ekv[:, :], ek[:, m, :], b_v[m][:, :], MUL))
                tt(num[:, m, :], ekt[:, m, :], b_v[m][:, :], MUL).then_inc(c_vread, 1)
                scan_s.wait()
                dve.wait_ge(c_vread, b * DC + m + 1)
                decay = ew[:, m:m + 1].broadcast_to([P, BLK])
                scan_s.mark(nc.vector.tensor_tensor_scan(st_b[:, m, 1:BLK + 1], decay, ek[:, m, :], st_b[:, m, 0:1], MUL, ADD))
                scan_s.link(nc.vector.tensor_tensor_scan(st_a[:, m, 1:BLK + 1], decay, ekv[:, :], st_a[:, m, 0:1], MUL, ADD))
                scan_s.mark(tt(num[:, m, :], num[:, m, :], st_a[:, m, 0:BLK], ADD))
                scan_s.link(stt(ekt[:, m, :], st_b[:, m, 0:BLK], 1e-8, ekt[:, m, :], ADD, ADD))
                tt(st_a[:, m, 0:1], st_a[:, m, BLK:BLK + 1], carry_on[:, bass.ds(b + 1, 1)], MUL)
                tt(st_b[:, m, 0:1], st_b[:, m, BLK:BLK + 1], carry_on[:, bass.ds(b + 1, 1)], MUL)
                dve.wait_ge(c_er, b * DC + m + 1)
                scan_s.link(stt(ekt[:, m, :], e_r[:, m, :], 1.0, ekt[:, m, :], ADD, MUL))
                scan_s.link(nc.vector.reciprocal(ekt[:, m, :], ekt[:, m, :]))
                tt(num[:, m, :], num[:, m, :], ekt[:, m, :], MUL).then_inc(c_rw, 1)

            def wkv_low(b, m):
                dve.wait_ge(c_rwhi, b * DC + m + 1)
                tt(rw[1][:, m, :], num[:, m, :], rw[0][:, m, :].bitcast(fp32), SUB).then_inc(c_rwlo, 1)

            def out_add(b):
                x1_s.start(b)
                dve.wait_ge(c_yres, b + 1)
                for n in range(2):
                    dve.wait_ge(c_wo, b * 2 + n + 1)
                    last = tt(x1[:, 2 * n:2 * n + 2, :], y_res[:, 2 * n:2 * n + 2, :], b_w[n][:, :].rearrange("p (t d) -> p t d", d=D), ADD)
                last.then_inc(c_x1, 1)
                dve.wait_ge(c_x1, b + 1)
                stats(x1_s, x1, bnB, mvB)
                x1_s.link(tt(msq[:, :], mvB[:, :, 0], mvB[:, :, 0], MUL))
                x1_s.link(stt(varB[:, :], msq[:, :], RMS_EPS, mvB[:, :, 1], ADD, ADD))
                nc.vector.reciprocal(varB[:, :], varB[:, :]).then_inc(c_vb, 1)

            def x1_norm(b):
                dve.wait_ge(c_rb, b + 1)
                for t in range(TPB):
                    last = ts(h2n[:, t, :], x1[:, t, :], rootB[:, t:t + 1], None, MUL)
                last.then_inc(c_h2n, 1)

            def mixes(b):
                dve.wait_ge(c_h2, b * DC + DC)
                for c in range(DC):
                    last = tt(d2[:, c, :], h2T[:, c, 1:BLK + 1], h2T[:, c, 0:BLK], SUB)
                x1_s.link(last)
                for n in range(4):
                    kind, c = n // 2, n % 2
                    if n >= 2:
                        mix_low(b, n - 2)
                        dve.wait_ge(c_mixlo, b * 4 + n - 1)
                    stt(mixf[:, c, :], d2[:, c, :], vec(("mix_k2", "mix_r2")[kind], c), h2T[:, c, 0:BLK], MUL, ADD).then_inc(c_mix, 1)
                mix_low(b, 2)
                mix_low(b, 3)
                dve.wait_ge(c_mix, b * 4 + 4)
                tt(h2T[:, :, 0:1], h2T[:, :, BLK:BLK + 1], carry_on[:, bass.ds(b + 1, 1)].unsqueeze(1).to_broadcast([P, DC, 1]), MUL).then_inc(c_h2c, 1)
                x1_s.end()

            def mix_low(b, n):
                kind, c = n // 2, n % 2
                dve.wait_ge(c_mixhi, b * 4 + n + 1)
                tt((xk2, xr2)[kind][1][:, c, :], mixf[:, c, :], (xk2, xr2)[kind][0][:, c, :].bitcast(fp32), SUB).then_inc(c_mixlo, 1)

            def gated(b):
                fin_s.start(b)
                for n in range(2):
                    dve.wait_ge(c_v2p, b * 2 + n + 1)
                    dve.wait_ge(c_r2, b * 2 + n + 1)
                    last = tt(o3[:, 2 * n:2 * n + 2, :], o3[:, 2 * n:2 * n + 2, :], b_t[n][:, :].rearrange("p (t d) -> p t d", d=D), MUL)
                last.then_inc(c_f1, 1)
                dve.wait_ge(c_f1, b + 1)
                fin_s.mark(tt(o3[:, :, :], o3[:, :, :], x1[:, :, :], ADD))

            def final(b):
                fin_s.wait()
                stats(fin_s, o3, bnB, mvB)
                fin_s.link(ts(varC[:, :], mvB[:, :, 1], LN_EPS, None, ADD))
                nc.vector.reciprocal(varC[:, :], varC[:, :]).then_inc(c_vc, 1)
                dve.wait_ge(c_rc, b + 1)
                for t in range(TPB):
                    last = ts(o3[:, t, :], o3[:, t, :], mvB[:, t, 0:1], rootC[:, t:t + 1], SUB, MUL)
                fin_s.link(last)
                dve.wait_ge(c_xf, b * 16 + 16)
                tt(o3[:, :, :], o3[:, :, :], x_fin[:, :, :], ADD).then_inc(c_done, 1)
                dve.wait_ge(c_done, b + 1)
                stats(fin_s, o3, bnB, mvB)
                fin_s.link(ts(varD[:, :], mvB[:, :, 1], LN_EPS, None, ADD))
                nc.vector.reciprocal(varD[:, :], varD[:, :]).then_inc(r_vd, 1)
                if b_is_not_first(b):
                    dve.wait_ge(r_sc, b * (16 * 2 * TPB))
                dve.wait_ge(r_rd, b + 1)
                for t in range(TPB):
                    last = ts(xr[:, t, 0:D], o3[:, t, :], mvB[:, t, 0:1], rootD[:, t:t + 1], SUB, MUL)
                last.then_inc(r_xt, 1)
                fin_s.end()

            def residual(b):
                fin_s.wait() if b_is_not_first(b) else None
                dve.wait_ge(c_yn, b + 1)
                cp(y_res[:, :, :], y_new[:, :, :]).then_inc(c_yres, 1)

            def over_experts(v):
                return v.unsqueeze(2).to_broadcast([P, TPB, EXP])

            def over_tiles(v):
                return v.unsqueeze(1).to_broadcast([P, TPB, EXP])

            def top2(b):
                rt.start(b)
                dve.wait_ge(r_g, b + 1)
                g = b_w[0][:, 0:TPB * EXP].rearrange("p (t e) -> p t e", e=EXP)
                for logits, v, i, oh in ((g, v0, i0, oh0), (g2[:, :, :], v1, i1, oh1)):
                    rt.link(nc.vector.tensor_reduce(v[:, :], logits, axis=AX.X, op=MAX))
                    rt.link(tt(eq[:, :, :], logits, over_experts(v[:, :]), ALU.is_equal))
                    rt.link(stt(key[:, :, :], eq[:, :, :], -8.0, over_tiles(expert_no[:, :]), MUL, ADD))
                    rt.link(nc.vector.tensor_reduce(i[:, :], key[:, :, :], axis=AX.X, op=MIN))
                    rt.link(tt(oh[:, :, :], over_tiles(expert_no8[:, :]), over_experts(i[:, :]), ALU.is_equal))
                    if oh is oh0:
                        rt.link(stt(g2[:, :, :], oh0[:, :, :], -3.0e38, g, MUL, ADD))
                tt(gap[:, :], v1[:, :], v0[:, :], SUB).then_inc(r_dv, 1)
                tt(chosen[:, :, :], oh0[:, :, :], oh1[:, :, :], ADD).then_inc(r_m, 1)

            def positions(b):
                dve.wait_ge(r_ex, b + 1)
                rt.link(ts(gate0[:, :], e_gap[:, :], 1.0, None, ADD))
                rt.link(nc.vector.reciprocal(gate0[:, :], gate0[:, :]))
                rt.link(tt(gate1[:, :], e_gap[:, :], gate0[:, :], MUL))
                dve.wait_ge(r_rank, b + 1)
                ranks = b_w[1][:, 0:TPB * EXP].rearrange("p (t e) -> p t e", e=EXP)
                rt.link(tt(pr[:, :, :], ranks, over_tiles(taken[:, :]), ADD))
                tt(taken[:, :], b_w[1][:, TPB * EXP:(TPB + 1) * EXP], taken[:, :], ADD).then_inc(r_run, 1)
                rt.mark(tt(eq[:, :, :], oh0[:, :, :], pr[:, :, :], MUL))
                rt.link(tt(key[:, :, :], oh1[:, :, :], pr[:, :, :], MUL))
                rt.mark(nc.vector.tensor_reduce(pos_f[:, 0:TPB], eq[:, :, :], axis=AX.X, op=ADD))
                rt.link(nc.vector.tensor_reduce(pos_f[:, TPB:], key[:, :, :], axis=AX.X, op=ADD))
                cp(xr[:, :, D:D + 1], twice_token[:, :].unsqueeze(2))
                cp(xr[:, :, D + 1:D + 2], gate0[:, :].unsqueeze(2))
                cp(xr[:, :, D + 2:D + 3], gate1[:, :].unsqueeze(2))
                ts(xr[:, :, D + 3:D + 4], i0[:, :].unsqueeze(2), float(EXP), None, ADD)
                rt.link(ts(twice_token[:, :], twice_token[:, :], float(2 * BLK), None, ADD))
                cp(pos_i[:, :], pos_f[:, :]).then_inc(r_pos, 1)
                rt.end()

            k = [0]

            def link(ins):
                k[0] += 1
                ins.then_inc(c_prep, 1)
                dve.wait_ge(c_prep, k[0])

            nc.vector.memset(ones_bf[:, :], 1.0)
            dve.wait_ge(r_iota, 2)
            cp(expert_no[:, :], eno_i[:, :])
            cp(twice_token[:, :], ids_i[:, :])
            ts(expert_no8[:, :], eno_i[:, :], -float(EXP), None, ADD)
            ts(taken[:, :], eno_i[:, :], float(REGION), None, MUL)
            nc.vector.memset(st_a[:, :, 0:1], 0.0)
            nc.vector.memset(st_b[:, :, 0:1], 0.0)
            nc.vector.memset(h2T[:, :, 0:1], 0.0)
            for j, n in enumerate(("mix_k", "mix_v", "mix_r")):
                last = ts(one_minus[:, j * DC:(j + 1) * DC], vecs[:, VEC[n]:VEC[n] + DC], -1.0, 1.0, MUL, ADD)
            link(last)
            dve.wait_ge(c_act_const, 1)
            link(ts(ew[:, :], ew[:, :], -1.0, -20.0, MUL, MAX))
            ts(ew[:, :], ew[:, :], 20.0, None, MIN).then_inc(c_const, 1)
            dve.wait_ge(c_act_const, 2)
            pre(0)
            normed(0)

            def split_weight(w, src):
                link(cp(w[0][:, :, :], src.rearrange("p (c n) -> p c n", c=w[0].shape[1])))
                return tt(w[1][:, :, :], src.rearrange("p (c n) -> p c n", c=w[0].shape[1]), w[0][:, :, :].bitcast(fp32), SUB)

            for j, n in enumerate(("k", "v", "r")):
                dve.wait_ge(c_stage[n], 16)
                for c in range(DC):
                    ts(fold[0][:, c * D:(c + 1) * D], stage[n][:, c * D:(c + 1) * D], vec("mix_" + n, c), None, MUL)
                    last = ts(fold[1][:, c * D:(c + 1) * D], stage[n][:, c * D:(c + 1) * D], one_minus[:, j * DC + c:j * DC + c + 1], None, MUL)
                link(last)
                link(split_weight(kvr[n][0], fold[0][:, :]))
                split_weight(kvr[n][1], fold[1][:, :]).then_inc(c_w, 1)
                dve.wait_ge(c_w, j + 1)
            h_carry(0)
            h_low(0)
            for n, w in (("out", w_out), ("k2", w_k2), ("r2", w_r2), ("v2", w_v2)):
                dve.wait_ge(c_stage[n], 16)
                split_weight(w, stage[n][:, :]).then_inc(c_w, 1)
            dve.wait_ge(c_w, 7)
            scan(0, 0)
            wkv_low(0, 0)
            scan(0, 1)
            wkv_low(0, 1)
            scan_s.end()
            h_carry(1)
            pre(1)

            def step(i, first=False, more=True):
                h_low(i + 1)
                if not first:
                    gated(i - 1)
                residual(i)
                out_add(i)
                x1_norm(i)
                normed(i + 1)
                mixes(i)
                if not first:
                    final(i - 1)
                if more:
                    pre(i + 2)
                if not first:
                    top2(i - 1)
                scan(i + 1, 0)
                wkv_low(i + 1, 0)
                if not first:
                    positions(i - 1)
                if more:
                    h_carry(i + 2)
                scan(i + 1, 1)
                wkv_low(i + 1, 1)
                scan_s.end()

            step(0, first=True)
            with dve.Fori(1, NBLK - 2) as i:
                step(i)
            step(NBLK - 2, more=False)
            b = NBLK - 1
            gated(b - 1)
            residual(b)
            out_add(b)
            x1_norm(b)
            mixes(b)
            final(b - 1)
            top2(b - 1)
            positions(b - 1)
            gated(b)
            final(b)
            top2(b)
            positions(b)

        block_ctx.close()
        end_phase()

        cursor[0] = shared_from
        m1_hi, m2_hi = sb("m1_hi", [P, EXP, DC, FF], fp32r), sb("m2_hi", [P, EXP, DC, FF], fp32r)
        m3_hi = sb("m3_hi", [P, EXP, FC, D], fp32r)
        m1_lo, m2_lo = sb("m1_lo", [P, EXP, DC, FF], bf16), sb("m2_lo", [P, EXP, DC, FF], bf16)
        m3_lo = sb("m3_lo", [P, EXP, FC, D], bf16)
        WIDE = 2 * FF + D
        biases = sb("biases", [P, WIDE], bf16)
        rowc = sb("rowc", [P, 1 + PARTS])
        row_expert = sb("row_expert", [P, P])
        fill = sb("fill", [P, ROW])
        fill_i = sb("fill_i", [P, 1], i32)
        tile_no, tile_no_i = sb("tile_no", [P, N_TILES]), sb("tile_no_i", [P, N_TILES], i32)
        tiles_of, ends = sb("tiles_of", [P, EXP]), sb("ends", [P, EXP])
        past = sb("past", [P, N_TILES, EXP])
        expert_of, start_of, row_of = (sb(n, [P, N_TILES]) for n in ("expert_of", "start_of", "row_of"))
        expert_reg, row_reg = sb("expert_reg", [1, N_TILES], i32), sb("row_reg", [1, N_TILES], i32)
        free_reg = sb("free_reg", [1, EXP], i32)
        U = 4
        rows4 = [sb(f"rows{n}", [P, ROW]) for n in range(U)]
        xT = [[sb(f"xT_{s}{n}", [P, DC, P], d) for s, d in (("hi", fp32r), ("lo", fp32r), ("bf", bf16))] for n in range(2)]
        sel = [sb(f"sel{n}", [P, P], bf16) for n in range(U)]
        silu = sb("silu", [P, FF])
        hid = sb("hid", [P, FF])
        hT4 = [[sb(f"hTe_{s}{n}", [P, FC, P], d) for s, d in (("hi", fp32r), ("lo", fp32r), ("bf", bf16))] for n in range(2)]
        mine = sb("mine", [P, U])
        weight4, dw = sb("weight4", [P, U]), sb("dw", [P, U])
        padding, tile_row = sb("padding", [P, U]), sb("tile_row", [P, N_TILES])
        dest_f, dest_i = sb("dest_f", [P, U]), sb("dest_i", [P, U], i32)
        y4 = [sb(f"y{n}", [P, D]) for n in range(U)]
        m_stage = [sb(f"m_stage{n}", [P, DC * FF]) for n in range(3)]
        bias_f, bias_p = sb("bias_f", [P, WIDE]), sb("bias_p", [P, WIDE], bf16)
        count, ones8 = sb("count", [P, EXP]), sb("ones8", [P, EXP])
        valid = sb("valid", [P, N_TILES])

        b_gv = [bank[0:2], bank[2:4]]
        b_x, b_h = bank[4], bank[5]
        b_y = bank[6:8]

        e_bias, e_rowc, e_mst = sem("e_bias_loaded"), sem("e_rowc_loaded"), [sem(f"e_staged{n}") for n in range(3)]
        e_hi, e_lo, e_prep = sem("e_weights_high"), sem("e_weights_low"), sem("e_prep_steps")
        e_iota, e_fill, e_tab, e_filled = sem("e_iotas"), sem("e_fill_ready"), sem("e_tables"), sem("e_filled")
        e_ld, e_t, e_xhi, e_xs, e_sel = [sem(f"e_rows_loaded{n}") for n in range(U)], sem("e_transposed"), sem("e_x_high"), sem("e_x_split"), sem("e_selected")
        e_g, e_v, e_silu, e_hid, e_th = sem("e_gate"), sem("e_value"), sem("e_silu"), sem("e_hidden"), sem("e_hidden_transposed")
        e_hhi, e_hs, e_y, e_meta, e_ye = sem("e_hidden_high"), sem("e_hidden_split"), sem("e_out_product"), sem("e_meta"), sem("e_out_weighted")
        e_sc = [sem(f"e_out_scattered{n}") for n in range(U)]
        f_ld, f_sum, f_steps, f_v, f_r, f_done = [sem(f"f_loaded{n}") for n in range(2)], sem("f_summed"), sem("f_steps"), sem("f_variances"), sem("f_roots"), sem("f_done")
        f_st = [sem(f"f_stored{n}") for n in range(2)]
        e_pool_on = sem("e_pool_goes_on")
        e_on, e_meta_s = sem("e_vector_goes_on"), sem("e_meta_steps")

        fx = [sb(f"fx{n}", [P, TPB, D], at=shared_from + n * 4 * TPB * D) for n in range(2)]
        fy = [sb(f"fy{n}", [P, TPB, 2 * D], at=shared_from + 8 * TPB * D + n * 8 * TPB * D) for n in range(2)]
        fbn, fmv = sb("fbn", [P, TPB, 6], at=shared_from + 24 * TPB * D), sb("fmv", [P, TPB, 2], at=shared_from + 24 * TPB * D + 128)
        fv, fr = sb("fv", [P, TPB], at=shared_from + 24 * TPB * D + 192), sb("fr", [P, TPB], at=shared_from + 24 * TPB * D + 256)

        block_ctx = ExitStack()
        block = block_ctx.enter_context(nc.Block())

        expert_weights = [(src[:, e * DC * FF:(e + 1) * DC * FF], hi[:, e, :, :].rearrange("p c n -> p (c n)"), lo[:, e, :, :].rearrange("p c n -> p (c n)"))
                          for e in range(EXP) for src, hi, lo in ((m1_in, m1_hi, m1_lo), (m2_in, m2_hi, m2_lo), (m3_in, m3_hi, m3_lo))]
        N_EW = len(expert_weights)

        @block.sync
        def _(sp):
            sp.dma_start(rowc[:, :], rowc_in).then_inc(e_rowc, 16)
            for n, (src, _, _) in enumerate(expert_weights[:3]):
                sp.dma_start(m_stage[n][:, :], src).then_inc(e_mst[n], 16)
            sp.wait_ge(e_prep, 1)
            for n in range(PARTS):
                sp.dma_start(bias_f[n * EXP:(n + 1) * EXP, :], bias_in).then_inc(e_bias, 16)
            for n in range(3, N_EW):
                sp.wait_ge(e_lo, n - 2)
                sp.dma_start(m_stage[n % 3][:, :], expert_weights[n][0]).then_inc(e_mst[n % 3], 16)
            sp.wait_ge(e_fill, 1)
            sp.dma_start(routed[EXP * REGION:, :], fill[:, :]).then_inc(e_filled, 16)
            sp.wait_ge(e_tab, 3)
            for e in range(EXP):
                free = sp.value_load(free_reg[0:1, e:e + 1], min_val=e * REGION, max_val=e * REGION + N_TOK)
                sp.dma_start(routed[bass.ds(free, P), :], fill[:, :]).then_inc(e_filled, 16)
            sp.wait_ge(e_filled, 16 * (EXP + 1))

            def load(j, u, first=False):
                if not first:
                    sp.wait_ge(e_t, j - U + 1)
                    sp.wait_ge(e_meta, j - U + 1)
                row = sp.value_load(row_reg[0:1, bass.ds(j, 1)], min_val=0, max_val=EXP * REGION)
                sp.dma_start(rows4[u][:, :], routed[bass.ds(row, P), :]).then_inc(e_ld[u], 16)

            for j in range(U):
                load(j, j, True)
            with sp.Fori(1, N_TILES // U) as i:
                for u in range(U):
                    load(i * U + u, u)
            def blocks(i, first=False):
                for n in range(2):
                    b = i * 2 + n
                    if not first:
                        sp.wait_ge(f_done, b - 1)
                        sp.dma_start(out_blocks[:, bass.ds((b - 2) * TPB, TPB), :], fx[n][:, :, :]).then_inc(f_st[n], 16)
                        sp.wait_ge(f_st[n], i * 16)
                    sp.dma_start(fx[n][:, :, :], x3_blocks[:, bass.ds(b * TPB, TPB), :]).then_inc(f_ld[n], 16)
                    sp.dma_start(fy[n][:, :, :], pairs[:, bass.ds(b * TPB, TPB), :]).then_inc(f_ld[n], 16)

            pairs = expert_out[0:2 * N_TOK, :].rearrange("(t p k) d -> p t (k d)", p=P, k=2)
            for u in range(U):
                sp.wait_ge(e_sc[u], 16 * (N_TILES // U))
            blocks(0, True)
            with sp.Fori(1, NBLK // 2) as i:
                blocks(i)
            for n in range(2):
                b = NBLK - 2 + n
                sp.wait_ge(f_done, b + 1)
                sp.dma_start(out_blocks[:, b * TPB:(b + 1) * TPB, :], fx[n][:, :, :]).then_inc(f_st[n], 16)
            for n in range(2):
                sp.wait_ge(f_st[n], 16 * (NBLK // 2))

        @block.gpsimd
        def _(pool):
            nc.gpsimd.iota(tile_no_i[:, :], pattern=[[1, N_TILES]], base=0, channel_multiplier=0).then_inc(e_iota, 1)
            nc.gpsimd.iota(fill_i[:, :], pattern=[[0, 1]], base=2 * N_TOK - 1, channel_multiplier=1).then_inc(e_iota, 1)

            def scatter(j, u):
                pool.wait_ge(e_ye, j + 1)
                pool.sem_inc(e_pool_on)
                nc.gpsimd.indirect_dma_start(expert_out, bass.IndirectOffsetOnAxis(ap=dest_i[:, u:u + 1], axis=0),
                                             y4[u][:, :], None).then_inc(e_sc[u], 16)

            with pool.Fori(0, N_TILES // U) as i:
                for u in range(U):
                    scatter(i * U + u, u)
            with pool.Fori(0, NBLK // 2) as i:
                for n in range(2):
                    pool.wait_ge(f_ld[n], i * 32 + 32)
                    nc.gpsimd.tensor_tensor(fy[n][:, :, 0:D], fy[n][:, :, 0:D], fy[n][:, :, D:2 * D], ADD).then_inc(f_sum, 1)

        @block.tensor
        def _(pe):
            mm = nc.tensor.matmul

            def rows_in(j, u, turn):
                pe.wait_ge(e_ld[u % U], turn * 16 + 16)
                if not (isinstance(j, int) and j == 0):
                    pe.wait_ge(e_xs, j)
                for c in range(DC):
                    last = nc.tensor.transpose(b_x[:, c * P:(c + 1) * P], rows4[u % U][:, c * P:(c + 1) * P], ident[:, :])
                last.then_inc(e_t, 1)

            def gate_value(j, u):
                e = pe.value_load(expert_reg[0:1, bass.ds(j, 1)], min_val=0, max_val=EXP - 1)
                pe.wait_ge(e_xs, j + 1)
                pe.wait_ge(e_sel, j + 1)
                if not (isinstance(j, int) and j < 2):
                    pe.wait_ge(e_hid, j - 1)
                hi, lo, bf = xT[u % 2]
                for n, (w_hi, w_lo, done) in enumerate(((m1_hi, m1_lo, e_g), (m2_hi, m2_lo, e_v))):
                    dst = b_gv[u % 2][n]
                    mm(dst[:, :], sel[u % U][:, :], biases[:, n * FF:(n + 1) * FF], start=True, stop=False)
                    for c in range(DC):
                        w = w_hi[:, bass.ds(e, 1), c, :].rearrange("p a n -> p (a n)")
                        mm(dst[:, :], hi[:, c, :], w, start=False, stop=False)
                        mm(dst[:, :], lo[:, c, :], w, start=False, stop=False)
                        last = mm(dst[:, :], bf[:, c, :], w_lo[:, bass.ds(e, 1), c, :].rearrange("p a n -> p (a n)"), start=False, stop=c == DC - 1)
                    last.then_inc(done, 1)

            def hidden_back(j, u):
                pe.wait_ge(e_hid, j + 1)
                if not (isinstance(j, int) and j == 0):
                    pe.wait_ge(e_hs, j)
                for c in range(FC):
                    last = nc.tensor.transpose(b_h[:, c * P:(c + 1) * P], hid[:, c * P:(c + 1) * P], ident[:, :])
                last.then_inc(e_th, 1)

            def out_rows(j, u):
                e = pe.value_load(expert_reg[0:1, bass.ds(j, 1)], min_val=0, max_val=EXP - 1)
                pe.wait_ge(e_hs, j + 1)
                if not (isinstance(j, int) and j < 2):
                    pe.wait_ge(e_ye, j - 1)
                hi, lo, bf = hT4[u % 2]
                dst = b_y[u % 2][:, 0:D]
                mm(dst, sel[u % U][:, :], biases[:, 2 * FF:2 * FF + D], start=True, stop=False)
                for c in range(FC):
                    w = m3_hi[:, bass.ds(e, 1), c, :].rearrange("p a n -> p (a n)")
                    mm(dst, hi[:, c, :], w, start=False, stop=False)
                    mm(dst, lo[:, c, :], w, start=False, stop=False)
                    last = mm(dst, bf[:, c, :], m3_lo[:, bass.ds(e, 1), c, :].rearrange("p a n -> p (a n)"), start=False, stop=c == FC - 1)
                last.then_inc(e_y, 1)

            def step(j, u, turn):
                known = isinstance(j, int)
                if not known or j + 1 < N_TILES:
                    gate_value(j + 1, u + 1)
                if not known or j + 2 < N_TILES:
                    rows_in(j + 2, u + 2, turn + (u + 2) // U)
                if not known or j < N_TILES:
                    hidden_back(j, u)
                if not known or j >= 1:
                    out_rows(j - 1, u - 1 if u else U - 1)

            pe.wait_ge(e_tab, 3)
            pe.wait_ge(e_lo, N_EW)
            rows_in(0, 0, 0)
            rows_in(1, 1, 0)
            gate_value(0, 0)
            for u in range(U):
                step(u, u, 0)
            with pe.Fori(1, N_TILES // U - 1) as i:
                for u in range(U):
                    step(i * U + u, u, i)
            for u in range(U + 1):
                step(N_TILES - U + u, u, N_TILES // U - 1)

        @block.scalar
        def _(act):
            fn = nc.scalar.activation
            for n, (_, hi, _) in enumerate(expert_weights):
                act.wait_ge(e_mst[n % 3], (n // 3) * 16 + 16)
                fn(hi, m_stage[n % 3][:, :], ACT.Copy).then_inc(e_hi, 1)

            def x_high(j, u):
                act.wait_ge(e_t, j + 1)
                fn(xT[u % 2][0][:, :, :], b_x[:, 0:D].rearrange("p (c n) -> p c n", c=DC), ACT.Copy).then_inc(e_xhi, 1)

            def gate(j, u):
                act.wait_ge(e_g, j + 1)
                if not (isinstance(j, int) and j == 0):
                    act.wait_ge(e_hid, j)
                fn(silu[:, :], b_gv[u % 2][0][:, :], ACT.Silu).then_inc(e_silu, 1)

            def h_high(j, u):
                act.wait_ge(e_th, j + 1)
                fn(hT4[u % 2][0][:, :, :], b_h[:, :].rearrange("p (c n) -> p c n", c=FC), ACT.Copy).then_inc(e_hhi, 1)

            def weighted(j, u, turn):
                act.wait_ge(e_y, j + 1)
                act.wait_ge(e_meta, j + 1)
                if not (isinstance(turn, int) and turn == 0):
                    act.wait_ge(e_sc[u % U], turn * 16)
                fn(y4[u % U][:, :], b_y[u % 2][:, 0:D], ACT.Copy, scale=weight4[:, u % U:u % U + 1]).then_inc(e_ye, 1)

            def step(j, u, turn):
                known = isinstance(j, int)
                gate(j, u)
                if not known or j + 2 < N_TILES:
                    x_high(j + 2, u + 2)
                h_high(j, u)
                if not known or j >= 1:
                    weighted(j - 1, u - 1 if u else U - 1, turn if u else turn - 1)

            x_high(0, 0)
            x_high(1, 1)
            for u in range(U):
                step(u, u, 0)
            with act.Fori(1, N_TILES // U - 1) as i:
                for u in range(U):
                    step(i * U + u, u, i)
            for u in range(U):
                step(N_TILES - U + u, u, N_TILES // U - 1)
            weighted(N_TILES - 1, U - 1, N_TILES // U - 1)

            def last_pass(i):
                for n in range(2):
                    b = i * 2 + n
                    act.wait_ge(f_v, b + 1)
                    fn(fr[:, :], fv[:, :], ACT.Sqrt).then_inc(f_r, 1)

            with act.Fori(0, NBLK // 2) as i:
                last_pass(i)

        @block.vector
        def _(dve):
            ts, tt, stt, cp = nc.vector.tensor_scalar, nc.vector.tensor_tensor, nc.vector.scalar_tensor_tensor, nc.vector.tensor_copy
            k = [0]

            def link(ins):
                k[0] += 1
                ins.then_inc(e_prep, 1)
                dve.wait_ge(e_prep, k[0])

            link(nc.vector.memset(bias_f[:, :], 0.0))
            dve.wait_ge(e_iota, 2)
            link(nc.vector.memset(fill[:, :], 0.0))
            link(nc.vector.memset(fill[:, D + 3:D + 4], -1.0))
            cp(fill[:, D:D + 1], fill_i[:, :]).then_inc(e_fill, 1)
            cp(free_reg[:, :], taken[0:1, :]).then_inc(e_tab, 1)
            nc.vector.memset(ones8[:, :], 1.0)
            cp(tile_no[:, :], tile_no_i[:, :])
            ts(tile_row[:, :], tile_no_i[:, :], float(P), None, MUL)
            link(stt(count[:, :], expert_no[:, :], -float(REGION), taken[:, :], MUL, ADD))
            link(ts(count[:, :], count[:, :], 1.0 / P, 0.5 - 0.5 / P, MUL, ADD))
            link(ts(count[:, :], count[:, :], 2.0 ** 23, None, ADD))
            link(ts(count[:, :], count[:, :], -2.0 ** 23, None, ADD))
            link(nc.vector.tensor_tensor_scan(ends[:, :], ones8[:, :], count[:, :], 0.0, MUL, ADD))
            by_tile = lambda v: v.unsqueeze(2).to_broadcast([P, N_TILES, EXP])
            by_expert = lambda v: v.unsqueeze(1).to_broadcast([P, N_TILES, EXP])
            link(tt(past[:, :, :], by_tile(tile_no[:, :]), by_expert(ends[:, :]), ALU.is_ge))
            link(nc.vector.tensor_reduce(expert_of[:, :], past[:, :, :], axis=AX.X, op=ADD))
            link(tt(past[:, :, :], past[:, :, :], by_expert(ends[:, :]), MUL))
            link(nc.vector.tensor_reduce(start_of[:, :], past[:, :, :], axis=AX.X, op=MAX))
            link(ts(valid[:, :], expert_of[:, :], EXP - 0.5, None, ALU.is_lt))
            link(tt(row_of[:, :], tile_no[:, :], start_of[:, :], SUB))
            link(stt(row_of[:, :], row_of[:, :], float(P), valid[:, :], MUL, MUL))
            link(stt(row_of[:, :], expert_of[:, :], float(REGION), row_of[:, :], MUL, ADD))
            link(ts(expert_of[:, :], expert_of[:, :], float(EXP - 1), None, MIN))
            cp(row_reg[:, :], row_of[0:1, :]).then_inc(e_tab, 1)
            cp(expert_reg[:, :], expert_of[0:1, :]).then_inc(e_tab, 1)
            dve.wait_ge(e_rowc, 16)
            dve.wait_ge(e_bias, 16 * PARTS)
            link(cp(row_expert[:, :], rowc[:, 0:1].broadcast_to([P, P])))
            for n in range(PARTS):
                link(cp(bias_p[:, :], bias_f[:, :]))
                if n == 0:
                    link(ts(biases[:, :], bias_p[:, :], rowc[:, 1:2], None, MUL))
                else:
                    link(stt(biases[:, :], bias_p[:, :], rowc[:, 1 + n:2 + n], biases[:, :], MUL, ADD))
                link(tt(bias_f[:, :], bias_f[:, :], bias_p[:, :], SUB))
            for n, (_, hi, lo) in enumerate(expert_weights):
                dve.wait_ge(e_hi, n + 1)
                tt(lo, m_stage[n % 3][:, :], hi.bitcast(fp32), SUB).then_inc(e_lo, 1)

            meta_s, fin_s = Steps(dve, e_meta_s, 3), Steps(dve, f_steps, 4)

            def x_split(j, u):
                dve.wait_ge(e_xhi, j + 1)
                hi, lo, bf = xT[u % 2]
                src = b_x[:, 0:D].rearrange("p (c n) -> p c n", c=DC)
                cp(bf[:, :, :], src)
                tt(lo[:, :, :], src, hi[:, :, :].bitcast(fp32), SUB).then_inc(e_xs, 1)
                ts(sel[u % U][:, :], row_expert[:, :], expert_of[:, bass.ds(j, 1)], None, ALU.is_equal).then_inc(e_sel, 1)

            def hidden(j, u):
                dve.wait_ge(e_v, j + 1)
                dve.wait_ge(e_silu, j + 1)
                tt(hid[:, :], silu[:, :], b_gv[u % 2][1][:, :], MUL).then_inc(e_hid, 1)

            def meta(j, u, turn):
                meta_s.start(j)
                dve.wait_ge(e_ld[u], turn * 16 + 16)
                if not (isinstance(turn, int) and turn == 0):
                    dve.wait_ge(e_sc[u], turn * 16)
                row, c = rows4[u], slice(u, u + 1)
                meta_s.mark(ts(mine[:, c], row[:, D + 3:D + 4], expert_of[:, bass.ds(j, 1)], None, ALU.is_equal))
                meta_s.link(tt(dw[:, c], row[:, D + 1:D + 2], row[:, D + 2:D + 3], SUB))
                ts(padding[:, c], row[:, D + 3:D + 4], 0.0, tile_row[:, bass.ds(j, 1)], ALU.is_lt, MUL)
                stt(weight4[:, c], dw[:, c], mine[:, c], row[:, D + 2:D + 3], MUL, ADD)
                meta_s.link(stt(dest_f[:, c], row[:, D:D + 1], 1.0, mine[:, c], ADD, SUB))
                tt(dest_i[:, c], dest_f[:, c], padding[:, c], ADD).then_inc(e_meta, 1)
                meta_s.end()

            def h_split(j, u):
                dve.wait_ge(e_hhi, j + 1)
                hi, lo, bf = hT4[u % 2]
                src = b_h[:, :].rearrange("p (c n) -> p c n", c=FC)
                cp(bf[:, :, :], src)
                tt(lo[:, :, :], src, hi[:, :, :].bitcast(fp32), SUB).then_inc(e_hs, 1)

            def step(j, u, turn):
                hidden(j, u)
                meta(j, u, turn)
                if not isinstance(j, int) or j + 2 < N_TILES:
                    x_split(j + 2, u + 2)
                h_split(j, u)

            x_split(0, 0)
            x_split(1, 1)
            for u in range(U):
                step(u, u, 0)
            with dve.Fori(1, N_TILES // U - 1) as i:
                for u in range(U):
                    step(i * U + u, u, i)
            for u in range(U):
                step(N_TILES - U + u, u, N_TILES // U - 1)

            def last_pass(i):
                for n in range(2):
                    b = i * 2 + n
                    y = fy[n][:, :, 0:D]
                    fin_s.start(b)
                    dve.wait_ge(f_sum, b + 1)
                    for t in range(TPB):
                        last = nc.vector.bn_stats(fbn[:, t, :], fy[n][:, t, 0:D])
                    fin_s.link(last)
                    dve.sem_inc(e_on)
                    for t in range(TPB):
                        last = nc.vector.bn_aggr(fmv[:, t, :], fbn[:, t, :])
                    fin_s.link(last)
                    fin_s.link(ts(fv[:, :], fmv[:, :, 1], LN_EPS, None, ADD))
                    nc.vector.reciprocal(fv[:, :], fv[:, :]).then_inc(f_v, 1)
                    dve.wait_ge(f_r, b + 1)
                    for t in range(TPB):
                        last = ts(fy[n][:, t, 0:D], fy[n][:, t, 0:D], fmv[:, t, 0:1], fr[:, t:t + 1], SUB, MUL)
                    fin_s.link(last)
                    tt(fx[n][:, :, :], fx[n][:, :, :], y, ADD).then_inc(f_done, 1)
                    fin_s.end()

            with dve.Fori(0, NBLK // 2) as i:
                last_pass(i)

        block_ctx.close()
        end_phase()


_WEIGHTS = {"wg": ("L0_attn_Wg", True), "wc": ("L0_attn_Wc", True), "w1": ("L0_ffn_w1_w", True), "w2": ("L0_ffn_w2_w", True),
            "h1": ("L0_ffn_h1_w", True), "h2": ("L0_ffn_h2_w", True), "w3": ("L0_ffn_w3_w", True), "wk": ("L1_attn_W_key", False), "wv": ("L1_attn_W_value", False),
            "wr": ("L1_attn_W_recept", False), "wo": ("L1_attn_W_out", False), "wk2": ("L1_attn_W_key2", False),
            "wv2": ("L1_attn_W_value2", False), "wr2": ("L1_attn_W_recept2", False), "wg8": ("L1_ffn_Wg", True)}
_VECTORS = {"gamma": "L0_attn_gamma", "beta": "L0_attn_beta", "bg": "L0_attn_bg", "bc": "L0_attn_bc", "w1_s": "L0_ffn_w1_s",
            "w2_s": "L0_ffn_w2_s", "h1_s": "L0_ffn_h1_s", "h2_s": "L0_ffn_h2_s", "ln1_w": "L1_attn_ln1_w",
            "ln2_w": "L1_attn_ln2_w", "decay": "L1_attn_time_decay", "first": "L1_attn_time_first",
            "mix_k": "L1_attn_time_mix_k", "mix_v": "L1_attn_time_mix_v", "mix_r": "L1_attn_time_mix_r",
            "mix_k2": "L1_attn_time_mix_k2", "mix_r2": "L1_attn_time_mix_r2"}


def layouts(inputs):
    import numpy as np

    def rows(name, transpose):
        w = np.asarray(inputs[name])
        w = w.T if transpose else w
        return np.ascontiguousarray(w.reshape(-1, P, w.shape[1]).transpose(1, 0, 2)).reshape(P, -1)

    arrays = {"x": np.ascontiguousarray(np.asarray(inputs["L0_attn_x"]).reshape(N_TOK, D))}
    arrays["vecs"] = np.ascontiguousarray(np.concatenate(
        [np.asarray(inputs[_VECTORS[n]]).reshape(-1, P).T for n in VEC], axis=1))
    arrays["w3s"] = np.ascontiguousarray(np.broadcast_to(np.asarray(inputs["L0_ffn_w3_s"]), (P, D)))
    for k, (name, transpose) in _WEIGHTS.items():
        arrays[k] = rows(name, transpose)

    def experts(name):
        w = np.asarray(inputs[name])
        e, o, i = w.shape
        return np.ascontiguousarray(w.transpose(2, 0, 1).reshape(i // P, P, e, o).transpose(1, 2, 0, 3)).reshape(P, -1)

    for n in (1, 2, 3):
        arrays[f"m{n}"] = experts(f"L1_ffn_W{n}")
    arrays["bias"] = np.ascontiguousarray(np.concatenate([np.asarray(inputs[f"L1_ffn_b{n}"]) for n in (1, 2, 3)], axis=1))
    rowc = np.full((P, 1 + PARTS), 0.0, np.float32)
    rowc[:, 0] = [n % EXP if n < PARTS * EXP else -2 for n in range(P)]
    for n in range(PARTS):
        rowc[n * EXP:(n + 1) * EXP, 1 + n] = 1.0
    arrays["rowc"] = rowc
    return arrays


def kernel(**inputs):
    import numpy as _np
    import concourse.bacc as _bacc
    from concourse import mybir as _mybir
    from concourse.bass_utils import run_bass_kernel_spmd as _run

    nc = _bacc.Bacc("TRN2", target_bir_lowering=False, num_devices=1)
    arrays, args = {}, []
    for name, a in layouts(inputs).items():
        arrays[f"in_{name}_dram"] = a
        args.append(nc.dram_tensor(f"in_{name}_dram", a.shape, _mybir.dt.from_np(a.dtype), kind="ExternalInput").ap())
    args.append(nc.dram_tensor("out_dram", (N_TOK, D), _mybir.dt.float32, kind="ExternalOutput").ap())
    build(nc, *args)
    r = _run(nc, [arrays], core_ids=[0])
    return r.results[0]["out_dram"].reshape(4, SEQ, D)
```

```python
import concourse.bass as bass
from concourse import mybir
from contextlib import ExitStack
import numpy as np

fp32 = mybir.dt.float32
fp32r = mybir.dt.float32r
u32 = mybir.dt.uint32
i32 = mybir.dt.int32
bf16 = mybir.dt.bfloat16
ALU = mybir.AluOpType
ACT = mybir.ActivationFunctionType
AX = mybir.AxisListType
ADD, SUB, MUL, MAX, MIN = ALU.add, ALU.subtract, ALU.mult, ALU.max, ALU.min

P = 128
N_TOK = 4096
SEQ = 1024
D = 256
DC = D // P
HID = 1024
HC = HID // P
PIECE = 512
BLK = 512
TPB = BLK // P
NBLK = N_TOK // BLK
EXP = 8
FF = 512
FC = FF // P
REGION = N_TOK + P
N_TILES = 2 * N_TOK // P + EXP
ROW = D + 4
FFN_PIECES = 7
PARTS = 3
LN_EPS = 1e-5
RMS_EPS = 1e-6
CLIP = (float(np.exp(np.float32(-20.0))), float(np.exp(np.float32(20.0))))

VEC = {}
_at = 0
for _name, _n in [("gamma", DC), ("beta", DC), ("bg", DC), ("bc", DC), ("w1_s", HC), ("w2_s", HC),
                  ("h1_s", HC), ("h2_s", HC), ("ln1_w", DC), ("ln2_w", DC), ("decay", DC), ("first", DC),
                  ("mix_k", DC), ("mix_v", DC), ("mix_r", DC), ("mix_k2", DC), ("mix_r2", DC)]:
    VEC[_name] = _at
    _at += _n
N_VEC = _at


class Steps:
    def __init__(self, eng, s, per):
        self.eng, self.s, self.per = eng, s, per

    def start(self, b):
        self.base, self.k = b * self.per, 0

    def mark(self, ins):
        self.k += 1
        ins.then_inc(self.s, 1)

    def link(self, ins):
        self.mark(ins)
        self.wait()

    def wait(self):
        self.eng.wait_ge(self.s, self.base + self.k)

    def end(self):
        assert self.k == self.per, self.k


def build(nc, x_in, vecs_in, w3s_in, wg_in, wc_in, w1_in, w2_in, h1_in, h2_in, w3_in,
          wk_in, wv_in, wr_in, wo_in, wk2_in, wv2_in, wr2_in,
          wg8_in, m1_in, m2_in, m3_in, bias_in, rowc_in, out):
    with ExitStack() as ctx:
        cursor = [nc.sbuf_base + (-nc.sbuf_base) % 64]

        def sb(name, shape, dt=fp32, at=None):
            size = 2 if dt == bf16 else 4
            for n in shape[1:]:
                size *= n
            where = cursor[0] if at is None else at
            place[name] = where
            if at is None:
                cursor[0] += size + (-size) % 64
            return nc.alloc_sbuf_tensor_at(name, shape, dt, offset=where)

        place = {}
        phase_sems = []

        def sem(name):
            phase_sems.append(nc.alloc_semaphore(name))
            return phase_sems[-1]

        def end_phase():
            nc.clear_and_free_semaphores(list(phase_sems))
            phase_sems.clear()
            nc.all_engine_barrier()

        xs_mid = nc.dram_tensor("x_after_ffn", [N_TOK, D], fp32, kind="Internal").ap()
        x_blocks = x_in.rearrange("(t p) d -> p t d", p=P)
        mid_blocks = xs_mid.rearrange("(t p) d -> p t d", p=P)
        out_blocks = out.rearrange("(t p) d -> p t d", p=P)
        x3_dram = nc.dram_tensor("x_after_mixing", [N_TOK, D], fp32, kind="Internal").ap()
        x3_blocks = x3_dram.rearrange("(t p) d -> p t d", p=P)
        routed = nc.dram_tensor("routed_rows", [EXP * REGION + P, ROW], fp32, kind="Internal").ap()
        expert_out = nc.dram_tensor("expert_rows", [2 * N_TOK + N_TILES * P, D], fp32, kind="Internal").ap()

        expert_parts = [[nc.dram_tensor(f"expert_w{n}_{s}", [P, EXP * DC * FF], d, kind="Internal").ap()
                         for s, d in (("hi", fp32), ("lo", bf16))] for n in (1, 2, 3)]
        expert_pieces = [(m_in, hi, lo, half * PIECE) for m_in, (hi, lo) in zip((m1_in, m2_in, m3_in), expert_parts)
                         for half in range(DC * FF // PIECE)]

        ident = sb("ident", [P, P])
        vecs = sb("vecs", [P, N_VEC])
        neg_bg = sb("neg_bg", [P, DC])
        carry_on = sb("carry_on", [P, NBLK + 2])
        w3s_row = sb("w3s_row", [P, D])

        def vec(name, c):
            return vecs[:, VEC[name] + c:VEC[name] + c + 1]

        wg8 = sb("wg8", [P, DC, EXP])
        upper, ones_bf = sb("upper", [P, P], bf16), sb("ones_bf", [P, P], bf16)
        expert_no = sb("expert_no", [P, EXP])
        expert_no8 = sb("expert_no8", [P, EXP])
        taken = sb("taken", [P, EXP])
        twice_token = sb("twice_token", [P, TPB])
        ids_i = sb("ids_i", [P, TPB], i32)
        eno_i = sb("eno_i", [P, EXP], i32)
        shared_from = cursor[0]
        w_gate_hi, w_gate_lo = (sb(f"w_gate_{s}", [P, DC, D], fp32r) for s in ("hi", "lo"))
        w_cand_hi, w_cand_lo = (sb(f"w_cand_{s}", [P, DC, D], fp32r) for s in ("hi", "lo"))
        w1 = sb("w1", [P, DC, HID], fp32r)
        w2 = sb("w2", [P, DC, HID], fp32r)
        h1w = sb("h1w", [P, HC, HID], fp32r)
        h2w = sb("h2w", [P, HC, HID], fp32r)
        w3 = sb("w3", [P, HC, D], fp32r)

        ha_hi, ha_lo = (sb(f"ha_{s}", [P, HC, BLK], fp32r) for s in ("hi", "lo"))
        hb_hi, hb_lo = (sb(f"hb_{s}", [P, HC, BLK], fp32r) for s in ("hi", "lo"))
        yt_hi, yt_lo = (sb(f"yt_{s}", [P, DC, BLK], fp32r) for s in ("hi", "lo"))
        xa = [sb(f"xa{n}", [P, TPB, D]) for n in range(2)]
        yn = sb("yn", [P, TPB, D])
        o1 = sb("o1", [P, TPB, D])
        hs = o1[:, :, :].rearrange("p t d -> p (t d)").rearrange("p (c n) -> p c n", c=DC)
        o2 = sb("o2", [P, TPB, D])
        act2 = sb("act2", [P, 2, BLK])
        f2 = sb("f2", [P, 2, BLK])
        zc = sb("zc", [P, BLK])
        carry = sb("carry", [P, DC])
        piece = sb("piece", [P, PIECE])
        piece_hi, piece_lo = sb("piece_hi", [P, PIECE], fp32r), sb("piece_lo", [P, PIECE], bf16)
        st1, mv1 = sb("st1", [P, TPB, 6]), sb("mv1", [P, TPB, 2])
        st2, mv2 = sb("st2", [P, TPB, 6]), sb("mv2", [P, TPB, 2])
        v1a, r1a = sb("v1a", [P, 2, TPB]), sb("r1a", [P, 2, TPB])
        inv_r2 = sb("inv_r2", [P, TPB])
        r12 = sb("r12", [P, TPB])
        v2a, r2a = sb("v2a", [P, TPB]), sb("r2a", [P, TPB])
        chk = sb("chk", [P, FFN_PIECES])
        chk1, chk_all = sb("chk1", [P, 1]), sb("chk_all", [P, 1])
        split_flag = sb("split_flag", [1, 1], u32)

        bank = [ctx.enter_context(nc.psum_tensor(f"bank{n}", [P, BLK], fp32)) for n in range(8)]
        ff = bank[0:4]
        pyo = bank[4:6]
        pt = bank[6:8]

        s_const = sem("const_loaded")
        s_ident0, s_ident = sem("ident_zeroed"), sem("ident_ready")
        s_masks = sem("masks_ready")
        s_wst = sem("small_weights_staged")
        s_stage = [sem(f"staged{n}") for n in range(7)]
        s_round = sem("weights_rounded")
        s_chk = sem("weights_checked")
        s_raw = sem("weights_in_place")
        s_flag0, s_flag1, s_flag = sem("flag_summed"), sem("flag_reduced"), sem("flag_ready")
        s_wsplit = sem("small_weights_split")
        s_wlo = sem("small_weights_low")
        s_x = [sem(f"x_loaded{n}") for n in range(2)]
        s_dve_on, s_pool_on = sem("vector_goes_on"), sem("pool_goes_on")
        s_p1 = sem("p1_steps")
        s_v1 = sem("p1_variances")
        s_r1 = sem("p1_roots")
        s_yn = sem("p1_normalized")
        s_t1 = sem("p1_transposed")
        s_aff = sem("p1_affine")
        s_nt = sem("p1_split")
        s_z, s_c = sem("gate_product"), sem("candidate_product")
        s_sig = sem("gates_ready")
        s_zc = sem("gated_candidate")
        s_scan = sem("scanned")
        s_ht = sem("scan_transposed")
        s_vo, s_ro = sem("p1_out_variances"), sem("p1_out_roots")
        s_xa = sem("p1_done")
        s_v2, s_r2 = sem("ffn_in_variances"), sem("ffn_in_roots")
        s_y2 = sem("ffn_normalized")
        s_t2 = sem("ffn_transposed")
        s_yhi, s_ylo = sem("ffn_in_high"), sem("ffn_in_low")
        s_l1a, s_l1b = sem("w1_product"), sem("w2_product")
        s_silu = sem("silu_ready")
        s_f1, s_f1hi, s_f1lo = sem("h_product"), sem("h_high"), sem("h_low")
        s_l2, s_l3 = sem("h1_product"), sem("h2_product")
        s_g2, s_g2hi, s_g2lo = sem("gelu1_ready"), sem("gelu1_high"), sem("gelu1_low")
        s_g3, s_g3hi, s_g3lo = sem("gelu2_ready"), sem("gelu2_high"), sem("gelu2_low")
        s_l4 = sem("w3_product")
        s_y4 = sem("ffn_scaled")
        s_p2 = sem("ffn_steps")
        s_p3 = sem("ffn_out_steps")
        s_v4, s_r4 = sem("ffn_out_variances"), sem("ffn_out_roots")
        s_on, s_o2 = sem("ffn_out_normed"), sem("ffn_done")
        s_st = sem("ffn_stored")
        w_ld, w_hi, w_lo, w_st = sem("piece_loaded"), sem("piece_high"), sem("piece_low"), sem("piece_stored")

        block_ctx = ExitStack()
        block = block_ctx.enter_context(nc.Block())

        stage_w1 = sb("stage_w1", [P, DC * HID], at=place["ha_hi"])
        stage_w2 = sb("stage_w2", [P, DC * HID], at=place["ha_hi"] + 4 * DC * HID)
        stage_w3 = sb("stage_w3", [P, HC * D], at=place["ha_lo"])
        HALF = HC * HID // 2
        stage_h1 = [sb(f"stage_h1_{s}", [P, HALF], at=place["hb_" + s]) for s in ("hi", "lo")]
        stage_h2 = [sb(f"stage_h2_{n}", [P, HALF], at=place[s + "_hi"]) for n, s in enumerate(("ha", "hb"))]

        def flat(w):
            return w[:, :, :].rearrange("p c n -> p (c n)")

        ffn_weights = [(w1_in, stage_w1, flat(w1)), (w2_in, stage_w2, flat(w2)), (w3_in, stage_w3, flat(w3)),
                       (h1_in[:, 0:HALF], stage_h1[0], flat(h1w)[:, 0:HALF]), (h1_in[:, HALF:], stage_h1[1], flat(h1w)[:, HALF:]),
                       (h2_in[:, 0:HALF], stage_h2[0], flat(h2w)[:, 0:HALF]), (h2_in[:, HALF:], stage_h2[1], flat(h2w)[:, HALF:])]
        EARLY = 5

        @block.sync
        def _(sp):
            sp.dma_start(xa[0][:, :, :], x_blocks[:, 0:TPB, :]).then_inc(s_x[0], 16)
            sp.dma_start(vecs[:, :], vecs_in).then_inc(s_const, 16)
            sp.dma_start(o2[:, 0:2, :], wg_in).then_inc(s_wst, 16)
            sp.dma_start(o2[:, 2:4, :], wc_in).then_inc(s_wst, 16)
            sp.dma_start(w3s_row[:, :], w3s_in).then_inc(s_const, 16)
            for n, (src, stage, _) in enumerate(ffn_weights[:EARLY]):
                sp.dma_start(stage[:, :], src).then_inc(s_stage[n], 16)
            for n, checked in ((5, 2), (6, 4)):
                sp.wait_ge(s_chk, checked)
                sp.dma_start(ffn_weights[n][1][:, :], ffn_weights[n][0]).then_inc(s_stage[n], 16)
            sp.dma_start(xa[1][:, :, :], x_blocks[:, TPB:2 * TPB, :]).then_inc(s_x[1], 16)
            sp.wait_ge(s_flag, 1)
            with sp.If(sp.value_load(split_flag[0:1, 0:1], min_val=0, max_val=1) != 0):
                for n, (src, stage, dst) in enumerate(ffn_weights):
                    sp.dma_start(stage[:, :], src).then_inc(s_raw, 16)
                    sp.wait_ge(s_raw, 16 * (2 * n + 1))
                    sp.dma_start(dst.bitcast(fp32), stage[:, :]).then_inc(s_raw, 16)
                    sp.wait_ge(s_raw, 16 * (2 * n + 2))

            N_PIECES = len(expert_pieces)

            def split_expert(e):
                for k, (src, hi, lo, col) in enumerate(expert_pieces):
                    if not (isinstance(e, int) and e == 0 and k == 0):
                        sp.wait_ge(w_lo, e * N_PIECES + k)
                    sp.dma_start(piece[:, :], src[:, bass.ds(e * DC * FF + col, PIECE)]).then_inc(w_ld, 16)
                    sp.wait_ge(w_lo, e * N_PIECES + k + 1)
                    sp.dma_start(hi[:, bass.ds(e * DC * FF + col, PIECE)], piece_hi[:, :].bitcast(fp32)).then_inc(w_st, 16)
                    sp.dma_start(lo[:, bass.ds(e * DC * FF + col, PIECE)], piece_lo[:, :]).then_inc(w_st, 16)

            def store(b, n, more=True):
                split_expert(b)
                sp.wait_ge(s_o2, b + 1)
                sp.dma_start(mid_blocks[:, bass.ds(b * TPB, TPB), :], o2[:, :, :]).then_inc(s_st, 16)
                if more:
                    sp.dma_start(xa[n][:, :, :], x_blocks[:, bass.ds((b + 2) * TPB, TPB), :]).then_inc(s_x[n], 16)

            for n in range(2):
                store(n, n)
            with sp.Fori(1, NBLK // 2 - 1) as i:
                for n in range(2):
                    store(i * 2 + n, n)
            for n in range(2):
                store(NBLK - 2 + n, n, False)
            sp.wait_ge(w_st, 32 * EXP * N_PIECES)
            sp.wait_ge(s_st, 16 * NBLK)

        @block.gpsimd
        def _(pool):
            nc.gpsimd.memset(ident[:, :], 0.0).then_inc(s_ident0, 1)
            pool.wait_ge(s_ident0, 1)
            nc.gpsimd.affine_select(out=ident[:, :], in_=ident[:, :], compare_op=ALU.not_equal, fill=1.0, base=0,
                                    pattern=[[-1, P]], channel_multiplier=1).then_inc(s_ident, 1)
            pool.wait_ge(s_wst, 32)
            nc.gpsimd.tensor_copy(w_gate_hi[:, :, :], o2[:, 0:2, :]).then_inc(s_wsplit, 1)
            nc.gpsimd.tensor_copy(w_cand_hi[:, :, :], o2[:, 2:4, :]).then_inc(s_wsplit, 1)
            pool.wait_ge(s_flag0, 1)
            nc.gpsimd.partition_all_reduce(chk_all[:, :], chk1[:, :], P, bass.bass_isa.ReduceOp.max).then_inc(s_flag1, 1)

            def split_expert(e):
                for k in range(len(expert_pieces)):
                    m = e * len(expert_pieces) + k
                    pool.wait_ge(w_ld, m * 16 + 16)
                    if not (isinstance(m, int) and m == 0):
                        pool.wait_ge(w_st, m * 32)
                    pool.sem_inc(s_pool_on)
                    nc.gpsimd.tensor_copy(piece_hi[:, :], piece[:, :]).then_inc(w_hi, 1)
                    pool.wait_ge(w_hi, m + 1)
                    nc.gpsimd.tensor_tensor(piece_lo[:, :], piece[:, :], piece_hi[:, :].bitcast(fp32), SUB).then_inc(w_lo, 1)

            def ffn_out(b, n):
                pool.wait_ge(s_r4, b + 1)
                pool.sem_inc(s_pool_on)
                for t in range(TPB):
                    last = nc.gpsimd.tensor_scalar(o2[:, t, :], o2[:, t, :], mv2[:, t, 0:1], r2a[:, t:t + 1], SUB, MUL)
                last.then_inc(s_on, 1)
                pool.wait_ge(s_on, b + 1)
                pool.wait_ge(s_xa, b + 1)
                nc.gpsimd.tensor_tensor(o2[:, :, :], o2[:, :, :], xa[n][:, :, :], ADD).then_inc(s_o2, 1)

            assert EXP == NBLK
            for n in range(2):
                split_expert(n)
                ffn_out(n, n)
            with pool.Fori(1, NBLK // 2) as i:
                for n in range(2):
                    split_expert(i * 2 + n)
                    ffn_out(i * 2 + n, n)


        @block.tensor
        def _(pe):
            mm = nc.tensor.matmul

            def transpose_in(b, s_in, s_out, n_out):
                pe.wait_ge(s_in, b + 1)
                for c in range(DC):
                    for t in range(TPB):
                        last = nc.tensor.transpose(pt[c][:, t * P:(t + 1) * P], yn[:, t, c * P:(c + 1) * P], ident[:, :])
                    last.then_inc(s_out, 1)

            def p1_transpose(b, first=False):
                if not first:
                    pe.wait_ge(s_ylo, b * DC)
                transpose_in(b, s_yn, s_t1, DC)

            def p1_gates(b, m):
                pe.wait_ge(s_nt, b * DC + 2)
                if m:
                    pe.wait_ge(s_zc, b * DC + m)
                for dst, hi, lo, done in ((pt[0], w_gate_hi, w_gate_lo, s_z), (pt[1], w_cand_hi, w_cand_lo, s_c)):
                    n = 0
                    for c in range(DC):
                        for w, y in ((hi, yt_hi), (lo, yt_hi), (hi, yt_lo)):
                            last = mm(dst[:, :], w[:, c, m * P:(m + 1) * P], y[:, c, :], start=n == 0, stop=n == 3 * DC - 1)
                            n += 1
                    last.then_inc(done, 1)

            def p1_back(b):
                pe.wait_ge(s_scan, b * DC + DC)
                for t in range(TPB):
                    for c in range(DC):
                        last = nc.tensor.transpose(pt[t // 2][:, (t % 2) * D + c * P:(t % 2) * D + (c + 1) * P],
                                                   hs[:, c, t * P:(t + 1) * P], ident[:, :])
                last.then_inc(s_ht, 1)

            def ffn_transpose(b):
                transpose_in(b, s_y2, s_t2, DC)

            def group(dst, w, m, hi, lo, n_k, fast, before=None):
                n = 0
                for k in range(n_k):
                    if before:
                        before(k)
                    for x in (hi, lo):
                        a, y = w[:, k, m * P:(m + 1) * P], x[:, k, :]
                        if not fast:
                            a, y = a.bitcast(fp32), y.bitcast(fp32)
                        last = mm(dst[:, :], a, y, start=n == 0, stop=n == 2 * n_k - 1)
                        n += 1
                return last

            def layer1(b, fast):
                pe.wait_ge(s_ylo, b * DC + DC)
                for m in range(HC):
                    if m >= 2:
                        pe.wait_ge(s_f1, b * HC + m - 1)
                    group(ff[2 * (m % 2)], w1, m, yt_hi, yt_lo, DC, fast).then_inc(s_l1a, 1)
                    group(ff[2 * (m % 2) + 1], w2, m, yt_hi, yt_lo, DC, fast).then_inc(s_l1b, 1)

            def layer2(b, ms, fast):
                for m in ms:
                    if m == 0:
                        pe.wait_ge(s_f1, b * HC + HC - 1)
                    if m >= 4:
                        pe.wait_ge(s_g2, b * HC + m - 3)
                    group(ff[m % 4], h1w, m, ha_hi, ha_lo, HC, fast,
                          (lambda k: pe.wait_ge(s_f1lo, b * HC + k + 1)) if m == 0 else None).then_inc(s_l2, 1)

            def layer3(b, ms, fast):
                for m in ms:
                    if m < 4:
                        pe.wait_ge(s_g2, b * HC + m + 5)
                    else:
                        pe.wait_ge(s_g3, b * HC + m - 3)
                    group(ff[m % 4], h2w, m, hb_hi, hb_lo, HC, fast,
                          (lambda k: pe.wait_ge(s_g2lo, b * HC + k + 1)) if m == 0 else None).then_inc(s_l3, 1)

            def layer4(b, fast):
                for t in range(TPB):
                    n = 0
                    for k in range(HC):
                        if t == 0:
                            pe.wait_ge(s_g3lo, b * HC + k + 1)
                        for x in (ha_hi, ha_lo):
                            a, y = x[:, k, t * P:(t + 1) * P], w3[:, k, :]
                            if not fast:
                                a, y = a.bitcast(fp32), y.bitcast(fp32)
                            last = mm(pyo[t // 2][:, (t % 2) * D:(t % 2 + 1) * D], a, y, start=n == 0, stop=n == 2 * HC - 1)
                            n += 1
                    if t % 2:
                        last.then_inc(s_l4, 1)

            pe.wait_ge(s_ident, 1)
            p1_transpose(0, first=True)
            pe.wait_ge(s_wlo, 2)
            p1_gates(0, 0)
            p1_gates(0, 1)
            p1_back(0)
            ffn_transpose(0)
            pe.wait_ge(s_flag, 1)
            needs_split = pe.value_load(split_flag[0:1, 0:1], min_val=0, max_val=1)
            with pe.If(needs_split != 0):
                pe.wait_ge(s_raw, 32 * len(ffn_weights))

            def both(layer, *args):
                with pe.If(needs_split == 0):
                    layer(*args, True)
                with pe.Else():
                    layer(*args, False)

            with pe.Fori(0, NBLK - 1) as i:
                both(layer1, i)
                both(layer2, i, range(0, 4))
                p1_transpose(i + 1)
                both(layer2, i, range(4, 6))
                p1_gates(i + 1, 0)
                both(layer2, i, range(6, 8))
                p1_gates(i + 1, 1)
                both(layer3, i, range(0, 4))
                p1_back(i + 1)
                both(layer3, i, range(4, 8))
                ffn_transpose(i + 1)
                both(layer4, i)
            both(layer1, NBLK - 1)
            both(layer2, NBLK - 1, range(8))
            both(layer3, NBLK - 1, range(8))
            both(layer4, NBLK - 1)

        @block.scalar
        def _(act):
            fn = nc.scalar.activation

            def p1_roots(b):
                act.wait_ge(s_v1, b + 1)
                fn(r1a[:, :, :], v1a[:, :, :], ACT.Sqrt).then_inc(s_r1, 1)

            def p1_affine(b):
                for c in range(DC):
                    act.wait_ge(s_t1, b * DC + c + 1)
                    fn(act2[:, c, :], pt[c][:, :], ACT.Identity, scale=vec("gamma", c), bias=vec("beta", c)).then_inc(s_aff, 1)

            def p1_gates(b, m):
                act.wait_ge(s_z, b * DC + m + 1)
                if m == 0:
                    act.wait_ge(s_nt, b * DC + DC)
                else:
                    act.wait_ge(s_scan, b * DC + m)
                fn(act2[:, 0, :], pt[0][:, :], ACT.Sigmoid, bias=vec("bg", m)).then_inc(s_sig, 1)
                fn(act2[:, 1, :], pt[0][:, :], ACT.Sigmoid, bias=neg_bg[:, m:m + 1], scale=-1.0).then_inc(s_sig, 1)

            def roots(b, s_in, s_out, v, r):
                act.wait_ge(s_in, b + 1)
                fn(r, v, ACT.Sqrt).then_inc(s_out, 1)

            def p1_out(b):
                roots(b, s_vo, s_ro, v1a[:, 0, :], r1a[:, 0, :])
                roots(b, s_v2, s_r2, v1a[:, 1, :], r1a[:, 1, :])

            def ffn_in(b):
                for c in range(DC):
                    act.wait_ge(s_t2, b * DC + c + 1)
                    fn(yt_hi[:, c, :], pt[c][:, :], ACT.Copy).then_inc(s_yhi, 1)

            def layer1(b, first=False):
                def silu(m):
                    act.wait_ge(s_l1a, b * HC + m + 1)
                    if m >= 2:
                        act.wait_ge(s_f1, b * HC + m - 1)
                    fn(act2[:, m % 2, :], ff[2 * (m % 2)][:, :], ACT.Silu, scale=vec("w1_s", m)).then_inc(s_silu, 1)

                silu(0)
                for m in range(HC):
                    if m == 2 and not first:
                        roots(b - 1, s_v4, s_r4, v2a[:, :], r2a[:, :])
                    if m + 1 < HC:
                        silu(m + 1)
                    act.wait_ge(s_f1, b * HC + m + 1)
                    fn(ha_hi[:, m, :], f2[:, m % 2, :], ACT.Copy).then_inc(s_f1hi, 1)

            def hidden(b, ms, s_in, s_low, s_out, scale):
                for m in ms:
                    act.wait_ge(s_in, b * HC + m + 1)
                    if m >= 2:
                        act.wait_ge(s_low, b * HC + m - 1)
                    fn(f2[:, m % 2, :], ff[m % 4][:, :], ACT.Gelu, scale=vec(scale, m)).then_inc(s_out, 1)

            def layer2(b, ms):
                hidden(b, ms, s_l2, s_g2lo, s_g2, "h1_s")

            def layer3(b, ms):
                hidden(b, ms, s_l3, s_g3lo, s_g3, "h2_s")

            act.wait_ge(s_const, 32)
            fn(neg_bg[:, :], vecs[:, VEC["bg"]:VEC["bg"] + DC], ACT.Copy, scale=-1.0).then_inc(s_masks, 1)
            p1_roots(0)
            p1_affine(0)

            def round_weights(ns):
                for n in ns:
                    act.wait_ge(s_stage[n], 16)
                    fn(ffn_weights[n][2], ffn_weights[n][1][:, :], ACT.Copy).then_inc(s_round, 1)

            round_weights(range(0, 3))
            act.wait_ge(s_masks, 3)
            p1_gates(0, 0)
            p1_gates(0, 1)
            round_weights(range(3, 5))
            p1_out(0)
            ffn_in(0)
            round_weights(range(5, 7))

            def step(i, first=False):
                layer1(i, first)
                layer2(i, range(0, 2))
                p1_roots(i + 1)
                layer2(i, range(2, 4))
                p1_affine(i + 1)
                layer2(i, range(4, 6))
                p1_gates(i + 1, 0)
                layer2(i, range(6, 8))
                p1_gates(i + 1, 1)
                layer3(i, range(0, 4))
                p1_out(i + 1)
                layer3(i, range(4, 8))
                ffn_in(i + 1)

            step(0, True)
            with act.Fori(1, NBLK - 1) as i:
                step(i)
            layer1(NBLK - 1)
            layer2(NBLK - 1, range(8))
            layer3(NBLK - 1, range(8))
            roots(NBLK - 1, s_v4, s_r4, v2a[:, :], r2a[:, :])

        @block.vector
        def _(dve):
            ts, tt, stt, cp = nc.vector.tensor_scalar, nc.vector.tensor_tensor, nc.vector.scalar_tensor_tensor, nc.vector.tensor_copy

            p1, p2, p3 = Steps(dve, s_p1, 16), Steps(dve, s_p2, 3), Steps(dve, s_p3, 3)

            def stats(steps, src, st, mv):
                for t in range(TPB):
                    last = nc.vector.bn_stats(st[:, t, :], src[:, t, :])
                steps.link(last)
                dve.sem_inc(s_dve_on)
                for t in range(TPB):
                    last = nc.vector.bn_aggr(mv[:, t, :], st[:, t, :])
                steps.link(last)

            def recip_var(steps, mv, dst, s_out):
                steps.link(ts(dst, mv[:, :, 1], LN_EPS, None, ADD))
                nc.vector.reciprocal(dst, dst).then_inc(s_out, 1)

            def p1_in(b, n, turn):
                p1.start(b)
                dve.wait_ge(s_x[n], turn * 16 + 16)
                stats(p1, xa[n], st1, mv1)
                p1.link(ts(v1a[:, 0, :], mv1[:, :, 1], LN_EPS, None, ADD))
                p1.link(nc.vector.reciprocal(v1a[:, 0, :], v1a[:, 0, :]))
                p1.link(tt(v1a[:, 1, :], mv1[:, :, 1], v1a[:, 0, :], MUL))
                p1.link(ts(v1a[:, 1, :], v1a[:, 1, :], LN_EPS, None, ADD))
                nc.vector.reciprocal(v1a[:, 1, :], v1a[:, 1, :]).then_inc(s_v1, 1)
                dve.wait_ge(s_r1, b + 1)
                p1.mark(tt(r12[:, :], r1a[:, 0, :], r1a[:, 1, :], MUL))
                p1.link(nc.vector.reciprocal(inv_r2[:, :], r1a[:, 1, :]))
                for t in range(TPB):
                    last = ts(yn[:, t, :], xa[n][:, t, :], mv1[:, t, 0:1], r12[:, t:t + 1], SUB, MUL)
                last.then_inc(s_yn, 1)

            def p1_split(b):
                for c in range(DC):
                    dve.wait_ge(s_aff, b * DC + c + 1)
                    last = cp(yt_hi[:, c, :], act2[:, c, :])
                p1.link(last)
                for c in range(DC):
                    tt(yt_lo[:, c, :], act2[:, c, :], yt_hi[:, c, :].bitcast(fp32), SUB).then_inc(s_nt, 1)

            def p1_scan(b, m):
                dve.wait_ge(s_c, b * DC + m + 1)
                dve.wait_ge(s_sig, (b * DC + m) * 2 + 2)
                stt(zc[:, :], pt[1][:, :], vec("bc", m), act2[:, 0, :], ADD, MUL).then_inc(s_zc, 1)
                dve.wait_ge(s_zc, b * DC + m + 1)
                nc.vector.tensor_tensor_scan(hs[:, m, :], act2[:, 1, :], zc[:, :], carry[:, m:m + 1], MUL, ADD).then_inc(s_scan, 1)
                dve.wait_ge(s_scan, b * DC + m + 1)
                p1.link(tt(carry[:, m:m + 1], hs[:, m, BLK - 1:BLK], carry_on[:, bass.ds(b + 1, 1)], MUL))

            def p1_out(b, n):
                dve.wait_ge(s_ht, b + 1)
                for t in range(TPB):
                    last = stt(o1[:, t, :], yn[:, t, :], inv_r2[:, t:t + 1], pt[t // 2][:, (t % 2) * D:(t % 2 + 1) * D], MUL, ADD)
                p1.link(last)
                stats(p1, o1, st1, mv1)
                recip_var(p1, mv1, v1a[:, 0, :], s_vo)
                dve.wait_ge(s_ro, b + 1)
                for t in range(TPB):
                    last = ts(o1[:, t, :], o1[:, t, :], mv1[:, t, 0:1], r1a[:, 0, t:t + 1], SUB, MUL)
                p1.link(last)
                tt(xa[n][:, :, :], xa[n][:, :, :], o1[:, :, :], ADD).then_inc(s_xa, 1)
                p1.end()
                dve.wait_ge(s_xa, b + 1)

            def ffn_norm(b, n):
                p2.start(b)
                stats(p2, xa[n], st1, mv1)
                recip_var(p2, mv1, v1a[:, 1, :], s_v2)
                dve.wait_ge(s_r2, b + 1)
                for t in range(TPB):
                    last = ts(yn[:, t, :], xa[n][:, t, :], mv1[:, t, 0:1], r1a[:, 1, t:t + 1], SUB, MUL)
                last.then_inc(s_y2, 1)
                p2.end()

            def ffn_in(b):
                for c in range(DC):
                    dve.wait_ge(s_yhi, b * DC + c + 1)
                    tt(yt_lo[:, c, :], pt[c][:, :], yt_hi[:, c, :].bitcast(fp32), SUB).then_inc(s_ylo, 1)

            def layer1(b, first=False):
                for m in range(HC):
                    if m == 2 and not first:
                        ffn_out(b - 1)
                    dve.wait_ge(s_l1b, b * HC + m + 1)
                    dve.wait_ge(s_silu, b * HC + m + 1)
                    if m >= 2:
                        dve.wait_ge(s_f1lo, b * HC + m - 1)
                    stt(f2[:, m % 2, :], ff[2 * (m % 2) + 1][:, :], vec("w2_s", m), act2[:, m % 2, :], MUL, MUL).then_inc(s_f1, 1)
                    if m:
                        low1(b, m - 1)
                low1(b, HC - 1)

            def low1(b, m):
                dve.wait_ge(s_f1hi, b * HC + m + 1)
                tt(ha_lo[:, m, :], f2[:, m % 2, :], ha_hi[:, m, :].bitcast(fp32), SUB).then_inc(s_f1lo, 1)

            def hidden(b, ms, s_in, s_high, s_low, hi, lo):
                for m in ms:
                    dve.wait_ge(s_in, b * HC + m + 1)
                    cp(hi[:, m, :], f2[:, m % 2, :]).then_inc(s_high, 1)
                    dve.wait_ge(s_high, b * HC + m + 1)
                    tt(lo[:, m, :], f2[:, m % 2, :], hi[:, m, :].bitcast(fp32), SUB).then_inc(s_low, 1)

            def layer2(b, ms):
                hidden(b, ms, s_g2, s_g2hi, s_g2lo, hb_hi, hb_lo)

            def layer3(b, ms):
                hidden(b, ms, s_g3, s_g3hi, s_g3lo, ha_hi, ha_lo)

            def ffn_scaled(b, first=False):
                if not first:
                    dve.wait_ge(s_st, b * 16)
                for n in range(2):
                    dve.wait_ge(s_l4, 2 * b + n + 1)
                    for t in range(2 * n, 2 * n + 2):
                        last = tt(o2[:, t, :], pyo[n][:, (t % 2) * D:(t % 2 + 1) * D], w3s_row[:, :], MUL)
                last.then_inc(s_y4, 1)

            def ffn_out(b):
                p3.start(b)
                dve.wait_ge(s_y4, b + 1)
                stats(p3, o2, st2, mv2)
                p3.link(ts(v2a[:, :], mv2[:, :, 1], LN_EPS, None, ADD))
                nc.vector.reciprocal(v2a[:, :], v2a[:, :]).then_inc(s_v4, 1)
                p3.end()

            nc.vector.memset(carry[:, :], 0.0)
            nc.vector.memset(carry_on[:, 0:NBLK + 2:2], 0.0).then_inc(s_masks, 1)
            nc.vector.memset(carry_on[:, 1:NBLK + 2:2], 1.0).then_inc(s_masks, 1)
            p1_in(0, 0, 0)
            p1_split(0)
            dve.wait_ge(s_wsplit, 2)
            tt(w_gate_lo[:, :, :], o2[:, 0:2, :], w_gate_hi[:, :, :].bitcast(fp32), SUB).then_inc(s_wlo, 1)
            tt(w_cand_lo[:, :, :], o2[:, 2:4, :], w_cand_hi[:, :, :].bitcast(fp32), SUB).then_inc(s_wlo, 1)

            def weight_check(ns):
                for n in ns:
                    _, staged, rounded = ffn_weights[n]
                    dve.wait_ge(s_round, n + 1)
                    stt(staged[:, :], rounded.bitcast(fp32), 0.0, staged[:, :], ADD, ALU.not_equal,
                        accum_out=chk[:, n:n + 1]).then_inc(s_chk, 1)

            weight_check(range(0, 3))
            dve.wait_ge(s_masks, 3)
            p1_scan(0, 0)
            p1_scan(0, 1)
            weight_check(range(3, 5))
            p1_out(0, 0)
            ffn_norm(0, 0)
            ffn_in(0)
            weight_check(range(5, 7))
            dve.wait_ge(s_chk, FFN_PIECES)
            nc.vector.reduce_sum(chk1[:, :], chk[:, :], axis=AX.X).then_inc(s_flag0, 1)
            dve.wait_ge(s_flag1, 1)
            ts(split_flag[:, :], chk_all[0:1, :], 0.0, None, ALU.is_gt).then_inc(s_flag, 1)

            def step(i, n, turn, first=False):
                layer1(i, first)
                layer2(i, range(0, 2))
                p1_in(i + 1, n, turn)
                layer2(i, range(2, 4))
                p1_split(i + 1)
                layer2(i, range(4, 6))
                p1_scan(i + 1, 0)
                layer2(i, range(6, 8))
                p1_scan(i + 1, 1)
                layer3(i, range(0, 4))
                p1_out(i + 1, n)
                ffn_norm(i + 1, n)
                layer3(i, range(4, 8))
                ffn_in(i + 1)
                ffn_scaled(i, first)

            step(0, 1, 0, True)
            with dve.Fori(1, NBLK // 2) as i:
                step(i * 2 - 1, 0, i)
                step(i * 2, 1, i)
            layer1(NBLK - 1)
            layer2(NBLK - 1, range(8))
            layer3(NBLK - 1, range(8))
            ffn_scaled(NBLK - 1)
            ffn_out(NBLK - 1)

        block_ctx.close()
        end_phase()

        cursor[0] = shared_from
        kvr = {n: [[sb(f"w_{n}_{when}_{s}", [P, DC, D], fp32r) for s in ("hi", "lo")] for when in ("now", "before")]
               for n in ("k", "v", "r")}
        w_out = [sb(f"w_out_{s}", [P, DC, D], fp32r) for s in ("hi", "lo")]
        w_r2 = [sb(f"w_r2_{s}", [P, DC, D], fp32r) for s in ("hi", "lo")]
        w_k2 = [sb(f"w_k2_{s}", [P, DC, HID], fp32r) for s in ("hi", "lo")]
        w_v2 = [sb(f"w_v2_{s}", [P, HC, D], fp32r) for s in ("hi", "lo")]
        x_pre, x_fin = sb("x_pre", [P, TPB, D]), sb("x_fin", [P, TPB, D])
        y_new, y_res = sb("y_new", [P, TPB, D]), sb("y_res", [P, TPB, D])
        y_rms = sb("y_rms", [P, TPB, D])
        x1 = y_res
        h2n = sb("h2n", [P, TPB, D])
        xr = sb("xr", [P, TPB, ROW])
        EXT = BLK + 2
        hT = [sb(f"hT_{s}", [P, DC, EXT], fp32r) for s in ("hi", "lo")]
        h2T = sb("h2T", [P, DC, EXT])
        ek, ekt, e_r = (sb(n, [P, DC, BLK]) for n in ("ek", "ekt", "e_r"))
        st_a, st_b = sb("st_a", [P, DC, EXT]), sb("st_b", [P, DC, EXT])
        ekv, num = sb("ekv", [P, BLK]), sb("num", [P, DC, BLK])
        rw = [sb(f"rw_{s}", [P, DC, BLK], fp32r) for s in ("hi", "lo")]
        mixf = sb("mixf", [P, 2, BLK])
        d2 = sb("d2", [P, DC, BLK], at=place["h2n"])
        xk2 = [sb(f"xk2_{s}", [P, DC, BLK], fp32r) for s in ("hi", "lo")]
        xr2 = [sb(f"xr2_{s}", [P, DC, BLK], fp32r) for s in ("hi", "lo")]
        kf, kg = sb("kf", [P, 2, BLK]), sb("kg", [P, 2, BLK])
        k2 = [sb(f"k2_{s}", [P, HC, BLK], fp32r) for s in ("hi", "lo")]
        o3 = sb("o3", [P, TPB, D])
        ew = sb("ew", [P, DC])
        one_minus = sb("one_minus", [P, 3 * DC])
        bnA, mvA = sb("bnA", [P, TPB, 6]), sb("mvA", [P, TPB, 2])
        bnB, mvB, mvC = sb("bnB", [P, TPB, 6]), sb("mvB", [P, TPB, 2]), sb("mvC", [P, TPB, 2])
        varA, rootA = sb("varA", [P, 2, TPB]), sb("rootA", [P, 2, TPB])
        varB, rootB = sb("varB", [P, TPB]), sb("rootB", [P, TPB])
        varC, rootC = sb("varC", [P, TPB]), sb("rootC", [P, TPB])
        msq, r12A = sb("msq", [P, TPB]), sb("r12A", [P, TPB])
        v0, v1, i0, i1 = (sb(n, [P, TPB]) for n in ("v0", "v1", "i0", "i1"))
        oh0, oh1 = sb("oh0", [P, TPB, EXP]), sb("oh1", [P, TPB, EXP])
        eq, key, g2, pr = (sb(n, [P, TPB, EXP], at=place["ekv"] + 4 * j * TPB * EXP)
                           for j, n in enumerate(("eq", "key", "g2", "pr")))
        chosen = sb("chosen", [P, TPB, EXP], bf16)
        gap, e_gap, gate0, gate1 = (sb(n, [P, TPB]) for n in ("gap", "e_gap", "gate0", "gate1"))
        pos_f, pos_i = sb("pos_f", [P, 2 * TPB]), sb("pos_i", [P, 2 * TPB], i32)
        varD, rootD = sb("varD", [P, TPB]), sb("rootD", [P, TPB])
        xtT = sb("xtT", [P, DC, BLK], at=place["h2n"])
        stage = {}
        at = place["k2_hi"]
        for n, size in (("k", DC * D), ("v", DC * D), ("r", DC * D), ("out", DC * D), ("r2", DC * D),
                        ("k2", DC * HID), ("v2", HC * D)):
            stage[n] = sb(f"stage_{n}", [P, size], at=at)
            at += 4 * size
        fold = [sb(f"fold_{n}", [P, DC * D], at=place["xk2_hi"] + n * 4 * DC * D) for n in range(2)]

        later_weights = (("out", w_out), ("k2", w_k2), ("r2", w_r2), ("v2", w_v2))

        b_t = bank[0:2]
        b_w = bank[2:4]
        b_k, b_r = bank[4], bank[5]
        b_v = bank[6:8]

        c_stage = {n: sem(f"staged_{n}") for n in stage}
        c_prep, c_const = sem("c_prep_steps"), sem("c_constants")
        c_act_const = sem("c_act_constants")
        c_w, c_w2, c_whi = sem("c_weights_split"), sem("c_later_weights_split"), sem("c_weights_high")
        c_fold, c_fhi = sem("c_weights_folded"), sem("c_folded_high")
        c_x, c_xf = sem("c_x_loaded"), sem("c_x_reloaded")
        c_pre, c_va, c_ra, c_y = sem("c_pre_steps"), sem("c_pre_variances"), sem("c_pre_roots"), sem("c_normalized")
        c_yn, c_vread, c_f1 = sem("c_residual_ready"), sem("c_values_read"), sem("c_gated")
        c_yres = sem("c_residual_copied")
        c_t, c_carry, c_hhi, c_hsplit = sem("c_transposed"), sem("c_h_carried"), sem("c_h_high"), sem("c_h_split")
        c_kp, c_vp, c_rp = sem("c_key_product"), sem("c_value_product"), sem("c_recept_product")
        c_ek, c_er = sem("c_exp_key"), sem("c_exp_recept")
        c_scan = sem("c_scan_steps")
        c_rw, c_rwhi, c_rwlo = sem("c_wkv_ready"), sem("c_wkv_high"), sem("c_wkv_low")
        c_wo = sem("c_out_product")
        c_x1s, c_x1, c_vb, c_rb, c_h2n = sem("c_x1_steps"), sem("c_x1_ready"), sem("c_x1_variances"), sem("c_x1_roots"), sem("c_x1_normalized")
        c_t2, c_h2 = sem("c_x1_transposed"), sem("c_h2_affine")
        c_mixlo_r = sem("c_mix_recept_low")
        c_mix, c_mixhi, c_mixlo, c_h2c = sem("c_mixed"), sem("c_mix_high"), sem("c_mix_low"), sem("c_h2_carried")
        c_k2p, c_relu, c_k2hi, c_k2sq, c_k2lo = sem("c_key2_product"), sem("c_relu"), sem("c_key2_high"), sem("c_key2_squared"), sem("c_key2_low")
        c_r2p, c_r2 = sem("c_recept2_product"), sem("c_recept2_ready")
        c_v2p = sem("c_value2_product")
        c_fin, c_vc, c_rc, c_done, c_st = sem("c_final_steps"), sem("c_final_variances"), sem("c_final_roots"), sem("c_block_done"), sem("c_stored")
        r_pool_on = sem("r_pool_goes_on")
        c_dve_on = sem("c_vector_goes_on")
        r_iota, r_wg = sem("r_iotas"), sem("r_gate_loaded")
        r_vd, r_rd, r_xt = sem("r_variances"), sem("r_roots"), sem("r_normalized")
        r_t, r_tc, r_g = sem("r_transposed"), sem("r_copied"), sem("r_gate_product")
        r_steps, r_dv, r_ex, r_m, r_rank = sem("r_steps"), sem("r_gap"), sem("r_exp"), sem("r_chosen"), sem("r_rank_product")
        r_run, r_pos, r_sc = sem("r_ranks_read"), sem("r_positions"), sem("r_scattered")

        block_ctx = ExitStack()
        block = block_ctx.enter_context(nc.Block())

        @block.sync
        def _(sp):
            sp.dma_start(x_pre[:, :, :], mid_blocks[:, 0:TPB, :]).then_inc(c_x, 16)
            for n, src in (("k", wk_in), ("v", wv_in), ("r", wr_in), ("out", wo_in), ("k2", wk2_in), ("r2", wr2_in), ("v2", wv2_in)):
                sp.dma_start(stage[n][:, :], src).then_inc(c_stage[n], 16)

            sp.dma_start(wg8[:, :, :], wg8_in).then_inc(r_wg, 16)
            sp.dma_start(x_fin[:, :, :], mid_blocks[:, 0:TPB, :]).then_inc(c_xf, 16)
            sp.wait_ge(c_y, 1)
            sp.wait_ge(c_yn, 1)
            sp.dma_start(x_pre[:, :, :], mid_blocks[:, TPB:2 * TPB, :]).then_inc(c_x, 16)

            def load_pre(i):
                sp.wait_ge(c_y, i + 2)
                sp.wait_ge(c_yn, i + 2)
                sp.dma_start(x_pre[:, :, :], mid_blocks[:, bass.ds((i + 2) * TPB, TPB), :]).then_inc(c_x, 16)

            def store(b, last=False):
                sp.wait_ge(c_done, b + 1)
                sp.dma_start(x3_blocks[:, bass.ds(b * TPB, TPB), :], o3[:, :, :]).then_inc(c_st, 16)
                if not last:
                    sp.dma_start(x_fin[:, :, :], mid_blocks[:, bass.ds((b + 1) * TPB, TPB), :]).then_inc(c_xf, 16)

            load_pre(0)
            with sp.Fori(1, NBLK - 2) as i:
                load_pre(i)
                store(i - 1)
            store(NBLK - 3)
            store(NBLK - 2)
            store(NBLK - 1, True)
            sp.wait_ge(c_st, 16 * NBLK)
            sp.wait_ge(r_sc, 16 * 2 * TPB * NBLK)

        @block.gpsimd
        def _(pool):
            def squares(b):
                for m in range(HC):
                    pool.wait_ge(c_relu, b * HC + m + 1)
                    if m >= 2:
                        pool.wait_ge(c_k2lo, b * HC + m - 1)
                    nc.gpsimd.tensor_tensor(kg[:, m % 2, :], kf[:, m % 2, :], kf[:, m % 2, :], MUL).then_inc(c_k2sq, 1)
                    pool.wait_ge(c_k2sq, b * HC + m + 1)
                    pool.wait_ge(c_k2hi, b * HC + m + 1)
                    nc.gpsimd.tensor_tensor(k2[1][:, m, :], kg[:, m % 2, :], k2[0][:, m, :].bitcast(fp32), SUB).then_inc(c_k2lo, 1)

            def normed(b):
                pool.wait_ge(c_ra, b + 1)
                if not (isinstance(b, int) and b == 0):
                    pool.wait_ge(c_yres, b)
                pool.sem_inc(r_pool_on)
                for t in range(TPB):
                    last = nc.gpsimd.tensor_scalar(y_new[:, t, :], x_pre[:, t, :], mvA[:, t, 0:1], rootA[:, 0, t:t + 1], SUB, MUL)
                last.then_inc(c_yn, 1)

            def mix_r_low(b):
                for c in range(DC):
                    pool.wait_ge(c_mixhi, b * 4 + 3 + c)
                    nc.gpsimd.tensor_tensor(xr2[1][:, c, :], mixf[:, c, :], xr2[0][:, c, :].bitcast(fp32), SUB).then_inc(c_mixlo_r, 1)

            def scatter(b):
                pool.wait_ge(r_pos, b + 1)
                pool.sem_inc(r_pool_on)
                for k in range(2):
                    for t in range(TPB):
                        nc.gpsimd.indirect_dma_start(
                            routed, bass.IndirectOffsetOnAxis(ap=pos_i[:, k * TPB + t:k * TPB + t + 1], axis=0),
                            xr[:, t, :], None).then_inc(r_sc, 16)

            nc.gpsimd.iota(eno_i[:, :], pattern=[[1, EXP]], base=0, channel_multiplier=0).then_inc(r_iota, 1)
            nc.gpsimd.iota(ids_i[:, :], pattern=[[2 * P, TPB]], base=0, channel_multiplier=2).then_inc(r_iota, 1)
            nc.gpsimd.memset(upper[:, :], 1.0).then_inc(r_iota, 1)
            pool.wait_ge(r_iota, 3)
            nc.gpsimd.affine_select(out=upper[:, :], in_=upper[:, :], compare_op=ALU.is_gt, fill=0.0, base=0,
                                    pattern=[[1, P]], channel_multiplier=-1).then_inc(r_iota, 1)
            normed(0)
            for j, (n, w) in enumerate(later_weights):
                pool.wait_ge(c_whi, j + 1)
                nc.gpsimd.tensor_tensor(w[1][:, :, :], stage[n][:, :].rearrange("p (c n) -> p c n", c=w[0].shape[1]),
                                        w[0][:, :, :].bitcast(fp32), SUB).then_inc(c_w2, 1)
            normed(1)
            mix_r_low(0)
            squares(0)
            with pool.Fori(1, NBLK - 1) as i:
                normed(i + 1)
                mix_r_low(i)
                squares(i)
                scatter(i - 1)
            mix_r_low(NBLK - 1)
            squares(NBLK - 1)
            scatter(NBLK - 2)
            scatter(NBLK - 1)

        @block.tensor
        def _(pe):
            mm = nc.tensor.matmul

            def transpose(dst, src, b, s_in, s_out):
                pe.wait_ge(s_in, b + 1)
                for c in range(DC):
                    for t in range(TPB):
                        last = nc.tensor.transpose(dst[c][:, t * P:(t + 1) * P], src[:, t, c * P:(c + 1) * P], ident[:, :])
                    last.then_inc(s_out, 1)

            def product(dst, m, pairs):
                terms = [(w[i][:, c, m * P:(m + 1) * P], y[j](c)) for w, y in pairs for c in range(DC) for i, j in ((0, 0), (1, 0), (0, 1))]
                for n, (a, y) in enumerate(terms):
                    last = mm(dst[:, :], a, y, start=n == 0, stop=n == len(terms) - 1)
                return last

            now = [lambda c, h=h: h[:, c, 1:BLK + 1] for h in hT]
            before = [lambda c, h=h: h[:, c, 0:BLK] for h in hT]

            def kvr_products(b, m, first=False, second=False):
                pe.wait_ge(c_hsplit, b * DC + DC)
                if m == 0:
                    if not first and not second:
                        pe.wait_ge(c_relu, b * HC - HC)
                else:
                    pe.wait_ge(c_ek, (b * DC + m) * 2)
                if first:
                    pe.wait_ge(c_w, 1)
                product(b_k, m, ((kvr["k"][0], now), (kvr["k"][1], before))).then_inc(c_kp, 1)
                if first:
                    pe.wait_ge(c_w, 2)
                product(b_v[m], m, ((kvr["v"][0], now), (kvr["v"][1], before))).then_inc(c_vp, 1)
                if first:
                    pe.wait_ge(c_w, 3)
                if m:
                    pe.wait_ge(c_er, b * DC + m)
                product(b_r, m, ((kvr["r"][0], now), (kvr["r"][1], before))).then_inc(c_rp, 1)

            def token_product(dst, x, w, n_k, s_done):
                for t in range(TPB):
                    terms = [(x[i][:, k, t * P:(t + 1) * P], w[j][:, k, :]) for k in range(n_k) for i, j in ((0, 0), (0, 1), (1, 0))]
                    for n, (a, y) in enumerate(terms):
                        last = mm(dst[t // 2][:, (t % 2) * D:(t % 2 + 1) * D], a, y, start=n == 0, stop=n == len(terms) - 1)
                    if t % 2:
                        last.then_inc(s_done, 1)

            def out_product(b, first=False):
                pe.wait_ge(c_rwlo, b * DC + DC)
                if not first:
                    pe.wait_ge(c_r2, b * 2)
                token_product(b_w, rw, w_out, DC, c_wo)

            def keys2(b, ms):
                pe.wait_ge(c_mixlo, b * 2 + 2)
                for m in ms:
                    if m >= 2:
                        pe.wait_ge(c_relu, b * HC + m - 1)
                    product((b_k, b_r)[m % 2], m, ((w_k2, [lambda c, h=h: h[:, c, :] for h in xk2]),)).then_inc(c_k2p, 1)

            def recept2(b):
                pe.wait_ge(c_mixlo_r, b * 2 + 2)
                token_product(b_w, xr2, w_r2, DC, c_r2p)

            def values2(b):
                pe.wait_ge(c_k2lo, b * HC + HC)
                token_product(b_t, k2, w_v2, HC, c_v2p)

            def route_in(b):
                pe.wait_ge(r_xt, b + 1)
                for c in range(DC):
                    for t in range(TPB):
                        last = nc.tensor.transpose(b_w[c][:, t * P:(t + 1) * P], xr[:, t, c * P:(c + 1) * P], ident[:, :])
                    last.then_inc(r_t, 1)

            def route_gate(b):
                pe.wait_ge(r_tc, b * DC + DC)
                for t in range(TPB):
                    for c in range(DC):
                        last = mm(b_w[0][:, t * EXP:(t + 1) * EXP], xtT[:, c, t * P:(t + 1) * P], wg8[:, c, :], start=c == 0, stop=c == DC - 1)
                last.then_inc(r_g, 1)

            def route_rank(b):
                pe.wait_ge(r_m, b + 1)
                for t in range(TPB):
                    for n in range(t + 1):
                        mm(b_w[1][:, t * EXP:(t + 1) * EXP], (upper if n == t else ones_bf)[:, :], chosen[:, n, :], start=n == 0, stop=n == t)
                for n in range(TPB):
                    last = mm(b_w[1][:, TPB * EXP:(TPB + 1) * EXP], ones_bf[:, :], chosen[:, n, :], start=n == 0, stop=n == TPB - 1)
                last.then_inc(r_rank, 1)

            def transpose_in(b):
                if not (isinstance(b, int) and b == 0):
                    pe.wait_ge(c_vread, b * DC)
                transpose(b_v, y_rms, b, c_y, c_t)

            def transpose_mid(b):
                if not (isinstance(b, int) and b == 0):
                    pe.wait_ge(c_f1, b)
                transpose(b_t, h2n, b, c_h2n, c_t2)

            def second_half(b, first=False, more=True):
                keys2(b, range(0, 5))
                if not first:
                    route_in(b - 1)
                keys2(b, range(5, 6))
                if not first:
                    route_gate(b - 1)
                keys2(b, range(6, HC))
                if not first:
                    route_rank(b - 1)
                values2(b)
                if more:
                    transpose_in(b + 2)
                if not first:
                    pe.wait_ge(r_run, b)
                recept2(b)

            transpose_in(0)
            kvr_products(0, 0, True)
            kvr_products(0, 1, True)
            transpose_in(1)

            def step(i, first=False, more=True):
                out_product(i, first)
                kvr_products(i + 1, 0, second=first)
                transpose_mid(i)
                kvr_products(i + 1, 1)
                pe.wait_ge(c_ek, (i + 2) * DC * 2)
                pe.wait_ge(c_er, (i + 2) * DC)
                second_half(i, first, more)

            pe.wait_ge(c_w2, len(later_weights))
            pe.wait_ge(r_iota, 4)
            pe.wait_ge(r_wg, 16)
            step(0, True)
            with pe.Fori(1, NBLK - 2) as i:
                step(i)
            step(NBLK - 2, more=False)
            out_product(NBLK - 1)
            transpose_mid(NBLK - 1)
            second_half(NBLK - 1, more=False)
            pe.wait_ge(c_r2, NBLK * 2)
            route_in(NBLK - 1)
            route_gate(NBLK - 1)
            route_rank(NBLK - 1)

        @block.scalar
        def _(act):
            fn = nc.scalar.activation

            def root(b, s_in, s_out, v, r):
                act.wait_ge(s_in, b + 1)
                fn(r, v, ACT.Sqrt).then_inc(s_out, 1)

            def pre_root(b):
                root(b, c_va, c_ra, varA[:, :, :], rootA[:, :, :])

            def h_high(b):
                act.wait_ge(c_carry, b + 1)
                for c in range(DC):
                    act.wait_ge(c_t, b * DC + c + 1)
                    fn(hT[0][:, c, 1:BLK + 1], b_v[c][:, :], ACT.Copy, scale=vec("ln1_w", c)).then_inc(c_hhi, 1)

            def exp_key(b, m):
                act.wait_ge(c_kp, b * DC + m + 1)
                fn(ek[:, m, :], b_k[:, :], ACT.Exp).then_inc(c_ek, 1)
                fn(ekt[:, m, :], b_k[:, :], ACT.Exp, bias=vec("first", m)).then_inc(c_ek, 1)

            def exp_recept(b, m):
                act.wait_ge(c_rp, b * DC + m + 1)
                fn(e_r[:, m, :], b_r[:, :], ACT.Exp, scale=-1.0).then_inc(c_er, 1)

            def wkv_high(b, m):
                act.wait_ge(c_rw, b * DC + m + 1)
                fn(rw[0][:, m, :], num[:, m, :], ACT.Copy).then_inc(c_rwhi, 1)

            def h2_affine(b):
                if isinstance(b, int) and b == 0:
                    pass
                else:
                    act.wait_ge(c_h2c, b)
                for c in range(DC):
                    act.wait_ge(c_t2, b * DC + c + 1)
                    fn(h2T[:, c, 1:BLK + 1], b_t[c][:, :], ACT.Copy, scale=vec("ln2_w", c)).then_inc(c_h2, 1)

            def mix_high(b):
                for n in range(4):
                    act.wait_ge(c_mix, b * 4 + n + 1)
                    fn((xk2, xr2)[n // 2][0][:, n % 2, :], mixf[:, n % 2, :], ACT.Copy).then_inc(c_mixhi, 1)

            def keys2(b, m):
                act.wait_ge(c_k2p, b * HC + m + 1)
                if m >= 2:
                    act.wait_ge(c_k2sq, b * HC + m - 1)
                fn(kf[:, m % 2, :], (b_k, b_r)[m % 2][:, :], ACT.Relu).then_inc(c_relu, 1)
                act.wait_ge(c_relu, b * HC + m + 1)
                fn(k2[0][:, m, :], kf[:, m % 2, :], ACT.Square).then_inc(c_k2hi, 1)

            def recept2(b):
                for n in range(2):
                    act.wait_ge(c_r2p, b * 2 + n + 1)
                    fn(o3[:, 2 * n:2 * n + 2, :], b_w[n][:, :].rearrange("p (t d) -> p t d", d=D), ACT.Sigmoid).then_inc(c_r2, 1)

            def route_copy(b):
                for c in range(DC):
                    act.wait_ge(r_t, b * DC + c + 1)
                    fn(xtT[:, c, :], b_w[c][:, :], ACT.Copy).then_inc(r_tc, 1)

            def route_exp(b):
                act.wait_ge(r_dv, b + 1)
                fn(e_gap[:, :], gap[:, :], ACT.Exp).then_inc(r_ex, 1)

            def high_weights(a, z):
                for n, w in later_weights[a:z]:
                    act.wait_ge(c_stage[n], 16)
                    fn(w[0][:, :, :], stage[n][:, :].rearrange("p (c n) -> p c n", c=w[0].shape[1]), ACT.Copy).then_inc(c_whi, 1)

            fn(ew[:, :], vecs[:, VEC["decay"]:VEC["decay"] + DC], ACT.Exp).then_inc(c_act_const, 1)
            act.wait_ge(c_const, 1)
            fn(ew[:, :], ew[:, :], ACT.Exp).then_inc(c_act_const, 1)
            pre_root(0)
            for j, n in enumerate(("k", "v", "r")):
                act.wait_ge(c_fold, j + 1)
                for part in range(2):
                    last = fn(kvr[n][part][0][:, :, :], fold[part][:, :].rearrange("p (c n) -> p c n", c=DC), ACT.Copy)
                last.then_inc(c_fhi, 1)
                if j == 0:
                    h_high(0)
            high_weights(0, 1)
            for m in range(DC):
                exp_key(0, m)
                exp_recept(0, m)
                high_weights(1 + m, 2 + m)
            wkv_high(0, 0)
            pre_root(1)
            high_weights(3, 4)
            wkv_high(0, 1)
            h_high(1)

            def second_half(b, first=False, more=True):
                for m in range(2):
                    keys2(b, m)
                if not first:
                    root(b - 1, r_vd, r_rd, varD[:, :], rootD[:, :])
                for m in range(2, 5):
                    keys2(b, m)
                if more:
                    pre_root(b + 2)
                keys2(b, 5)
                if not first:
                    route_copy(b - 1)
                keys2(b, 6)
                keys2(b, 7)

            def recept2_out(b):
                if not (isinstance(b, int) and b == 0):
                    act.wait_ge(c_st, b * 16)
                recept2(b)

            def step(i, first=False, more=True):
                exp_key(i + 1, 0)
                if not first:
                    root(i - 1, c_vc, c_rc, varC[:, :], rootC[:, :])
                root(i, c_vb, c_rb, varB[:, :], rootB[:, :])
                exp_recept(i + 1, 0)
                h2_affine(i)
                exp_key(i + 1, 1)
                mix_high(i)
                exp_recept(i + 1, 1)
                second_half(i, first, more)
                wkv_high(i + 1, 0)
                if not first:
                    route_exp(i - 1)
                if more:
                    h_high(i + 2)
                wkv_high(i + 1, 1)
                recept2_out(i)

            step(0, first=True)
            with act.Fori(1, NBLK - 2) as i:
                step(i)
            step(NBLK - 2, more=False)
            b = NBLK - 1
            root(b - 1, c_vc, c_rc, varC[:, :], rootC[:, :])
            root(b, c_vb, c_rb, varB[:, :], rootB[:, :])
            h2_affine(b)
            mix_high(b)
            second_half(b, more=False)
            route_exp(b - 1)
            recept2_out(b)
            root(b, c_vc, c_rc, varC[:, :], rootC[:, :])
            root(b, r_vd, r_rd, varD[:, :], rootD[:, :])
            route_copy(b)
            route_exp(b)

        @block.vector
        def _(dve):
            ts, tt, stt, cp = nc.vector.tensor_scalar, nc.vector.tensor_tensor, nc.vector.scalar_tensor_tensor, nc.vector.tensor_copy

            pre_s, scan_s, x1_s, fin_s = Steps(dve, c_pre, 7), Steps(dve, c_scan, 18), Steps(dve, c_x1s, 5), Steps(dve, c_fin, 8)
            rt = Steps(dve, r_steps, 20)

            def stats(steps, src, bn, mv):
                for t in range(TPB):
                    last = nc.vector.bn_stats(bn[:, t, :], src[:, t, :])
                steps.link(last)
                dve.sem_inc(c_dve_on)
                for t in range(TPB):
                    last = nc.vector.bn_aggr(mv[:, t, :], bn[:, t, :])
                steps.link(last)

            def pre(b):
                pre_s.start(b)
                dve.wait_ge(c_x, (b + 1) * 16)
                stats(pre_s, x_pre, bnA, mvA)
                pre_s.link(ts(varA[:, 0, :], mvA[:, :, 1], LN_EPS, None, ADD))
                pre_s.link(nc.vector.reciprocal(varA[:, 0, :], varA[:, 0, :]))
                pre_s.link(tt(varA[:, 1, :], mvA[:, :, 1], varA[:, 0, :], MUL))
                pre_s.link(ts(varA[:, 1, :], varA[:, 1, :], RMS_EPS, None, ADD))
                nc.vector.reciprocal(varA[:, 1, :], varA[:, 1, :]).then_inc(c_va, 1)
                dve.wait_ge(c_ra, b + 1)
                pre_s.link(tt(r12A[:, :], rootA[:, 0, :], rootA[:, 1, :], MUL))
                for t in range(TPB):
                    last = ts(y_rms[:, t, :], x_pre[:, t, :], mvA[:, t, 0:1], r12A[:, t:t + 1], SUB, MUL)
                last.then_inc(c_y, 1)
                pre_s.end()

            def b_is_not_first(b):
                return not (isinstance(b, int) and b == 0)

            def h_carry(b):
                if b_is_not_first(b):
                    dve.wait_ge(c_rp, b * DC)
                    for h in hT:
                        last = tt(h[:, :, 0:1], h[:, :, BLK:BLK + 1].bitcast(fp32),
                                  carry_on[:, bass.ds(b, 1)].unsqueeze(1).to_broadcast([P, DC, 1]), MUL)
                else:
                    for h in hT:
                        last = cp(h[:, :, 0:1], carry_on[:, 0:1].unsqueeze(1).to_broadcast([P, DC, 1]))
                last.then_inc(c_carry, 1)

            def h_low(b):
                dve.wait_ge(c_carry, b + 1)
                for c in range(DC):
                    dve.wait_ge(c_hhi, b * DC + c + 1)
                    stt(hT[1][:, c, 1:BLK + 1], b_v[c][:, :], vec("ln1_w", c), hT[0][:, c, 1:BLK + 1].bitcast(fp32), MUL, SUB).then_inc(c_hsplit, 1)

            def scan(b, m):
                if m == 0:
                    scan_s.start(b)
                lo, hi = CLIP
                dve.wait_ge(c_ek, (b * DC + m) * 2 + 2)
                scan_s.mark(ts(ek[:, m, :], ek[:, m, :], lo, hi, MAX, MIN))
                scan_s.link(ts(ekt[:, m, :], ekt[:, m, :], lo, hi, MAX, MIN))
                dve.wait_ge(c_vp, b * DC + m + 1)
                scan_s.mark(tt(ekv[:, :], ek[:, m, :], b_v[m][:, :], MUL))
                tt(num[:, m, :], ekt[:, m, :], b_v[m][:, :], MUL).then_inc(c_vread, 1)
                scan_s.wait()
                dve.wait_ge(c_vread, b * DC + m + 1)
                decay = ew[:, m:m + 1].broadcast_to([P, BLK])
                scan_s.mark(nc.vector.tensor_tensor_scan(st_b[:, m, 1:BLK + 1], decay, ek[:, m, :], st_b[:, m, 0:1], MUL, ADD))
                scan_s.link(nc.vector.tensor_tensor_scan(st_a[:, m, 1:BLK + 1], decay, ekv[:, :], st_a[:, m, 0:1], MUL, ADD))
                scan_s.mark(tt(num[:, m, :], num[:, m, :], st_a[:, m, 0:BLK], ADD))
                scan_s.link(stt(ekt[:, m, :], st_b[:, m, 0:BLK], 1e-8, ekt[:, m, :], ADD, ADD))
                tt(st_a[:, m, 0:1], st_a[:, m, BLK:BLK + 1], carry_on[:, bass.ds(b + 1, 1)], MUL)
                tt(st_b[:, m, 0:1], st_b[:, m, BLK:BLK + 1], carry_on[:, bass.ds(b + 1, 1)], MUL)
                dve.wait_ge(c_er, b * DC + m + 1)
                scan_s.link(stt(ekt[:, m, :], e_r[:, m, :], 1.0, ekt[:, m, :], ADD, MUL))
                scan_s.link(nc.vector.reciprocal(ekt[:, m, :], ekt[:, m, :]))
                tt(num[:, m, :], num[:, m, :], ekt[:, m, :], MUL).then_inc(c_rw, 1)

            def wkv_low(b, m):
                dve.wait_ge(c_rwhi, b * DC + m + 1)
                tt(rw[1][:, m, :], num[:, m, :], rw[0][:, m, :].bitcast(fp32), SUB).then_inc(c_rwlo, 1)

            def out_add(b):
                x1_s.start(b)
                dve.wait_ge(c_yres, b + 1)
                for n in range(2):
                    dve.wait_ge(c_wo, b * 2 + n + 1)
                    last = tt(x1[:, 2 * n:2 * n + 2, :], y_res[:, 2 * n:2 * n + 2, :], b_w[n][:, :].rearrange("p (t d) -> p t d", d=D), ADD)
                last.then_inc(c_x1, 1)
                dve.wait_ge(c_x1, b + 1)
                stats(x1_s, x1, bnB, mvB)
                x1_s.link(tt(msq[:, :], mvB[:, :, 0], mvB[:, :, 0], MUL))
                x1_s.link(stt(varB[:, :], msq[:, :], RMS_EPS, mvB[:, :, 1], ADD, ADD))
                nc.vector.reciprocal(varB[:, :], varB[:, :]).then_inc(c_vb, 1)

            def x1_norm(b):
                dve.wait_ge(c_rb, b + 1)
                for t in range(TPB):
                    last = ts(h2n[:, t, :], x1[:, t, :], rootB[:, t:t + 1], None, MUL)
                last.then_inc(c_h2n, 1)

            def mixes(b):
                dve.wait_ge(c_h2, b * DC + DC)
                for c in range(DC):
                    last = tt(d2[:, c, :], h2T[:, c, 1:BLK + 1], h2T[:, c, 0:BLK], SUB)
                x1_s.link(last)
                for n in range(4):
                    kind, c = n // 2, n % 2
                    if n >= 2:
                        mix_low(b, n - 2)
                        dve.wait_ge(c_mixlo, b * 2 + n - 1)
                    stt(mixf[:, c, :], d2[:, c, :], vec(("mix_k2", "mix_r2")[kind], c), h2T[:, c, 0:BLK], MUL, ADD).then_inc(c_mix, 1)
                dve.wait_ge(c_mix, b * 4 + 4)
                tt(h2T[:, :, 0:1], h2T[:, :, BLK:BLK + 1], carry_on[:, bass.ds(b + 1, 1)].unsqueeze(1).to_broadcast([P, DC, 1]), MUL).then_inc(c_h2c, 1)
                x1_s.end()

            def mix_low(b, n):
                dve.wait_ge(c_mixhi, b * 4 + n + 1)
                tt(xk2[1][:, n, :], mixf[:, n, :], xk2[0][:, n, :].bitcast(fp32), SUB).then_inc(c_mixlo, 1)

            def gated(b):
                fin_s.start(b)
                for n in range(2):
                    dve.wait_ge(c_v2p, b * 2 + n + 1)
                    dve.wait_ge(c_r2, b * 2 + n + 1)
                    last = tt(o3[:, 2 * n:2 * n + 2, :], o3[:, 2 * n:2 * n + 2, :], b_t[n][:, :].rearrange("p (t d) -> p t d", d=D), MUL)
                last.then_inc(c_f1, 1)
                dve.wait_ge(c_f1, b + 1)
                fin_s.link(tt(o3[:, :, :], o3[:, :, :], x1[:, :, :], ADD))
                stats(fin_s, o3, bnB, mvC)
                fin_s.link(ts(varC[:, :], mvC[:, :, 1], LN_EPS, None, ADD))
                nc.vector.reciprocal(varC[:, :], varC[:, :]).then_inc(c_vc, 1)

            def final(b):
                dve.wait_ge(c_rc, b + 1)
                for t in range(TPB):
                    last = ts(o3[:, t, :], o3[:, t, :], mvC[:, t, 0:1], rootC[:, t:t + 1], SUB, MUL)
                fin_s.link(last)
                dve.wait_ge(c_xf, b * 16 + 16)
                tt(o3[:, :, :], o3[:, :, :], x_fin[:, :, :], ADD).then_inc(c_done, 1)
                dve.wait_ge(c_done, b + 1)
                stats(fin_s, o3, bnB, mvB)
                fin_s.link(ts(varD[:, :], mvB[:, :, 1], LN_EPS, None, ADD))
                nc.vector.reciprocal(varD[:, :], varD[:, :]).then_inc(r_vd, 1)
                if b_is_not_first(b):
                    dve.wait_ge(r_sc, b * (16 * 2 * TPB))
                dve.wait_ge(r_rd, b + 1)
                for t in range(TPB):
                    last = ts(xr[:, t, 0:D], o3[:, t, :], mvB[:, t, 0:1], rootD[:, t:t + 1], SUB, MUL)
                last.then_inc(r_xt, 1)
                fin_s.end()

            def residual(b):
                dve.wait_ge(c_yn, b + 1)
                cp(y_res[:, :, :], y_new[:, :, :]).then_inc(c_yres, 1)

            def over_experts(v):
                return v.unsqueeze(2).to_broadcast([P, TPB, EXP])

            def over_tiles(v):
                return v.unsqueeze(1).to_broadcast([P, TPB, EXP])

            def top2(b):
                rt.start(b)
                dve.wait_ge(r_g, b + 1)
                g = b_w[0][:, 0:TPB * EXP].rearrange("p (t e) -> p t e", e=EXP)
                for logits, v, i, oh in ((g, v0, i0, oh0), (g2[:, :, :], v1, i1, oh1)):
                    rt.link(nc.vector.tensor_reduce(v[:, :], logits, axis=AX.X, op=MAX))
                    rt.link(tt(eq[:, :, :], logits, over_experts(v[:, :]), ALU.is_equal))
                    rt.link(stt(key[:, :, :], eq[:, :, :], -8.0, over_tiles(expert_no[:, :]), MUL, ADD))
                    rt.link(nc.vector.tensor_reduce(i[:, :], key[:, :, :], axis=AX.X, op=MIN))
                    rt.link(tt(oh[:, :, :], over_tiles(expert_no8[:, :]), over_experts(i[:, :]), ALU.is_equal))
                    if oh is oh0:
                        rt.link(stt(g2[:, :, :], oh0[:, :, :], -3.0e38, g, MUL, ADD))
                tt(gap[:, :], v1[:, :], v0[:, :], SUB).then_inc(r_dv, 1)
                tt(chosen[:, :, :], oh0[:, :, :], oh1[:, :, :], ADD).then_inc(r_m, 1)

            def positions(b):
                dve.wait_ge(r_ex, b + 1)
                rt.link(ts(gate0[:, :], e_gap[:, :], 1.0, None, ADD))
                rt.link(nc.vector.reciprocal(gate0[:, :], gate0[:, :]))
                rt.link(tt(gate1[:, :], e_gap[:, :], gate0[:, :], MUL))
                dve.wait_ge(r_rank, b + 1)
                ranks = b_w[1][:, 0:TPB * EXP].rearrange("p (t e) -> p t e", e=EXP)
                rt.link(tt(pr[:, :, :], ranks, over_tiles(taken[:, :]), ADD))
                tt(taken[:, :], b_w[1][:, TPB * EXP:(TPB + 1) * EXP], taken[:, :], ADD).then_inc(r_run, 1)
                rt.mark(tt(eq[:, :, :], oh0[:, :, :], pr[:, :, :], MUL))
                rt.link(tt(key[:, :, :], oh1[:, :, :], pr[:, :, :], MUL))
                rt.mark(nc.vector.tensor_reduce(pos_f[:, 0:TPB], eq[:, :, :], axis=AX.X, op=ADD))
                rt.link(nc.vector.tensor_reduce(pos_f[:, TPB:], key[:, :, :], axis=AX.X, op=ADD))
                cp(xr[:, :, D:D + 1], twice_token[:, :].unsqueeze(2))
                cp(xr[:, :, D + 1:D + 2], gate0[:, :].unsqueeze(2))
                cp(xr[:, :, D + 2:D + 3], gate1[:, :].unsqueeze(2))
                ts(xr[:, :, D + 3:D + 4], i0[:, :].unsqueeze(2), float(EXP), None, ADD)
                rt.link(ts(twice_token[:, :], twice_token[:, :], float(2 * BLK), None, ADD))
                cp(pos_i[:, :], pos_f[:, :]).then_inc(r_pos, 1)
                rt.end()

            k = [0]

            def link(ins):
                k[0] += 1
                ins.then_inc(c_prep, 1)
                dve.wait_ge(c_prep, k[0])

            nc.vector.memset(ones_bf[:, :], 1.0)
            dve.wait_ge(r_iota, 2)
            cp(expert_no[:, :], eno_i[:, :])
            cp(twice_token[:, :], ids_i[:, :])
            ts(expert_no8[:, :], eno_i[:, :], -float(EXP), None, ADD)
            ts(taken[:, :], eno_i[:, :], float(REGION), None, MUL)
            nc.vector.memset(st_a[:, :, 0:1], 0.0)
            nc.vector.memset(st_b[:, :, 0:1], 0.0)
            nc.vector.memset(h2T[:, :, 0:1], 0.0)
            for j, n in enumerate(("mix_k", "mix_v", "mix_r")):
                last = ts(one_minus[:, j * DC:(j + 1) * DC], vecs[:, VEC[n]:VEC[n] + DC], -1.0, 1.0, MUL, ADD)
            link(last)
            dve.wait_ge(c_act_const, 1)
            link(ts(ew[:, :], ew[:, :], -1.0, -20.0, MUL, MAX))
            ts(ew[:, :], ew[:, :], 20.0, None, MIN).then_inc(c_const, 1)
            dve.wait_ge(c_act_const, 2)
            pre(0)

            def low_weight(w, src):
                return tt(w[1][:, :, :], src.rearrange("p (c n) -> p c n", c=DC), w[0][:, :, :].bitcast(fp32), SUB)

            for j, n in enumerate(("k", "v", "r")):
                dve.wait_ge(c_stage[n], 16)
                for c in range(DC):
                    ts(fold[0][:, c * D:(c + 1) * D], stage[n][:, c * D:(c + 1) * D], vec("mix_" + n, c), None, MUL)
                    last = ts(fold[1][:, c * D:(c + 1) * D], stage[n][:, c * D:(c + 1) * D], one_minus[:, j * DC + c:j * DC + c + 1], None, MUL)
                last.then_inc(c_fold, 1)
                dve.wait_ge(c_fhi, j + 1)
                low_weight(kvr[n][0], fold[0][:, :])
                low_weight(kvr[n][1], fold[1][:, :]).then_inc(c_w, 1)
                dve.wait_ge(c_w, j + 1)
                if j == 0:
                    h_carry(0)
                    h_low(0)
            scan(0, 0)
            wkv_low(0, 0)
            pre(1)
            scan(0, 1)
            wkv_low(0, 1)
            scan_s.end()
            h_carry(1)

            def step(i, first=False, more=True):
                h_low(i + 1)
                if not first:
                    gated(i - 1)
                residual(i)
                out_add(i)
                x1_norm(i)
                mixes(i)
                if not first:
                    final(i - 1)
                if more:
                    pre(i + 2)
                scan(i + 1, 0)
                if not first:
                    top2(i - 1)
                wkv_low(i + 1, 0)
                if not first:
                    positions(i - 1)
                if more:
                    h_carry(i + 2)
                scan(i + 1, 1)
                wkv_low(i + 1, 1)
                scan_s.end()

            step(0, first=True)
            with dve.Fori(1, NBLK - 2) as i:
                step(i)
            step(NBLK - 2, more=False)
            b = NBLK - 1
            gated(b - 1)
            residual(b)
            out_add(b)
            x1_norm(b)
            mixes(b)
            final(b - 1)
            top2(b - 1)
            positions(b - 1)
            gated(b)
            final(b)
            top2(b)
            positions(b)

        block_ctx.close()
        end_phase()

        cursor[0] = shared_from
        m1_hi, m2_hi = sb("m1_hi", [P, EXP, DC, FF], fp32r), sb("m2_hi", [P, EXP, DC, FF], fp32r)
        m3_hi = sb("m3_hi", [P, EXP, FC, D], fp32r)
        m1_lo, m2_lo = sb("m1_lo", [P, EXP, DC, FF], bf16), sb("m2_lo", [P, EXP, DC, FF], bf16)
        m3_lo = sb("m3_lo", [P, EXP, FC, D], bf16)
        WIDE = 2 * FF + D
        biases = sb("biases", [P, WIDE], bf16)
        rowc = sb("rowc", [P, 1 + PARTS])
        row_expert = sb("row_expert", [P, P])
        fill = sb("fill", [P, ROW])
        fill_i = sb("fill_i", [P, 1], i32)
        tile_no, tile_no_i = sb("tile_no", [P, N_TILES]), sb("tile_no_i", [P, N_TILES], i32)
        ends = sb("ends", [P, EXP])
        past = sb("past", [P, N_TILES, EXP])
        expert_of, start_of, row_of = (sb(n, [P, N_TILES]) for n in ("expert_of", "start_of", "row_of"))
        expert_reg, row_reg = sb("expert_reg", [1, N_TILES], i32), sb("row_reg", [1, N_TILES], i32)
        free_reg = sb("free_reg", [1, EXP], i32)
        U = 8
        rows4 = [sb(f"rows{n}", [P, ROW]) for n in range(U)]
        xT = [[sb(f"xT_{s}{n}", [P, DC, P], d) for s, d in (("hi", fp32r), ("lo", fp32r), ("bf", bf16))] for n in range(2)]
        sel = [sb(f"sel{n}", [P, P], bf16) for n in range(U)]
        silu = sb("silu", [P, FF])
        hid = sb("hid", [P, FF])
        hT4 = [[sb(f"hTe_{s}{n}", [P, FC, P], d) for s, d in (("hi", fp32r), ("lo", fp32r), ("bf", bf16))] for n in range(2)]
        mine = sb("mine", [P, U])
        weight4, dw = sb("weight4", [P, U]), sb("dw", [P, U])
        padding, tile_row = sb("padding", [P, U]), sb("tile_row", [P, N_TILES])
        dest_f, dest_i = sb("dest_f", [P, U]), sb("dest_i", [P, U], i32)
        y4 = [sb(f"y{n}", [P, D]) for n in range(U)]
        wait_for, need_reg = sb("wait_for", [P, N_TILES]), sb("need_reg", [1, N_TILES], i32)
        bias_f, bias_p = sb("bias_f", [P, WIDE]), sb("bias_p", [P, WIDE], bf16)
        count, ones8 = sb("count", [P, EXP]), sb("ones8", [P, EXP])
        valid = sb("valid", [P, N_TILES])

        b_gv = [bank[0:2], bank[2:4]]
        b_x, b_h = bank[4], bank[5]
        b_y = bank[6:8]

        e_bias, e_rowc = sem("e_bias_loaded"), sem("e_rowc_loaded")
        e_rows_on = sem("e_first_tiles_on_the_way")
        e_w_first, e_w_rest = sem("e_first_experts_loaded"), sem("e_other_experts_loaded")
        e_prep = sem("e_prep_steps")
        e_iota, e_fill, e_tab, e_filled = sem("e_iotas"), sem("e_fill_ready"), sem("e_tables"), sem("e_filled")
        e_ld, e_t, e_xhi, e_xs, e_sel = [sem(f"e_rows_loaded{n}") for n in range(U)], sem("e_transposed"), sem("e_x_high"), sem("e_x_split"), sem("e_selected")
        e_g, e_v, e_silu, e_hid, e_th = sem("e_gate"), sem("e_value"), sem("e_silu"), sem("e_hidden"), sem("e_hidden_transposed")
        e_hhi, e_hs, e_y, e_meta, e_ye = sem("e_hidden_high"), sem("e_hidden_split"), sem("e_out_product"), sem("e_meta"), sem("e_out_weighted")
        e_sc = [sem(f"e_out_scattered{n}") for n in range(U)]
        e_pool_on = sem("e_pool_goes_on")
        e_on, e_meta_s = sem("e_vector_goes_on"), sem("e_meta_steps")

        FS = 4
        fx = [sb(f"fx{n}", [P, TPB, D], at=shared_from + n * 4 * TPB * D) for n in range(FS)]
        at = shared_from + FS * 4 * TPB * D
        fy = [sb(f"fy{n}", [P, TPB, 2 * D], at=at + n * 8 * TPB * D) for n in range(FS)]
        at += FS * 8 * TPB * D
        f_ld, f_sum, f_steps, f_v, f_r, f_done = [sem(f"f_loaded{n}") for n in range(FS)], sem("f_summed"), sem("f_steps"), sem("f_variances"), sem("f_roots"), sem("f_done")
        f_st = [sem(f"f_stored{n}") for n in range(FS)]
        fbn, fmv = sb("fbn", [P, TPB, 6], at=at), sb("fmv", [P, TPB, 2], at=at + 128)
        fv, fr = sb("fv", [P, TPB], at=at + 192), sb("fr", [P, TPB], at=at + 256)

        block_ctx = ExitStack()
        block = block_ctx.enter_context(nc.Block())

        FIRST = 2

        def load_experts(eng, a, z, done):
            for (hi, lo), on_chip in zip(expert_parts, ((m1_hi, m1_lo), (m2_hi, m2_lo), (m3_hi, m3_lo))):
                for part, w in zip((hi, lo), on_chip):
                    dst = w[:, a:z, :, :].rearrange("p e c n -> p (e c n)")
                    if w.dtype == fp32r:
                        dst = dst.bitcast(fp32)
                    eng.dma_start(dst, part[:, a * DC * FF:z * DC * FF]).then_inc(done, 16)

        @block.sync
        def _(sp):
            sp.dma_start(rowc[:, :], rowc_in).then_inc(e_rowc, 16)
            sp.sem_inc(e_w_rest)
            sp.wait_ge(e_prep, 1)
            for n in range(PARTS):
                sp.dma_start(bias_f[n * EXP:(n + 1) * EXP, :], bias_in).then_inc(e_bias, 16)
            load_experts(sp, 0, FIRST, e_w_first)
            sp.wait_ge(e_fill, 1)
            sp.dma_start(routed[EXP * REGION:, :], fill[:, :]).then_inc(e_filled, 16)
            sp.wait_ge(e_tab, 4)
            for e in range(EXP):
                free = sp.value_load(free_reg[0:1, e:e + 1], min_val=e * REGION, max_val=e * REGION + N_TOK)
                sp.dma_start(routed[bass.ds(free, P), :], fill[:, :]).then_inc(e_filled, 16)
            sp.wait_ge(e_filled, 16 * (EXP + 1))

            def load(j, u, first=False):
                if not first:
                    sp.wait_ge(e_t, j - U + 1)
                    sp.wait_ge(e_meta, j - U + 1)
                row = sp.value_load(row_reg[0:1, bass.ds(j, 1)], min_val=0, max_val=EXP * REGION)
                sp.dma_start(rows4[u][:, :], routed[bass.ds(row, P), :]).then_inc(e_ld[u], 16)

            for j in range(U):
                load(j, j, True)
            sp.sem_inc(e_rows_on)
            with sp.Fori(1, N_TILES // U) as i:
                for u in range(U):
                    load(i * U + u, u)
            pairs = expert_out[0:2 * N_TOK, :].rearrange("(t p k) d -> p t (k d)", p=P, k=2)
            for u in range(U):
                sp.wait_ge(e_sc[u], 16 * (N_TILES // U))

            def load_block(b, n):
                sp.dma_start(fy[n][:, :, :], pairs[:, bass.ds(b * TPB, TPB), :]).then_inc(f_ld[n], 16)
                sp.dma_start(fx[n][:, :, :], x3_blocks[:, bass.ds(b * TPB, TPB), :]).then_inc(f_ld[n], 16)

            def store_block(b, n):
                sp.wait_ge(f_done, b + 1)
                sp.dma_start(out_blocks[:, bass.ds(b * TPB, TPB), :], fx[n][:, :, :]).then_inc(f_st[n], 16)

            for n in range(FS):
                load_block(n, n)
            with sp.Fori(1, NBLK // FS) as i:
                for n in range(FS):
                    store_block(i * FS - FS + n, n)
                    sp.wait_ge(f_st[n], i * 16)
                    load_block(i * FS + n, n)
            for n in range(FS):
                store_block(NBLK - FS + n, n)
            for n in range(FS):
                sp.wait_ge(f_st[n], 16 * (NBLK // FS))

        @block.gpsimd
        def _(pool):
            nc.gpsimd.iota(tile_no_i[:, :], pattern=[[1, N_TILES]], base=0, channel_multiplier=0).then_inc(e_iota, 1)
            nc.gpsimd.iota(fill_i[:, :], pattern=[[0, 1]], base=2 * N_TOK - 1, channel_multiplier=1).then_inc(e_iota, 1)

            def scatter(j, u):
                pool.wait_ge(e_ye, j + 1)
                pool.sem_inc(e_pool_on)
                nc.gpsimd.indirect_dma_start(expert_out, bass.IndirectOffsetOnAxis(ap=dest_i[:, u:u + 1], axis=0),
                                             y4[u][:, :], None).then_inc(e_sc[u], 16)

            with pool.Fori(0, N_TILES // U) as i:
                for u in range(U):
                    scatter(i * U + u, u)
            with pool.Fori(0, NBLK // FS) as i:
                for n in range(FS):
                    pool.wait_ge(f_ld[n], i * 32 + 32)
                    nc.gpsimd.tensor_tensor(fy[n][:, :, 0:D], fy[n][:, :, 0:D], fy[n][:, :, D:2 * D], ADD).then_inc(f_sum, 1)

        @block.tensor
        def _(pe):
            mm = nc.tensor.matmul

            def rows_in(j, u, turn):
                pe.wait_ge(e_ld[u % U], turn * 16 + 16)
                if not (isinstance(j, int) and j == 0):
                    pe.wait_ge(e_xs, j)
                for c in range(DC):
                    last = nc.tensor.transpose(b_x[:, c * P:(c + 1) * P], rows4[u % U][:, c * P:(c + 1) * P], ident[:, :])
                last.then_inc(e_t, 1)

            def gate_value(j, u):
                e = pe.value_load(expert_reg[0:1, bass.ds(j, 1)], min_val=0, max_val=EXP - 1)
                pe.wait_ge(e_w_rest, pe.value_load(need_reg[0:1, bass.ds(j, 1)], min_val=1, max_val=1 + 16 * 6))
                pe.wait_ge(e_xs, j + 1)
                pe.wait_ge(e_sel, j + 1)
                if not (isinstance(j, int) and j < 2):
                    pe.wait_ge(e_hid, j - 1)
                hi, lo, bf = xT[u % 2]
                for n, (w_hi, w_lo, done) in enumerate(((m1_hi, m1_lo, e_g), (m2_hi, m2_lo, e_v))):
                    dst = b_gv[u % 2][n]
                    mm(dst[:, :], sel[u % U][:, :], biases[:, n * FF:(n + 1) * FF], start=True, stop=False)
                    for c in range(DC):
                        w = w_hi[:, bass.ds(e, 1), c, :].rearrange("p a n -> p (a n)")
                        mm(dst[:, :], hi[:, c, :], w, start=False, stop=False)
                        mm(dst[:, :], lo[:, c, :], w, start=False, stop=False)
                        last = mm(dst[:, :], bf[:, c, :], w_lo[:, bass.ds(e, 1), c, :].rearrange("p a n -> p (a n)"), start=False, stop=c == DC - 1)
                    last.then_inc(done, 1)

            def hidden_back(j, u):
                pe.wait_ge(e_hid, j + 1)
                if not (isinstance(j, int) and j == 0):
                    pe.wait_ge(e_hs, j)
                for c in range(FC):
                    last = nc.tensor.transpose(b_h[:, c * P:(c + 1) * P], hid[:, c * P:(c + 1) * P], ident[:, :])
                last.then_inc(e_th, 1)

            def out_rows(j, u):
                e = pe.value_load(expert_reg[0:1, bass.ds(j, 1)], min_val=0, max_val=EXP - 1)
                pe.wait_ge(e_hs, j + 1)
                if not (isinstance(j, int) and j < 2):
                    pe.wait_ge(e_ye, j - 1)
                hi, lo, bf = hT4[u % 2]
                dst = b_y[u % 2][:, 0:D]
                mm(dst, sel[u % U][:, :], biases[:, 2 * FF:2 * FF + D], start=True, stop=False)
                for c in range(FC):
                    w = m3_hi[:, bass.ds(e, 1), c, :].rearrange("p a n -> p (a n)")
                    mm(dst, hi[:, c, :], w, start=False, stop=False)
                    mm(dst, lo[:, c, :], w, start=False, stop=False)
                    last = mm(dst, bf[:, c, :], m3_lo[:, bass.ds(e, 1), c, :].rearrange("p a n -> p (a n)"), start=False, stop=c == FC - 1)
                last.then_inc(e_y, 1)

            def step(j, u, turn):
                known = isinstance(j, int)
                if not known or j + 1 < N_TILES:
                    gate_value(j + 1, u + 1)
                if not known or j + 2 < N_TILES:
                    rows_in(j + 2, u + 2, turn + (u + 2) // U)
                if not known or j < N_TILES:
                    hidden_back(j, u)
                if not known or j >= 1:
                    out_rows(j - 1, u - 1 if u else U - 1)

            pe.wait_ge(e_tab, 4)
            pe.wait_ge(e_w_first, 16 * 6)
            rows_in(0, 0, 0)
            rows_in(1, 1, 0)
            gate_value(0, 0)
            for u in range(U):
                step(u, u, 0)
            with pe.Fori(1, N_TILES // U - 1) as i:
                for u in range(U):
                    step(i * U + u, u, i)
            for u in range(U + 1):
                step(N_TILES - U + u, u, N_TILES // U - 1)

        @block.scalar
        def _(act):
            fn = nc.scalar.activation
            def x_high(j, u):
                act.wait_ge(e_t, j + 1)
                fn(xT[u % 2][0][:, :, :], b_x[:, 0:D].rearrange("p (c n) -> p c n", c=DC), ACT.Copy).then_inc(e_xhi, 1)

            def gate(j, u):
                act.wait_ge(e_g, j + 1)
                if not (isinstance(j, int) and j == 0):
                    act.wait_ge(e_hid, j)
                fn(silu[:, :], b_gv[u % 2][0][:, :], ACT.Silu).then_inc(e_silu, 1)

            def h_high(j, u):
                act.wait_ge(e_th, j + 1)
                fn(hT4[u % 2][0][:, :, :], b_h[:, :].rearrange("p (c n) -> p c n", c=FC), ACT.Copy).then_inc(e_hhi, 1)

            def weighted(j, u, turn):
                act.wait_ge(e_y, j + 1)
                act.wait_ge(e_meta, j + 1)
                if not (isinstance(turn, int) and turn == 0):
                    act.wait_ge(e_sc[u % U], turn * 16)
                fn(y4[u % U][:, :], b_y[u % 2][:, 0:D], ACT.Copy, scale=weight4[:, u % U:u % U + 1]).then_inc(e_ye, 1)

            def step(j, u, turn):
                known = isinstance(j, int)
                gate(j, u)
                if not known or j + 2 < N_TILES:
                    x_high(j + 2, u + 2)
                h_high(j, u)
                if not known or j >= 1:
                    weighted(j - 1, u - 1 if u else U - 1, turn if u else turn - 1)

            x_high(0, 0)
            x_high(1, 1)
            act.wait_ge(e_rows_on, 1)
            load_experts(act, FIRST, EXP, e_w_rest)
            for u in range(U):
                step(u, u, 0)
            with act.Fori(1, N_TILES // U - 1) as i:
                for u in range(U):
                    step(i * U + u, u, i)
            for u in range(U):
                step(N_TILES - U + u, u, N_TILES // U - 1)
            weighted(N_TILES - 1, U - 1, N_TILES // U - 1)

            def last_pass(i):
                for n in range(FS):
                    b = i * FS + n
                    act.wait_ge(f_v, b + 1)
                    fn(fr[:, :], fv[:, :], ACT.Sqrt).then_inc(f_r, 1)

            with act.Fori(0, NBLK // FS) as i:
                last_pass(i)

        @block.vector
        def _(dve):
            ts, tt, stt, cp = nc.vector.tensor_scalar, nc.vector.tensor_tensor, nc.vector.scalar_tensor_tensor, nc.vector.tensor_copy
            k = [0]

            def link(ins):
                k[0] += 1
                ins.then_inc(e_prep, 1)
                dve.wait_ge(e_prep, k[0])

            link(nc.vector.memset(bias_f[:, :], 0.0))
            dve.wait_ge(e_iota, 2)
            link(nc.vector.memset(fill[:, :], 0.0))
            link(nc.vector.memset(fill[:, D + 3:D + 4], -1.0))
            cp(fill[:, D:D + 1], fill_i[:, :]).then_inc(e_fill, 1)
            cp(free_reg[:, :], taken[0:1, :]).then_inc(e_tab, 1)
            nc.vector.memset(ones8[:, :], 1.0)
            cp(tile_no[:, :], tile_no_i[:, :])
            ts(tile_row[:, :], tile_no_i[:, :], float(P), None, MUL)
            link(stt(count[:, :], expert_no[:, :], -float(REGION), taken[:, :], MUL, ADD))
            link(ts(count[:, :], count[:, :], 1.0 / P, 0.5 - 0.5 / P, MUL, ADD))
            link(ts(count[:, :], count[:, :], 2.0 ** 23, None, ADD))
            link(ts(count[:, :], count[:, :], -2.0 ** 23, None, ADD))
            link(nc.vector.tensor_tensor_scan(ends[:, :], ones8[:, :], count[:, :], 0.0, MUL, ADD))
            by_tile = lambda v: v.unsqueeze(2).to_broadcast([P, N_TILES, EXP])
            by_expert = lambda v: v.unsqueeze(1).to_broadcast([P, N_TILES, EXP])
            link(tt(past[:, :, :], by_tile(tile_no[:, :]), by_expert(ends[:, :]), ALU.is_ge))
            link(nc.vector.tensor_reduce(expert_of[:, :], past[:, :, :], axis=AX.X, op=ADD))
            link(tt(past[:, :, :], past[:, :, :], by_expert(ends[:, :]), MUL))
            link(nc.vector.tensor_reduce(start_of[:, :], past[:, :, :], axis=AX.X, op=MAX))
            link(ts(valid[:, :], expert_of[:, :], EXP - 0.5, None, ALU.is_lt))
            link(tt(row_of[:, :], tile_no[:, :], start_of[:, :], SUB))
            link(stt(row_of[:, :], row_of[:, :], float(P), valid[:, :], MUL, MUL))
            link(stt(row_of[:, :], expert_of[:, :], float(REGION), row_of[:, :], MUL, ADD))
            link(ts(expert_of[:, :], expert_of[:, :], float(EXP - 1), None, MIN))
            link(ts(wait_for[:, :], expert_of[:, :], FIRST - 0.5, 16.0 * 6, ALU.is_gt, MUL))
            ts(need_reg[:, :], wait_for[0:1, :], 1.0, None, ADD).then_inc(e_tab, 1)
            cp(row_reg[:, :], row_of[0:1, :]).then_inc(e_tab, 1)
            cp(expert_reg[:, :], expert_of[0:1, :]).then_inc(e_tab, 1)
            dve.wait_ge(e_rowc, 16)
            dve.wait_ge(e_bias, 16 * PARTS)
            link(cp(row_expert[:, :], rowc[:, 0:1].broadcast_to([P, P])))
            for n in range(PARTS):
                link(cp(bias_p[:, :], bias_f[:, :]))
                if n == 0:
                    link(ts(biases[:, :], bias_p[:, :], rowc[:, 1:2], None, MUL))
                else:
                    link(stt(biases[:, :], bias_p[:, :], rowc[:, 1 + n:2 + n], biases[:, :], MUL, ADD))
                link(tt(bias_f[:, :], bias_f[:, :], bias_p[:, :], SUB))
            meta_s, fin_s = Steps(dve, e_meta_s, 3), Steps(dve, f_steps, 4)

            def x_split(j, u):
                dve.wait_ge(e_xhi, j + 1)
                hi, lo, bf = xT[u % 2]
                src = b_x[:, 0:D].rearrange("p (c n) -> p c n", c=DC)
                cp(bf[:, :, :], src)
                tt(lo[:, :, :], src, hi[:, :, :].bitcast(fp32), SUB).then_inc(e_xs, 1)
                ts(sel[u % U][:, :], row_expert[:, :], expert_of[:, bass.ds(j, 1)], None, ALU.is_equal).then_inc(e_sel, 1)

            def hidden(j, u):
                dve.wait_ge(e_v, j + 1)
                dve.wait_ge(e_silu, j + 1)
                tt(hid[:, :], silu[:, :], b_gv[u % 2][1][:, :], MUL).then_inc(e_hid, 1)

            def meta(j, u, turn):
                meta_s.start(j)
                dve.wait_ge(e_ld[u], turn * 16 + 16)
                if not (isinstance(turn, int) and turn == 0):
                    dve.wait_ge(e_sc[u], turn * 16)
                row, c = rows4[u], slice(u, u + 1)
                meta_s.mark(ts(mine[:, c], row[:, D + 3:D + 4], expert_of[:, bass.ds(j, 1)], None, ALU.is_equal))
                meta_s.link(tt(dw[:, c], row[:, D + 1:D + 2], row[:, D + 2:D + 3], SUB))
                ts(padding[:, c], row[:, D + 3:D + 4], 0.0, tile_row[:, bass.ds(j, 1)], ALU.is_lt, MUL)
                stt(weight4[:, c], dw[:, c], mine[:, c], row[:, D + 2:D + 3], MUL, ADD)
                meta_s.link(stt(dest_f[:, c], row[:, D:D + 1], 1.0, mine[:, c], ADD, SUB))
                tt(dest_i[:, c], dest_f[:, c], padding[:, c], ADD).then_inc(e_meta, 1)
                meta_s.end()

            def h_split(j, u):
                dve.wait_ge(e_hhi, j + 1)
                hi, lo, bf = hT4[u % 2]
                src = b_h[:, :].rearrange("p (c n) -> p c n", c=FC)
                cp(bf[:, :, :], src)
                tt(lo[:, :, :], src, hi[:, :, :].bitcast(fp32), SUB).then_inc(e_hs, 1)

            def step(j, u, turn):
                hidden(j, u)
                meta(j, u, turn)
                if not isinstance(j, int) or j + 2 < N_TILES:
                    x_split(j + 2, u + 2)
                h_split(j, u)

            x_split(0, 0)
            x_split(1, 1)
            for u in range(U):
                step(u, u, 0)
            with dve.Fori(1, N_TILES // U - 1) as i:
                for u in range(U):
                    step(i * U + u, u, i)
            for u in range(U):
                step(N_TILES - U + u, u, N_TILES // U - 1)

            def last_pass(i):
                for n in range(FS):
                    b = i * FS + n
                    y = fy[n][:, :, 0:D]
                    fin_s.start(b)
                    dve.wait_ge(f_sum, b + 1)
                    for t in range(TPB):
                        last = nc.vector.bn_stats(fbn[:, t, :], fy[n][:, t, 0:D])
                    fin_s.link(last)
                    dve.sem_inc(e_on)
                    for t in range(TPB):
                        last = nc.vector.bn_aggr(fmv[:, t, :], fbn[:, t, :])
                    fin_s.link(last)
                    fin_s.link(ts(fv[:, :], fmv[:, :, 1], LN_EPS, None, ADD))
                    nc.vector.reciprocal(fv[:, :], fv[:, :]).then_inc(f_v, 1)
                    dve.wait_ge(f_r, b + 1)
                    for t in range(TPB):
                        last = ts(fy[n][:, t, 0:D], fy[n][:, t, 0:D], fmv[:, t, 0:1], fr[:, t:t + 1], SUB, MUL)
                    fin_s.link(last)
                    tt(fx[n][:, :, :], fx[n][:, :, :], y, ADD).then_inc(f_done, 1)
                    fin_s.end()

            with dve.Fori(0, NBLK // FS) as i:
                last_pass(i)

        block_ctx.close()
        end_phase()


_WEIGHTS = {"wg": ("L0_attn_Wg", True), "wc": ("L0_attn_Wc", True), "w1": ("L0_ffn_w1_w", True), "w2": ("L0_ffn_w2_w", True),
            "h1": ("L0_ffn_h1_w", True), "h2": ("L0_ffn_h2_w", True), "w3": ("L0_ffn_w3_w", True), "wk": ("L1_attn_W_key", False), "wv": ("L1_attn_W_value", False),
            "wr": ("L1_attn_W_recept", False), "wo": ("L1_attn_W_out", False), "wk2": ("L1_attn_W_key2", False),
            "wv2": ("L1_attn_W_value2", False), "wr2": ("L1_attn_W_recept2", False), "wg8": ("L1_ffn_Wg", True)}
_VECTORS = {"gamma": "L0_attn_gamma", "beta": "L0_attn_beta", "bg": "L0_attn_bg", "bc": "L0_attn_bc", "w1_s": "L0_ffn_w1_s",
            "w2_s": "L0_ffn_w2_s", "h1_s": "L0_ffn_h1_s", "h2_s": "L0_ffn_h2_s", "ln1_w": "L1_attn_ln1_w",
            "ln2_w": "L1_attn_ln2_w", "decay": "L1_attn_time_decay", "first": "L1_attn_time_first",
            "mix_k": "L1_attn_time_mix_k", "mix_v": "L1_attn_time_mix_v", "mix_r": "L1_attn_time_mix_r",
            "mix_k2": "L1_attn_time_mix_k2", "mix_r2": "L1_attn_time_mix_r2"}


def layouts(inputs):
    import numpy as np

    def rows(name, transpose):
        w = np.asarray(inputs[name])
        w = w.T if transpose else w
        return np.ascontiguousarray(w.reshape(-1, P, w.shape[1]).transpose(1, 0, 2)).reshape(P, -1)

    arrays = {"x": np.ascontiguousarray(np.asarray(inputs["L0_attn_x"]).reshape(N_TOK, D))}
    arrays["vecs"] = np.ascontiguousarray(np.concatenate(
        [np.asarray(inputs[_VECTORS[n]]).reshape(-1, P).T for n in VEC], axis=1))
    arrays["w3s"] = np.ascontiguousarray(np.broadcast_to(np.asarray(inputs["L0_ffn_w3_s"]), (P, D)))
    for k, (name, transpose) in _WEIGHTS.items():
        arrays[k] = rows(name, transpose)

    def experts(name):
        w = np.asarray(inputs[name])
        e, o, i = w.shape
        return np.ascontiguousarray(w.transpose(2, 0, 1).reshape(i // P, P, e, o).transpose(1, 2, 0, 3)).reshape(P, -1)

    for n in (1, 2, 3):
        arrays[f"m{n}"] = experts(f"L1_ffn_W{n}")
    arrays["bias"] = np.ascontiguousarray(np.concatenate([np.asarray(inputs[f"L1_ffn_b{n}"]) for n in (1, 2, 3)], axis=1))
    rowc = np.full((P, 1 + PARTS), 0.0, np.float32)
    rowc[:, 0] = [n % EXP if n < PARTS * EXP else -2 for n in range(P)]
    for n in range(PARTS):
        rowc[n * EXP:(n + 1) * EXP, 1 + n] = 1.0
    arrays["rowc"] = rowc
    return arrays


def kernel(**inputs):
    import numpy as _np
    import concourse.bacc as _bacc
    from concourse import mybir as _mybir
    from concourse.bass_utils import run_bass_kernel_spmd as _run

    nc = _bacc.Bacc("TRN2", target_bir_lowering=False, num_devices=1)
    arrays, args = {}, []
    for name, a in layouts(inputs).items():
        arrays[f"in_{name}_dram"] = a
        args.append(nc.dram_tensor(f"in_{name}_dram", a.shape, _mybir.dt.from_np(a.dtype), kind="ExternalInput").ap())
    args.append(nc.dram_tensor("out_dram", (N_TOK, D), _mybir.dt.float32, kind="ExternalOutput").ap())
    build(nc, *args)
    r = _run(nc, [arrays], core_ids=[0])
    return r.results[0]["out_dram"].reshape(4, SEQ, D)
```
